# Optimizing a Trainium2 kernel written in Bass

```python
import numpy as np
import jax
import jax.numpy as jnp

def _softmax(x, axis=-1):
    return jax.nn.softmax(x, axis=axis)

def _gelu(x):
    return jax.nn.gelu(x, approximate=True)

def _silu(x):
    return jax.nn.silu(x)

def _sigmoid(x):
    return jax.nn.sigmoid(x)

def _layernorm(x, axis=-1, eps=1e-05):
    m = jnp.mean(x, axis=axis, keepdims=True)
    v = jnp.var(x, axis=axis, keepdims=True)
    return (x - m) / jnp.sqrt(v + eps)

def _scatter_add(tgt, idx, src, axis=0):
    return tgt.at[idx].add(src)

def _segment_sum(src, seg, n):
    return jax.ops.segment_sum(src, seg, n)
kernel_name = 'mk_gps_d2_gnn_r8_020376'

def setup_inputs(seed: int=0):
    np.random.seed(seed)
    _w = jnp.asarray

    def _rec_inputs():
        import jax
        import jax.numpy as jnp
        _gk = jax.random.key(seed)
        x = -0.0001126 + 1 * jax.random.normal(jax.random.fold_in(_gk, 1), (1250, 768), jnp.float32)
        src = jax.random.randint(jax.random.fold_in(_gk, 2), (20000,), 0, 1250, jnp.int32)
        dst = jnp.minimum((1250 * jax.random.uniform(jax.random.fold_in(_gk, 3), (20000,)) ** 2.0).astype(jnp.int32), 9999)
        _o = jnp.argsort(dst, stable=True)
        src = src[_o]
        dst = dst[_o]
        return (x, src, dst)
    x, src, dst = _rec_inputs()

    def _L0_gnn_setup():
        import jax, jax.numpy as jnp
        import numpy as np
        N_NODES = 1250
        N_EDGES = 12500
        DIM = 768
        key = jax.random.key(seed)
        k1, k2, k3, k4 = jax.random.split(key, 4)
        x = jax.random.normal(k1, (N_NODES, DIM), dtype=jnp.float32)
        edge_index = jax.random.randint(k2, (2, N_EDGES), 0, N_NODES, dtype=jnp.int32)
        W = jax.random.normal(k3, (DIM, DIM), dtype=jnp.float32) / np.sqrt(DIM)
        b = jnp.zeros((DIM,), dtype=jnp.float32)
        return {'x': x, 'edge_index': edge_index, 'W': W, 'b': b}
    _L0_gnn_all = _L0_gnn_setup()
    _L0_gnn_in = {k: v for k, v in _L0_gnn_all.items() if k in ('W', 'b')}
    del _L0_gnn_all

    def _L0_mix_setup():
        import jax, jax.numpy as jnp
        import numpy as np
        NUM_HEADS = 12

        def _reference_tuple_inner(x, w_qkv, w_proj, b_proj):
            B, N, C = x.shape
            H = NUM_HEADS
            D = C // H
            qkv = (x @ w_qkv).reshape(B, N, 3, H, D)
            q = jnp.transpose(qkv[:, :, 0], (0, 2, 1, 3))
            k = jnp.transpose(qkv[:, :, 1], (0, 2, 1, 3))
            v = jnp.transpose(qkv[:, :, 2], (0, 2, 1, 3))
            q = jax.nn.elu(q) + 1.0
            k = jax.nn.elu(k) + 1.0
            attn = jnp.einsum('bhnd,bhmd->bhnm', q, k)
            attn = attn / jnp.sum(attn, axis=-1, keepdims=True)
            out = jnp.einsum('bhnm,bhmd->bhnd', attn, v)
            out = jnp.transpose(out, (0, 2, 1, 3)).reshape(B, N, C)
            out = out @ w_proj + b_proj
            return (out, attn)
        key = jax.random.key(seed)
        k1, k2, k3 = jax.random.split(key, 3)
        B, N, C = (2, 256, 768)
        x = jax.random.normal(k1, (B, N, C), dtype=jnp.float32)
        w_qkv = jax.random.normal(k2, (C, 3 * C), dtype=jnp.float32) * 0.02
        w_proj = jax.random.normal(k3, (C, C), dtype=jnp.float32) * 0.02
        b_proj = jnp.zeros((C,), dtype=jnp.float32)
        return {'x': x, 'w_qkv': w_qkv, 'w_proj': w_proj, 'b_proj': b_proj}
    _L0_mix_all = _L0_mix_setup()
    _L0_mix_in = {k: v for k, v in _L0_mix_all.items() if k in ('w_qkv', 'w_proj', 'b_proj')}
    del _L0_mix_all

    def _L0_ffn_setup():
        import jax, jax.numpy as jnp
        import numpy as np
        B, S, H = (4, 1024, 768)
        E, K = (8, 2)
        key = jax.random.key(seed)
        ks = jax.random.split(key, 5)
        scale = 1.0 / np.sqrt(H)
        x = jax.random.normal(ks[0], (B, S, H), dtype=jnp.float32)
        router_w = jax.random.uniform(ks[1], (E, H), jnp.float32, -scale, scale)
        router_b = jax.random.uniform(ks[2], (E,), jnp.float32, -scale, scale)
        expert_w = jax.random.uniform(ks[3], (E, H, H), jnp.float32, -scale, scale)
        expert_b = jax.random.uniform(ks[4], (E, H), jnp.float32, -scale, scale)
        return {'x': x, 'router_w': router_w, 'router_b': router_b, 'expert_w': expert_w, 'expert_b': expert_b}
    _L0_ffn_all = _L0_ffn_setup()
    _L0_ffn_in = {k: v for k, v in _L0_ffn_all.items() if k in ('router_w', 'router_b', 'expert_w', 'expert_b')}
    del _L0_ffn_all

    def _L1_gnn_setup():
        import jax, jax.numpy as jnp
        import numpy as np
        N_NODES = 1250
        N_EDGES = 20000
        NEG_SLOPE = 0.2

        def _gat_layer(x, src, dst, W, a_src, a_dst, bias, concat):
            N = x.shape[0]
            H, C = a_src.shape
            h = (x @ W).reshape(N, H, C)
            al_s = jnp.einsum('nhc,hc->nh', h, a_src)
            al_d = jnp.einsum('nhc,hc->nh', h, a_dst)
            e = jax.nn.leaky_relu(al_s[src] + al_d[dst], NEG_SLOPE)
            m = jax.ops.segment_max(e, dst, num_segments=N)
            ex = jnp.exp(e - m[dst])
            denom = jax.ops.segment_sum(ex, dst, num_segments=N)
            alpha = ex / (denom[dst] + 1e-16)
            msg = h[src] * alpha[:, :, None]
            out = jax.ops.segment_sum(msg, dst, num_segments=N)
            out = out.reshape(N, H * C) if concat else out.mean(axis=1)
            return out + bias
        key = jax.random.key(seed)
        ks = jax.random.split(key, 10)
        in_dim, hid, out_dim, heads = (768, 512, 768, 4)
        x = jax.random.normal(ks[0], (N_NODES, in_dim), dtype=jnp.float32)
        edge_index = jax.random.randint(ks[1], (2, N_EDGES), 0, N_NODES, dtype=jnp.int64)
        g = lambda k, shape, fan: jax.random.normal(k, shape, jnp.float32) / np.sqrt(fan)
        return {'x': x, 'edge_index': edge_index, 'W1': g(ks[2], (in_dim, heads * hid), in_dim), 'att_src1': g(ks[3], (heads, hid), hid), 'att_dst1': g(ks[4], (heads, hid), hid), 'b1': jnp.zeros((heads * hid,), jnp.float32), 'W2': g(ks[5], (heads * hid, out_dim), heads * hid), 'att_src2': g(ks[6], (1, out_dim), out_dim), 'att_dst2': g(ks[7], (1, out_dim), out_dim), 'b2': jnp.zeros((out_dim,), jnp.float32)}
    _L1_gnn_all = _L1_gnn_setup()
    _L1_gnn_in = {k: v for k, v in _L1_gnn_all.items() if k in ('W1', 'att_src1', 'att_dst1', 'b1', 'W2', 'att_src2', 'att_dst2', 'b2')}
    del _L1_gnn_all

    def _L1_mix_setup():
        import jax, jax.numpy as jnp
        import numpy as np
        NUM_HEADS = 12
        EPS = 1e-06
        key = jax.random.key(seed)
        k1, k2, k3, k4, k5 = jax.random.split(key, 5)
        B, N, C = (8, 512, 768)
        scale = 1.0 / np.sqrt(C)
        return {'x': jax.random.normal(k1, (B, N, C), dtype=jnp.float32), 'W_qkv': jax.random.normal(k2, (C, 3 * C), dtype=jnp.float32) * scale, 'b_qkv': jax.random.normal(k3, (3 * C,), dtype=jnp.float32) * 0.02, 'W_proj': jax.random.normal(k4, (C, C), dtype=jnp.float32) * scale, 'b_proj': jax.random.normal(k5, (C,), dtype=jnp.float32) * 0.02}
    _L1_mix_all = _L1_mix_setup()
    _L1_mix_in = {k: v for k, v in _L1_mix_all.items() if k in ('W_qkv', 'b_qkv', 'W_proj', 'b_proj')}
    del _L1_mix_all

    def _L1_ffn_setup():
        import jax, jax.numpy as jnp
        import numpy as np
        DIM = 768
        MOE_INTER = 256
        N_EXPERTS = 16
        TOP_K = 2
        SHARED_INTER = 2 * 256
        ROUTE_SCALE = 1.0
        B, S = (8, 196)
        key = jax.random.key(seed)
        ks = jax.random.split(key, 8)
        sc = 0.02
        return {'x': jax.random.normal(ks[0], (B, S, DIM), jnp.float32), 'gate_w': jax.random.normal(ks[1], (N_EXPERTS, DIM), jnp.float32) * sc, 'w1': jax.random.normal(ks[2], (N_EXPERTS, MOE_INTER, DIM), jnp.float32) * sc, 'w2': jax.random.normal(ks[3], (N_EXPERTS, DIM, MOE_INTER), jnp.float32) * sc, 'w3': jax.random.normal(ks[4], (N_EXPERTS, MOE_INTER, DIM), jnp.float32) * sc, 'sw1': jax.random.normal(ks[5], (SHARED_INTER, DIM), jnp.float32) * sc, 'sw2': jax.random.normal(ks[6], (DIM, SHARED_INTER), jnp.float32) * sc, 'sw3': jax.random.normal(ks[7], (SHARED_INTER, DIM), jnp.float32) * sc}
    _L1_ffn_all = _L1_ffn_setup()
    _L1_ffn_in = {k: v for k, v in _L1_ffn_all.items() if k in ('gate_w', 'w1', 'w2', 'w3', 'sw1', 'sw2', 'sw3')}
    del _L1_ffn_all
    return {'x': x, 'src': src, 'dst': dst, 'L0_gnn_W': _L0_gnn_in['W'], 'L0_gnn_b': _L0_gnn_in['b'], 'L0_mix_w_qkv': _L0_mix_in['w_qkv'], 'L0_mix_w_proj': _L0_mix_in['w_proj'], 'L0_mix_b_proj': _L0_mix_in['b_proj'], 'L0_ffn_router_w': _L0_ffn_in['router_w'], 'L0_ffn_router_b': _L0_ffn_in['router_b'], 'L0_ffn_expert_w': _L0_ffn_in['expert_w'], 'L0_ffn_expert_b': _L0_ffn_in['expert_b'], 'L1_gnn_W1': _L1_gnn_in['W1'], 'L1_gnn_att_src1': _L1_gnn_in['att_src1'], 'L1_gnn_att_dst1': _L1_gnn_in['att_dst1'], 'L1_gnn_b1': _L1_gnn_in['b1'], 'L1_gnn_W2': _L1_gnn_in['W2'], 'L1_gnn_att_src2': _L1_gnn_in['att_src2'], 'L1_gnn_att_dst2': _L1_gnn_in['att_dst2'], 'L1_gnn_b2': _L1_gnn_in['b2'], 'L1_mix_W_qkv': _L1_mix_in['W_qkv'], 'L1_mix_b_qkv': _L1_mix_in['b_qkv'], 'L1_mix_W_proj': _L1_mix_in['W_proj'], 'L1_mix_b_proj': _L1_mix_in['b_proj'], 'L1_ffn_gate_w': _L1_ffn_in['gate_w'], 'L1_ffn_w1': _L1_ffn_in['w1'], 'L1_ffn_w2': _L1_ffn_in['w2'], 'L1_ffn_w3': _L1_ffn_in['w3'], 'L1_ffn_sw1': _L1_ffn_in['sw1'], 'L1_ffn_sw2': _L1_ffn_in['sw2'], 'L1_ffn_sw3': _L1_ffn_in['sw3']}

def reference(x, src, dst, L0_gnn_W, L0_gnn_b, L0_mix_w_qkv, L0_mix_w_proj, L0_mix_b_proj, L0_ffn_router_w, L0_ffn_router_b, L0_ffn_expert_w, L0_ffn_expert_b, L1_gnn_W1, L1_gnn_att_src1, L1_gnn_att_dst1, L1_gnn_b1, L1_gnn_W2, L1_gnn_att_src2, L1_gnn_att_dst2, L1_gnn_b2, L1_mix_W_qkv, L1_mix_b_qkv, L1_mix_W_proj, L1_mix_b_proj, L1_ffn_gate_w, L1_ffn_w1, L1_ffn_w2, L1_ffn_w3, L1_ffn_sw1, L1_ffn_sw2, L1_ffn_sw3):
    import jax
    import jax.numpy as jnp

    def _L0_gnn_ref(x, edge_index, W, b):
        import jax, jax.numpy as jnp
        import numpy as np
        N_NODES = 1250
        N_EDGES = 12500
        DIM = 768
        n = x.shape[0]
        loop = jnp.arange(n, dtype=edge_index.dtype)
        src = jnp.concatenate([edge_index[0], loop])
        dst = jnp.concatenate([edge_index[1], loop])
        deg = jax.ops.segment_sum(jnp.ones_like(dst, dtype=x.dtype), dst, num_segments=n)
        deg_inv_sqrt = jnp.where(deg > 0, jax.lax.rsqrt(deg), 0.0)
        norm = deg_inv_sqrt[src] * deg_inv_sqrt[dst]
        h = x @ W
        msg = h[src] * norm[:, None]
        out = jax.ops.segment_sum(msg, dst, num_segments=n)
        return out + b

    def _L0_mix_ref(x, w_qkv, w_proj, b_proj):
        import jax, jax.numpy as jnp
        import numpy as np
        NUM_HEADS = 12

        def _reference_tuple_inner(x, w_qkv, w_proj, b_proj):
            B, N, C = x.shape
            H = NUM_HEADS
            D = C // H
            qkv = (x @ w_qkv).reshape(B, N, 3, H, D)
            q = jnp.transpose(qkv[:, :, 0], (0, 2, 1, 3))
            k = jnp.transpose(qkv[:, :, 1], (0, 2, 1, 3))
            v = jnp.transpose(qkv[:, :, 2], (0, 2, 1, 3))
            q = jax.nn.elu(q) + 1.0
            k = jax.nn.elu(k) + 1.0
            attn = jnp.einsum('bhnd,bhmd->bhnm', q, k)
            attn = attn / jnp.sum(attn, axis=-1, keepdims=True)
            out = jnp.einsum('bhnm,bhmd->bhnd', attn, v)
            out = jnp.transpose(out, (0, 2, 1, 3)).reshape(B, N, C)
            out = out @ w_proj + b_proj
            return (out, attn)
        return _reference_tuple_inner(x, w_qkv, w_proj, b_proj)[0]

    def _L0_ffn_ref(x, router_w, router_b, expert_w, expert_b):
        import jax, jax.numpy as jnp
        import numpy as np
        B, S, H = (4, 1024, 768)
        E, K = (8, 2)
        scores = jnp.einsum('bsh,eh->bse', x, router_w) + router_b
        probs = jax.nn.softmax(scores, axis=-1)
        top_probs, expert_ids = jax.lax.top_k(probs, K)
        y = jnp.einsum('bsh,edh->bsed', x, expert_w) + expert_b
        out_k = jnp.take_along_axis(y, expert_ids[..., None], axis=2)
        w = top_probs / (jnp.sum(top_probs, axis=-1, keepdims=True) + 1e-09)
        out = jnp.einsum('bsk,bskh->bsh', w, out_k)
        return out

    def _L1_gnn_ref(x, edge_index, W1, att_src1, att_dst1, b1, W2, att_src2, att_dst2, b2):
        import jax, jax.numpy as jnp
        import numpy as np
        N_NODES = 1250
        N_EDGES = 20000
        NEG_SLOPE = 0.2

        def _gat_layer(x, src, dst, W, a_src, a_dst, bias, concat):
            N = x.shape[0]
            H, C = a_src.shape
            h = (x @ W).reshape(N, H, C)
            al_s = jnp.einsum('nhc,hc->nh', h, a_src)
            al_d = jnp.einsum('nhc,hc->nh', h, a_dst)
            e = jax.nn.leaky_relu(al_s[src] + al_d[dst], NEG_SLOPE)
            m = jax.ops.segment_max(e, dst, num_segments=N)
            ex = jnp.exp(e - m[dst])
            denom = jax.ops.segment_sum(ex, dst, num_segments=N)
            alpha = ex / (denom[dst] + 1e-16)
            msg = h[src] * alpha[:, :, None]
            out = jax.ops.segment_sum(msg, dst, num_segments=N)
            out = out.reshape(N, H * C) if concat else out.mean(axis=1)
            return out + bias
        N = x.shape[0]
        loops = jnp.arange(N, dtype=edge_index.dtype)
        src = jnp.concatenate([edge_index[0], loops])
        dst = jnp.concatenate([edge_index[1], loops])
        h = jax.nn.elu(_gat_layer(x, src, dst, W1, att_src1, att_dst1, b1, concat=True))
        out = _gat_layer(h, src, dst, W2, att_src2, att_dst2, b2, concat=False)
        return out

    def _L1_mix_ref(x, W_qkv, b_qkv, W_proj, b_proj):
        import jax, jax.numpy as jnp
        import numpy as np
        NUM_HEADS = 12
        EPS = 1e-06
        B, N, C = x.shape
        H = NUM_HEADS
        D = C // H
        qkv = (x @ W_qkv + b_qkv).reshape(B, N, 3, H, D).transpose(2, 0, 3, 1, 4)
        q, k, v = (qkv[0], qkv[1], qkv[2])
        q = jax.nn.sigmoid(q)
        k = jax.nn.sigmoid(k)
        ksum = k.sum(axis=2)
        qsum = q.sum(axis=2)
        sink_incoming = 1.0 / (jnp.einsum('bhnd,bhd->bhn', q + EPS, ksum + EPS) + EPS)
        source_outgoing = 1.0 / (jnp.einsum('bhnd,bhd->bhn', k + EPS, qsum + EPS) + EPS)
        conserved_sink = jnp.einsum('bhnd,bhd->bhn', q + EPS, (k * source_outgoing[..., None]).sum(axis=2) + EPS) + EPS
        conserved_source = jnp.einsum('bhnd,bhd->bhn', k + EPS, (q * sink_incoming[..., None]).sum(axis=2) + EPS) + EPS
        conserved_source = jnp.clip(conserved_source, -1.0, 1.0)
        sink_allocation = jax.nn.sigmoid(conserved_sink * (float(N) / float(N)))
        source_competition = jax.nn.softmax(conserved_source, axis=-1) * float(N)
        kv = jnp.einsum('bhnd,bhne->bhde', k, v * source_competition[..., None])
        x_update = jnp.einsum('bhnd,bhde->bhne', q, kv)
        x_update = x_update * sink_incoming[..., None] * sink_allocation[..., None]
        out = x_update.transpose(0, 2, 1, 3).reshape(B, N, C)
        out = out @ W_proj + b_proj
        return jax.nn.sigmoid(2.0 * out)

    def _L1_ffn_ref(x, gate_w, w1, w2, w3, sw1, sw2, sw3):
        import jax, jax.numpy as jnp
        import numpy as np
        DIM = 768
        MOE_INTER = 256
        N_EXPERTS = 16
        TOP_K = 2
        SHARED_INTER = 2 * 256
        ROUTE_SCALE = 1.0
        B, S = (8, 196)
        Bb, Ss, D = x.shape
        xf = x.reshape(-1, D)
        T = xf.shape[0]
        scores = jax.nn.softmax(xf @ gate_w.T, axis=-1)
        topw, topi = jax.lax.top_k(scores, TOP_K)
        topw = topw * ROUTE_SCALE
        comb = jnp.zeros((T, N_EXPERTS), xf.dtype).at[jnp.arange(T)[:, None], topi].set(topw)
        h = jax.nn.silu(jnp.einsum('td,eid->tei', xf, w1)) * jnp.einsum('td,eid->tei', xf, w3)
        h = h * comb[:, :, None]
        y = jnp.einsum('tei,edi->td', h, w2)
        z = jax.nn.silu(xf @ sw1.T) * (xf @ sw3.T) @ sw2.T
        return (y + z).reshape(Bb, Ss, D)
    edge_index = jnp.stack([src, dst])
    xn = _layernorm(x, axis=-1)
    x = x + _L0_gnn_ref(xn, edge_index, L0_gnn_W, L0_gnn_b) + _L0_mix_ref(xn[None], L0_mix_w_qkv, L0_mix_w_proj, L0_mix_b_proj)[0]
    x = x + _L0_ffn_ref(_layernorm(x, axis=-1)[None], L0_ffn_router_w, L0_ffn_router_b, L0_ffn_expert_w, L0_ffn_expert_b)[0]
    xn = _layernorm(x, axis=-1)
    x = x + _L1_gnn_ref(xn, edge_index, L1_gnn_W1, L1_gnn_att_src1, L1_gnn_att_dst1, L1_gnn_b1, L1_gnn_W2, L1_gnn_att_src2, L1_gnn_att_dst2, L1_gnn_b2) + _L1_mix_ref(xn[None], L1_mix_W_qkv, L1_mix_b_qkv, L1_mix_W_proj, L1_mix_b_proj)[0]
    x = x + _L1_ffn_ref(_layernorm(x, axis=-1)[None], L1_ffn_gate_w, L1_ffn_w1, L1_ffn_w2, L1_ffn_w3, L1_ffn_sw1, L1_ffn_sw2, L1_ffn_sw3)[0]
    return x

_drawn_inputs = setup_inputs


def setup_inputs(seed=0):
    import zlib

    import numpy as np

    out = dict(_drawn_inputs(seed))
    spreads = {'L0_gnn_b': (0.0, 0.1),
     'L0_mix_b_proj': (0.0, 0.1),
     'L1_gnn_b1': (0.0, 0.1),
     'L1_gnn_b2': (0.0, 0.1)}
    factors = {'L0_ffn_expert_b': 4.299,
     'L1_gnn_att_dst1': 3.621,
     'L1_gnn_att_src2': 3.022,
     'L1_gnn_att_dst2': 8.0,
     'L1_mix_b_qkv': 8.0,
     'L1_mix_b_proj': 7.002,
     'L1_ffn_gate_w': 6.873,
     'L1_ffn_w1': 6.253,
     'L1_ffn_w2': 6.066,
     'L1_ffn_w3': 5.991,
     'L1_ffn_sw1': 8.0,
     'L1_ffn_sw2': 8.0,
     'L1_ffn_sw3': 8.0}
    for name, (base, spread) in spreads.items():
        noise = np.random.default_rng([zlib.crc32(name.encode()), seed]).standard_normal(out[name].shape)
        drawn = base * np.exp(spread * noise) if base else spread * noise
        out[name] = jnp.asarray(drawn.astype(out[name].dtype))
    for name, factor in factors.items():
        out[name] = (out[name] * factor).astype(out[name].dtype)
    return out
```

```python
import concourse.bass as bass
from concourse import mybir
from contextlib import ExitStack

F32 = mybir.dt.float32
F16 = mybir.dt.float16
BF16 = mybir.dt.bfloat16
I32 = mybir.dt.int32
U32 = mybir.dt.uint32
ACT = mybir.ActivationFunctionType
ALU = mybir.AluOpType
AX_X = mybir.AxisListType.X

P = 128
T = 1250
NT = 125
TILES = T // NT
CW = 418
CH = 3
TP = CW * CH
D = 768
FC = D // P
HALF = D // 2
EC = 160
EPS = 1e-5
BIG = -1.0e30


class Chain:

    def __init__(self, eng, sem, start=0):
        self.eng, self.sem, self.n = eng, sem, start

    def step(self, ins):
        self.n = self.n + 1
        return ins.then_inc(self.sem, 1)

    def wait(self):
        self.eng.wait_ge(self.sem, self.n)

    def then(self, ins):
        self.step(ins)
        self.wait()


class Kit:

    def __init__(self, nc, ctx):
        self.nc, self.ctx, self.sems, self.sem_ctx = nc, ctx, [], ctx

    def sb(self, name, shape, dt=F32, ctx=None):
        return (ctx or self.ctx).enter_context(self.nc.sbuf_tensor(name, shape, dt))

    def sem(self, name):
        handle = self.sem_ctx.enter_context(self.nc.semaphore(name))
        self.sems.append(handle)
        return handle

    def clear_sems(self):
        with self.nc.Block(no_gpsimd_drain=True) as block:
            @block.gpsimd
            def _(pool):
                for handle in self.sems:
                    pool.sem_clear(handle)
        self.sems = []


def cols(c):
    return slice(c * CW, (c + 1) * CW)


def tile_cols(t):
    return slice(t * NT, (t + 1) * NT)


def ones_stage(k):
    nc = k.nc
    k.ident = k.sb("ident", [P, P])
    k.ones = k.sb("ones", [P, P])
    k.avg = k.sb("avg", [P, P])
    k.heads2 = k.sb("heads2", [P, P])
    k.index16 = k.sb("index16", [P, 16])
    made, zeroed = k.sem("const_made"), k.sem("const_zeroed")
    with nc.Block(no_gpsimd_drain=True) as block:
        @block.gpsimd
        def _(pool):
            nc.gpsimd.memset(k.ident[:], 0.0).then_inc(zeroed, 1)
            pool.wait_ge(zeroed, 1)
            nc.gpsimd.affine_select(out=k.ident[:], in_=k.ident[:], compare_op=ALU.not_equal, fill=1.0, base=0,
                                    pattern=[[-1, P]], channel_multiplier=1).then_inc(zeroed, 1)
            pool.wait_ge(zeroed, 2)
            nc.gpsimd.iota(k.index16[:], [[1, 16]], base=0, channel_multiplier=0,
                           allow_small_or_imprecise_dtypes=True).then_inc(zeroed, 1)

        @block.vector
        def _(dve):
            nc.vector.memset(k.heads2[:], 0.0).then_inc(made, 1)
            nc.vector.memset(k.ones[:], 1.0).then_inc(made, 1)
            nc.vector.memset(k.avg[:], 1.0 / D).then_inc(made, 1)
            dve.wait_ge(made, 1)
            nc.vector.memset(k.heads2[0:64, 0:64], 1.0).then_inc(made, 1)
            nc.vector.memset(k.heads2[64:128, 64:128], 1.0).then_inc(made, 1)


def norm_nodes_stage(k, x_dram):
    nc, ps = k.nc, k.ps
    loaded = [k.sem(f"x_loaded{g}") for g in range(2)]
    order, stats, rooted, normed = k.sem("ln0_order"), k.sem("ln0_var"), k.sem("ln0_std"), k.sem("ln0_normed")
    turned, copied = k.sem("ln0_turned"), k.sem("ln0_copied")
    with ExitStack() as ctx:
        six = k.sb("ln0_six", [NT, TILES, 12], ctx=ctx)
        mv = k.sb("ln0_mv", [NT, TILES, 2], ctx=ctx)
        rstd = k.sb("ln0_rstd", [NT, TILES], ctx=ctx)
        with nc.Block(no_gpsimd_drain=True) as block:
            @block.sync
            def _(sp):
                for g in range(2):
                    sp.dma_start(k.x_node[:, 5 * g:5 * g + 5, :],
                                 x_dram[625 * g:625 * g + 625, :].rearrange("(t p) d -> p t d", p=NT)).then_inc(loaded[g], 16)

            @block.vector
            def _(dve):
                ch = Chain(dve, order)
                ch.step(nc.vector.memset(k.nT[:, :, T:TP], 0.0))
                for t in range(TILES):
                    dve.wait_ge(loaded[t // 5], 16)
                    for h in range(2):
                        ch.step(nc.vector.bn_stats(six[:, t, 6 * h:6 * h + 6], k.x_node[:, t, h * HALF:(h + 1) * HALF]))
                ch.wait()
                for t in range(TILES):
                    ch.step(nc.vector.bn_aggr(mv[:, t, :], six[:, t, :]))
                ch.wait()
                nc.vector.tensor_scalar(rstd[:], mv[:, :, 1], EPS, None, ALU.add).then_inc(stats, 1)
                dve.wait_ge(rooted, 1)
                ch.then(nc.vector.reciprocal(rstd[:], rstd[:]))
                for t in range(TILES):
                    nc.vector.tensor_scalar(k.x_node[:, t, :], k.x_node[:, t, :], mv[:, t, 0:1], rstd[:, t:t + 1],
                                            ALU.subtract, ALU.mult).then_inc(normed, 1)

            @block.tensor
            def _(pe):
                for c in range(FC):
                    if c >= 2:
                        pe.wait_ge(copied, c - 1)
                    for t in range(TILES):
                        if c == 0:
                            pe.wait_ge(normed, t + 1)
                        mm = nc.tensor.transpose(ps[:, 3 * (c % 2) + t // 4, NT * (t % 4):NT * (t % 4) + NT],
                                                 k.x_node[:, t, P * c:P * c + P], k.ident[0:NT, 0:NT])
                    mm.then_inc(turned, 1)

            @block.scalar
            def _(act):
                act.wait_ge(stats, 1)
                nc.scalar.activation(rstd[:], rstd[:], ACT.Sqrt).then_inc(rooted, 1)
                for c in range(FC):
                    g = 3 * (c % 2)
                    act.wait_ge(turned, c + 1)
                    nc.scalar.activation(k.nT[:, c, 0:8 * NT].rearrange("p (b n) -> p b n", b=2), ps[:, g:g + 2, 0:4 * NT], ACT.Copy)
                    nc.scalar.activation(k.nT[:, c, 8 * NT:T], ps[:, g + 2, 0:2 * NT], ACT.Copy).then_inc(copied, 1)


def linear_attention_stage(k, w_kv, w_q):
    nc, ps = k.nc, k.ps
    wl = [k.sem(f"la_weights{h}") for h in range(2)]
    kv_done, kv_low, kv_exp, kv_out = k.sem("la_kv_done"), k.sem("la_kv_low"), k.sem("la_kv_exp"), k.sem("la_kv_out")
    with ExitStack() as ctx:
        kv = k.sb("la_kv", [NT, TILES, 2 * D], ctx=ctx)
        kvb = k.sb("la_kvb", [P, FC, 2 * P], ctx=ctx)
        wk = k.sb("la_w", [P, 2, FC, HALF], ctx=ctx)
        low = k.sb("la_low", [NT, 2, HALF], ctx=ctx)
        with nc.Block(no_gpsimd_drain=True) as block:
            @block.sync
            def _(sp):
                for j in range(4):
                    if j >= 2:
                        sp.wait_ge(kv_done, TILES * (j - 1))
                    sp.dma_start(wk[:, j % 2, :, :], w_kv[j]).then_inc(wl[j % 2], 16)

            @block.tensor
            def _(pe):
                for j in range(4):
                    pe.wait_ge(wl[j % 2], 16 * (j // 2 + 1))
                    for t in range(TILES):
                        n = j * TILES + t
                        if n >= 8:
                            pe.wait_ge(kv_out, n - 7)
                        for c in range(FC):
                            mm = nc.tensor.matmul(ps[0:NT, n % 8, 0:HALF], k.nT[:, c, tile_cols(t)], wk[:, j % 2, c, :],
                                                  start=(c == 0), stop=(c == FC - 1))
                        mm.then_inc(kv_done, 1)

            @block.vector
            def _(dve):
                for n in range(2 * TILES):
                    j, t = n // TILES, n % TILES
                    dve.wait_ge(kv_done, n + 1)
                    if n >= 2:
                        dve.wait_ge(kv_out, n - 1)
                    nc.vector.tensor_scalar(low[:, n % 2, :], ps[0:NT, n % 8, 0:HALF], 0.0, None, ALU.min).then_inc(kv_low, 1)
                    dve.wait_ge(kv_exp, n + 1)
                    nc.vector.scalar_tensor_tensor(out=kv[:, t, HALF * j:HALF * j + HALF], in0=ps[0:NT, n % 8, 0:HALF], scalar=0.0,
                                                   in1=low[:, n % 2, :], op0=ALU.max, op1=ALU.add).then_inc(kv_out, 1)
                for n in range(2 * TILES, 4 * TILES):
                    j, t = n // TILES, n % TILES
                    dve.wait_ge(kv_done, n + 1)
                    nc.vector.tensor_copy(kv[:, t, HALF * j:HALF * j + HALF], ps[0:NT, n % 8, 0:HALF]).then_inc(kv_out, 1)

            @block.scalar
            def _(act):
                for n in range(2 * TILES):
                    act.wait_ge(kv_low, n + 1)
                    nc.scalar.activation(low[:, n % 2, :], low[:, n % 2, :], ACT.Exp).then_inc(kv_exp, 1)

        state, masked = k.sem("la_state"), k.sem("la_masked")
        with nc.Block(no_gpsimd_drain=True) as block:
            @block.tensor
            def _(pe):
                for p in range(FC):
                    for t in range(TILES):
                        nc.tensor.matmul(ps[:, p, 0:P], kv[:, t, P * p:P * p + P], kv[:, t, D + P * p:D + P * p + P],
                                         start=(t == 0), stop=(t == TILES - 1))
                    for t in range(TILES):
                        mm = nc.tensor.matmul(ps[:, p, P:2 * P], kv[:, t, P * p:P * p + P], k.ones[0:NT, :],
                                              start=(t == 0), stop=(t == TILES - 1))
                    mm.then_inc(state, 1)

            @block.vector
            def _(dve):
                for p in range(FC):
                    dve.wait_ge(state, p + 1)
                    for h in range(2):
                        nc.vector.tensor_tensor(kvb[:, p, h * P:h * P + P], ps[:, p, h * P:h * P + P], k.heads2[:],
                                                ALU.mult).then_inc(masked, 1)

        wq = wk[:, :, 0:2, :].rearrange("p s a (b n) -> p s (a b) n", b=3)
        q_in = [k.sem(f"la_qweights{h}") for h in range(2)]
        q_done, q_low, q_exp, q_out = k.sem("la_q_done"), k.sem("la_q_low"), k.sem("la_q_exp"), k.sem("la_q_out")
        nd_done, inverted, nd_out = k.sem("la_numden"), k.sem("la_inverted"), k.sem("la_out")
        q = kv[:, 0:2, 0:TP]
        with ExitStack() as ctx2:
            q = k.sb("la_q", [P, 2, TP], ctx=ctx2)
            qlow = k.sb("la_qlow", [P, TP], ctx=ctx2)
            rec = k.sb("la_rec", [P, 2, CW], ctx=ctx2)
            with nc.Block(no_gpsimd_drain=True) as block:
                @block.sync
                def _(sp):
                    for p in range(FC):
                        if p >= 2:
                            sp.wait_ge(q_done, p - 1)
                        sp.dma_start(wq[:, p % 2], w_q[p]).then_inc(q_in[p % 2], 16)

                @block.tensor
                def _(pe):
                    for p in range(FC + 1):
                        if p < FC:
                            pe.wait_ge(q_in[p % 2], 16 * (p // 2 + 1))
                            if p >= 1:
                                pe.wait_ge(q_out, p)
                            for c in range(CH):
                                for f in range(FC):
                                    mm = nc.tensor.matmul(ps[:, c, 0:CW], wq[:, p % 2, f, :], k.nT[:, f, cols(c)],
                                                          start=(f == 0), stop=(f == FC - 1))
                            mm.then_inc(q_done, 1)
                        if p >= 1:
                            pe.wait_ge(q_out, p)
                            for c in range(CH):
                                n = (p - 1) * CH + c
                                if n >= 2:
                                    pe.wait_ge(nd_out, n - 1)
                                for h in range(2):
                                    mm = nc.tensor.matmul(ps[:, 3 + 2 * h + n % 2, 0:CW], kvb[:, p - 1, h * P:h * P + P],
                                                          q[:, (p - 1) % 2, cols(c)], start=True, stop=True)
                                mm.then_inc(nd_done, 1)

                @block.vector
                def _(dve):
                    for p in range(FC + 1):
                        if p < FC:
                            dve.wait_ge(q_done, p + 1)
                            if p >= 1:
                                dve.wait_ge(q_out, p)
                            nc.vector.tensor_scalar(qlow[:].rearrange("p (c n) -> p c n", c=CH), ps[:, 0:CH, 0:CW], 0.0, None,
                                                    ALU.min).then_inc(q_low, 1)
                            dve.wait_ge(q_exp, p + 1)
                            if p >= 2:
                                dve.wait_ge(nd_done, CH * (p - 1))
                            nc.vector.scalar_tensor_tensor(out=q[:, p % 2, :].rearrange("p (c n) -> p c n", c=CH),
                                                           in0=ps[:, 0:CH, 0:CW], scalar=0.0,
                                                           in1=qlow[:].rearrange("p (c n) -> p c n", c=CH),
                                                           op0=ALU.max, op1=ALU.add).then_inc(q_out, 1)
                        if p >= 1:
                            for c in range(CH):
                                n = (p - 1) * CH + c
                                dve.wait_ge(nd_done, n + 1)
                                if n >= 2:
                                    dve.wait_ge(nd_out, n - 1)
                                nc.vector.reciprocal(rec[:, n % 2, :], ps[:, 5 + n % 2, 0:CW]).then_inc(inverted, 1)
                                dve.wait_ge(inverted, n + 1)
                                nc.vector.tensor_tensor(k.attT[:, p - 1, cols(c)], ps[:, 3 + n % 2, 0:CW], rec[:, n % 2, :],
                                                        ALU.mult).then_inc(nd_out, 1)

                @block.scalar
                def _(act):
                    for p in range(FC):
                        act.wait_ge(q_low, p + 1)
                        nc.scalar.activation(qlow[:], qlow[:], ACT.Exp).then_inc(q_exp, 1)


def counts_stage(k, src_dram, dst_dram):
    nc, ps = k.nc, k.ps
    U = 4
    e_in, e_f, row = k.sem("edges_in"), k.sem("edges_float"), k.sem("index_row")
    hot, spent = k.sem("onehot_made"), k.sem("onehot_used")
    fin, staged, diag, summed = k.sem("counts_done"), k.sem("counts_staged"), k.sem("counts_diag"), k.sem("counts_summed")
    turned, placed, far_out = k.sem("counts_turned"), k.sem("counts_placed"), [k.sem(f"far_stored{h}") for h in range(2)]
    with ExitStack() as ctx:
        ei = k.sb("edge_int", [NT, 2, EC], I32, ctx=ctx)
        ef = k.sb("edge_float", [NT, 2, EC], F32, ctx=ctx)
        idx = k.sb("index_row", [NT, TP], F16, ctx=ctx)
        zero = k.sb("zero_weights", [NT, NT], F16, ctx=ctx)
        hs = k.sb("hot_src", [NT, U, TP], F16, ctx=ctx)
        hd = k.sb("hot_dst", [NT, U, 2 * NT], F16, ctx=ctx)
        st = k.sb("counts_rows", [NT, 2, TP], F32, ctx=ctx)
        far = k.sb("far_rows", [NT, 2, TP], BF16, ctx=ctx)
        with nc.Block(no_gpsimd_drain=True) as block:
            @block.sync
            def _(sp):
                sp.dma_start(ei[:, 0, :], src_dram).then_inc(e_in, 16)
                sp.dma_start(ei[:, 1, :], dst_dram).then_inc(e_in, 16)
                for t in range(TILES):
                    sp.wait_ge(summed, 2 * t + 2)
                    sp.dma_start(k.far_dram[t], far[:, t % 2, 0:T]).then_inc(far_out[t % 2], 16)
                for h in range(2):
                    sp.wait_ge(far_out[h], 16 * (TILES // 2))

            @block.gpsimd
            def _(pool):
                nc.gpsimd.memset(zero[:], 0.0).then_inc(row, 1)
                nc.gpsimd.iota(idx[:], [[1, TP]], base=0, channel_multiplier=0,
                               allow_small_or_imprecise_dtypes=True).then_inc(row, 1)

            @block.vector
            def _(dve):
                dve.wait_ge(e_in, 32)
                nc.vector.tensor_copy(ef[:], ei[:]).then_inc(e_f, 1)
                nc.vector.memset(k.counts[:, :, T:TP], 0.0)
                dve.wait_ge(e_f, 1)
                dve.wait_ge(row, 2)

                def make(g, i):
                    for u in range(U):
                        e = i * U + u
                        if not (g == 0 and isinstance(i, int)):
                            dve.wait_ge(spent, g * EC + e - U + 1)
                        nc.vector.tensor_scalar(hs[:, u, :], idx[:], ef[:, 0, bass.ds(e, 1)], None, ALU.is_equal)
                        nc.vector.tensor_scalar(hd[:, u, :], idx[:, 2 * NT * g:2 * NT * (g + 1)], ef[:, 1, bass.ds(e, 1)],
                                                None, ALU.is_equal).then_inc(hot, 1)

                for g in range(TILES // 2):
                    make(g, 0)
                    with dve.Fori(1, EC // U) as i:
                        make(g, i)
                    for h in range(2):
                        t = 2 * g + h
                        dve.wait_ge(staged, t + 1)
                        nc.vector.tensor_tensor(st[:, h, tile_cols(t)], st[:, h, tile_cols(t)], k.ident[0:NT, 0:NT],
                                                ALU.add).then_inc(diag, 1)
                        dve.wait_ge(diag, t + 1)
                        if t >= 2:
                            dve.wait_ge(far_out[h], 16 * (t // 2))
                        nc.vector.tensor_reduce(k.dinv[:, t:t + 1], st[:, h, 0:T], AX_X, ALU.add).then_inc(summed, 1)
                        nc.vector.tensor_scalar(far[:, h, :], st[:, h, :], 0.0, BIG, ALU.is_equal, ALU.mult).then_inc(summed, 1)

            @block.tensor
            def _(pe):
                pe.wait_ge(row, 2)
                for g in range(TILES // 2):
                    if g >= 1:
                        pe.wait_ge(staged, 2 * g)
                    for h in range(2):
                        for c in range(CH):
                            nc.tensor.matmul(ps[0:NT, 3 * h + c, 0:CW], zero[:], idx[:, cols(c)], start=True, stop=False,
                                             skip_group_check=True)
                    with pe.Fori(0, EC // U) as i:
                        for u in range(U):
                            pe.wait_ge(hot, g * EC + i * U + u + 1)
                            for h in range(2):
                                for c in range(CH):
                                    mm = nc.tensor.matmul(ps[0:NT, 3 * h + c, 0:CW], hd[:, u, h * NT:(h + 1) * NT],
                                                          hs[:, u, cols(c)], start=False, stop=False, skip_group_check=True)
                            mm.then_inc(spent, 1)
                    for h in range(2):
                        for c in range(CH):
                            mm = nc.tensor.matmul(ps[0:NT, 3 * h + c, 0:CW], zero[:], idx[:, cols(c)], start=False, stop=True,
                                                  skip_group_check=True)
                    mm.then_inc(fin, 1)
                    for h in range(2):
                        t = 2 * g + h
                        pe.wait_ge(diag, t + 1)
                        for q in range(3):
                            n = 3 * t + q
                            if n >= 2:
                                pe.wait_ge(placed, n - 1)
                            for s in range(4 * q, min(4 * q + 4, TILES)):
                                mm = nc.tensor.transpose(ps[0:NT, 6 + n % 2, NT * (s % 4):NT * (s % 4) + NT],
                                                         st[:, h, tile_cols(s)], k.ident[0:NT, 0:NT])
                            mm.then_inc(turned, 1)

            @block.scalar
            def _(act):
                for g in range(TILES // 2):
                    act.wait_ge(fin, g + 1)
                    for h in range(2):
                        t = 2 * g + h
                        if g >= 1:
                            act.wait_ge(summed, 2 * (t - 1))
                        nc.scalar.activation(st[:, h, :].rearrange("p (c n) -> p c n", c=CH), ps[0:NT, 3 * h:3 * h + CH, 0:CW],
                                             ACT.Copy).then_inc(staged, 1)
                    for h in range(2):
                        t = 2 * g + h
                        for q in range(3):
                            n = 3 * t + q
                            m = min(4, TILES - 4 * q)
                            act.wait_ge(turned, n + 1)
                            nc.scalar.activation(k.counts[:, 4 * q:4 * q + m, tile_cols(t)],
                                                 ps[0:NT, 6 + n % 2, 0:m * NT].rearrange("p (s n) -> p s n", s=m),
                                                 ACT.Copy).then_inc(placed, 1)


def spread(nc, k, eng, diag, column, made):
    nc.vector.tensor_scalar(diag, k.ident[0:NT, 0:NT], column, None, ALU.mult).then_inc(made, 1)


def aggregate_stage(k):
    nc, ps = k.nc, k.ps
    rooted, inv, scaled, dg = k.sem("deg_root"), k.sem("deg_inverse"), k.sem("agg_scaled"), k.sem("agg_diag")
    rowd, rows_out, done, out = k.sem("agg_row"), k.sem("agg_row_out"), k.sem("agg_done"), k.sem("agg_out")
    with ExitStack() as ctx:
        dg_sb = k.sb("agg_diag", [NT, TILES, NT], ctx=ctx)
        dinvb = k.sb("dinv_rows", [P, TP], ctx=ctx)
        with nc.Block(no_gpsimd_drain=True) as block:
            @block.scalar
            def _(act):
                nc.scalar.activation(k.dinv[:], k.dinv[:], ACT.Sqrt).then_inc(rooted, 1)
                act.wait_ge(rowd, 1)
                nc.scalar.activation(dinvb[:, 0:1000].rearrange("p (b n) -> p b n", b=2), ps[:, 6:8, 0:500], ACT.Copy)
                nc.scalar.activation(dinvb[:, 1000:T], ps[:, 5, 0:250], ACT.Copy).then_inc(rows_out, 1)

            @block.vector
            def _(dve):
                nc.vector.memset(dinvb[:, T:TP], 0.0)
                dve.wait_ge(rooted, 1)
                nc.vector.reciprocal(k.dinv[:], k.dinv[:]).then_inc(inv, 1)
                dve.wait_ge(inv, 1)
                for t in range(TILES):
                    nc.vector.tensor_scalar(k.x_node[:, t, :], k.x_node[:, t, :], k.dinv[:, t:t + 1], None,
                                            ALU.mult).then_inc(scaled, 1)
                for t in range(TILES):
                    nc.vector.tensor_scalar(dg_sb[:, t, :], k.ident[0:NT, 0:NT], k.dinv[:, t:t + 1], None, ALU.mult).then_inc(dg, 1)
                dve.wait_ge(rows_out, 1)
                for f in range(FC):
                    dve.wait_ge(done, f + 1)
                    g = 3 * (f % 2) if f else 0
                    nc.vector.tensor_tensor(k.nT[:, f, :].rearrange("p (c n) -> p c n", c=CH), ps[:, g:g + CH, 0:CW],
                                            dinvb[:].rearrange("p (c n) -> p c n", c=CH), ALU.mult).then_inc(out, 1)

            @block.tensor
            def _(pe):
                pe.wait_ge(dg, TILES)
                for t in range(TILES):
                    b = (6, 7, 5)[t // 4]
                    mm = nc.tensor.matmul(ps[:, b, NT * (t % 4):NT * (t % 4) + NT], k.ones[0:NT, :], dg_sb[:, t, :],
                                          start=True, stop=True)
                mm.then_inc(rowd, 1)
                pe.wait_ge(scaled, TILES)
                for f in range(FC):
                    if f == 1:
                        pe.wait_ge(rows_out, 1)
                    if f >= 2:
                        pe.wait_ge(out, f - 1)
                    for t in range(TILES):
                        for c in range(CH):
                            mm = nc.tensor.matmul(ps[:, 3 * (f % 2) + c, 0:CW], k.x_node[:, t, P * f:P * f + P],
                                                  k.counts[:, t, cols(c)], start=(t == 0), stop=(t == TILES - 1))
                    mm.then_inc(done, 1)


def project_stage(k, name, ins, w_dram, evacuate, extra_in=None):
    nc, ps = k.nc, k.ps
    nk = sum(n for _, n in ins)
    wl = [k.sem(f"{name}_weights{h}") for h in range(2)]
    done, out = k.sem(f"{name}_done"), k.sem(f"{name}_out")
    with ExitStack() as ctx:
        w = k.sb(f"{name}_w", [P, 2, nk, P], ctx=ctx)
        with nc.Block(no_gpsimd_drain=True) as block:
            @block.sync
            def _(sp):
                if extra_in:
                    extra_in(sp)
                for o in range(FC):
                    if o >= 2:
                        sp.wait_ge(done, o - 1)
                    sp.dma_start(w[:, o % 2], w_dram[o]).then_inc(wl[o % 2], 16)

            @block.tensor
            def _(pe):
                def pair(i):
                    for h in range(2):
                        pe.wait_ge(wl[h], 16 * i + 16)
                        if not isinstance(i, int):
                            pe.wait_ge(out, 2 * i + h - 1)
                        n = 0
                        for src, m in ins:
                            for f in range(m):
                                for c in range(CH):
                                    mm = nc.tensor.matmul(ps[:, 3 * h + c, 0:CW], w[:, h, n, :], src[:, f, cols(c)],
                                                          start=(n == 0), stop=(n == nk - 1))
                                n += 1
                        mm.then_inc(done, 1)
                pair(0)
                with pe.Fori(1, FC // 2) as i:
                    pair(i)

            @block.vector
            def _(dve):
                evacuate(dve, done, out)


def mix_project_stage(k, w_dram, bias_dram, x_dram):
    nc, ps = k.nc, k.ps
    x_in, b_in, badd = k.sem("x1_x"), k.sem("x1_bias"), k.sem("x1_bias_sum")
    with ExitStack() as ctx:
        bias = k.sb("x1_bias", [P, 2, FC], ctx=ctx)

        def loads(sp):
            for j in range(2):
                sp.dma_start(bias[:, j, :], bias_dram[j]).then_inc(b_in, 16)
            sp.dma_start(k.xT[:, :, 0:T], x_dram).then_inc(x_in, 16)

        def evacuate(dve, done, out):
            nc.vector.memset(k.xT[:, :, T:TP], 0.0).then_inc(badd, 1)
            dve.wait_ge(b_in, 32)
            nc.vector.tensor_tensor(bias[:, 0, :], bias[:, 0, :], bias[:, 1, :], ALU.add).then_inc(badd, 1)
            dve.wait_ge(badd, 2)
            dve.wait_ge(x_in, 16)
            for o in range(FC):
                dve.wait_ge(done, o + 1)
                g = 3 * (o % 2)
                xo = k.xT[:, o, :].rearrange("p (c n) -> p c n", c=CH)
                nc.vector.scalar_tensor_tensor(out=xo, in0=ps[:, g:g + CH, 0:CW], scalar=bias[:, 0, o:o + 1], in1=xo,
                                               op0=ALU.add, op1=ALU.add).then_inc(out, 1)
        project_stage(k, "x1", [(k.nT, FC), (k.attT, FC)], w_dram, evacuate, loads)


def norm_stage(k, name):
    nc, ps = k.nc, k.ps
    mean, cen, sq, var, eps, root, rec = (k.sem(f"{name}_{x}") for x in
                                          ("mean", "centred", "squared", "var", "eps", "root", "inverse"))
    with ExitStack() as ctx:
        s = k.sb(f"{name}_sq", [P, 2, TP], ctx=ctx)
        r = k.sb(f"{name}_r", [P, TP], ctx=ctx)
        r3 = r[:].rearrange("p (c n) -> p c n", c=CH)
        with nc.Block(no_gpsimd_drain=True) as block:
            @block.tensor
            def _(pe):
                for f in range(FC):
                    for c in range(CH):
                        mm = nc.tensor.matmul(ps[:, c, 0:CW], k.avg[:], k.xT[:, f, cols(c)], start=(f == 0), stop=(f == FC - 1))
                mm.then_inc(mean, 1)
                for f in range(FC):
                    pe.wait_ge(sq, f + 1)
                    for c in range(CH):
                        mm = nc.tensor.matmul(ps[:, 3 + c, 0:CW], k.avg[:], s[:, f % 2, cols(c)], start=(f == 0), stop=(f == FC - 1))
                    mm.then_inc(var, 1)

            @block.vector
            def _(dve):
                dve.wait_ge(mean, 1)
                for f in range(FC):
                    nc.vector.tensor_tensor(k.nT[:, f, :].rearrange("p (c n) -> p c n", c=CH),
                                            k.xT[:, f, :].rearrange("p (c n) -> p c n", c=CH), ps[:, 0:CH, 0:CW],
                                            ALU.subtract).then_inc(cen, 1)
                dve.wait_ge(var, FC)
                nc.vector.tensor_scalar(r3, ps[:, 3:6, 0:CW], EPS, None, ALU.add).then_inc(eps, 1)
                dve.wait_ge(root, 1)
                nc.vector.reciprocal(r[:], r[:]).then_inc(rec, 1)
                dve.wait_ge(rec, 1)
                for f in range(FC):
                    nc.vector.tensor_tensor(k.nT[:, f, :], k.nT[:, f, :], r[:], ALU.mult)

            @block.scalar
            def _(act):
                for f in range(FC):
                    act.wait_ge(cen, f + 1)
                    if f >= 2:
                        act.wait_ge(var, f - 1)
                    nc.scalar.activation(s[:, f % 2, :], k.nT[:, f, :], ACT.Square).then_inc(sq, 1)
                act.wait_ge(eps, 1)
                nc.scalar.activation(r[:], r[:], ACT.Sqrt).then_inc(root, 1)


def router_stage(k, name, E, rw_dram, rb_dram, renormalise, comb_dram, shared=0):
    nc, ps = k.nc, k.ps
    w_in, b_in, done, order, ex, turned, laid, stored = (k.sem(f"{name}_{x}") for x in (
        "w_in", "b_in", "scores", "order", "exp", "turned", "laid", "stored"))
    b0 = k.sem(f"{name}_neg")
    with ExitStack() as ctx:
        w = k.sb(f"{name}_w", [P, FC, E], ctx=ctx)
        rb = k.sb(f"{name}_b", [NT, E], ctx=ctx)
        sc = k.sb(f"{name}_sc", [NT, TILES, E], ctx=ctx)
        ex_sb = k.sb(f"{name}_ex", [NT, TILES, E], ctx=ctx)
        top = k.sb(f"{name}_top", [NT, TILES, 8], ctx=ctx)
        idx = k.sb(f"{name}_idx", [NT, TILES, 8], U32, ctx=ctx)
        idf = k.sb(f"{name}_idf", [NT, TILES, 8], ctx=ctx)
        tmp = k.sb(f"{name}_tmp", [NT, 6, TILES], ctx=ctx)
        pr = k.sb(f"{name}_pr", [NT, TILES, 2], ctx=ctx)
        comb = k.sb(f"{name}_comb", [NT, 2, TILES, E], ctx=ctx)
        combT = k.sb(f"{name}_combT", [E, TP], ctx=ctx)
        always = k.sb(f"{name}_always", [2, TP], ctx=ctx)
        with nc.Block(no_gpsimd_drain=True) as block:
            @block.sync
            def _(sp):
                sp.dma_start(w[:], rw_dram).then_inc(w_in, 16)
                if rb_dram is not None:
                    sp.dma_start(rb[:], rb_dram.partition_broadcast(NT)).then_inc(b_in, 16)
                sp.wait_ge(laid, 1)
                sp.dma_start(comb_dram[0:E, :], combT[:]).then_inc(stored, 16)
                if shared:
                    sp.wait_ge(order, 1)
                    sp.dma_start(comb_dram[E:E + shared, :], always[:]).then_inc(stored, 16)
                sp.wait_ge(stored, 32 if shared else 16)

            @block.tensor
            def _(pe):
                pe.wait_ge(w_in, 16)
                for t in range(TILES):
                    for f in range(FC):
                        mm = nc.tensor.matmul(ps[0:NT, 0, E * t:E * t + E], k.nT[:, f, tile_cols(t)], w[:, f, :],
                                              start=(f == 0), stop=(f == FC - 1))
                mm.then_inc(done, 1)
                pe.wait_ge(b0, 2)
                for t in range(TILES):
                    mm = nc.tensor.transpose(ps[0:E, 1 + t // 4, NT * (t % 4):NT * (t % 4) + NT], comb[:, 0, t, :],
                                             k.ident[0:NT, 0:NT])
                mm.then_inc(turned, 1)

            @block.scalar
            def _(act):
                act.wait_ge(b0, 1)
                nc.scalar.activation(ex_sb[:], ex_sb[:], ACT.Exp)
                nc.scalar.activation(tmp[:, 1, :], tmp[:, 0, :], ACT.Exp).then_inc(ex, 1)
                act.wait_ge(turned, 1)
                nc.scalar.activation(combT[:, 0:1000].rearrange("p (b n) -> p b n", b=2), ps[0:E, 1:3, 0:500], ACT.Copy)
                nc.scalar.activation(combT[:, 1000:T], ps[0:E, 3, 0:250], ACT.Copy).then_inc(laid, 1)

            @block.vector
            def _(dve):
                ch = Chain(dve, order)
                ch.step(nc.vector.memset(always[:], 1.0))
                ch.step(nc.vector.memset(combT[:, T:TP], 0.0))
                dve.wait_ge(done, 1)
                s3 = ps[0:NT, 0, 0:TILES * E].rearrange("p (t e) -> p t e", t=TILES)
                if rb_dram is not None:
                    dve.wait_ge(b_in, 16)
                    ch.then(nc.vector.tensor_tensor(sc[:], s3, rb[:].unsqueeze(1).broadcast_to([NT, TILES, E]), ALU.add))
                else:
                    ch.then(nc.vector.tensor_copy(sc[:], s3))
                for t in range(TILES):
                    ch.step(nc.vector.max(top[:, t, :], sc[:, t, :]))
                ch.wait()
                for t in range(TILES):
                    ch.step(nc.vector.max_index(idx[:, t, :], top[:, t, :], sc[:, t, :]))
                    ch.step(nc.vector.tensor_scalar(ex_sb[:, t, :], sc[:, t, :], top[:, t, 0:1], None, ALU.subtract))
                ch.wait()
                nc.vector.tensor_tensor(tmp[:, 0, :], top[:, :, 1], top[:, :, 0], ALU.subtract).then_inc(b0, 1)
                ch.step(nc.vector.tensor_copy(idf[:], idx[:]))
                dve.wait_ge(ex, 1)
                ch.then(nc.vector.tensor_reduce(tmp[:, 2, :], ex_sb[:], AX_X, ALU.add))
                ch.then(nc.vector.reciprocal(tmp[:, 3, :], tmp[:, 2, :]))
                ch.step(nc.vector.tensor_copy(pr[:, :, 0], tmp[:, 3, :]))
                ch.then(nc.vector.tensor_tensor(pr[:, :, 1], tmp[:, 1, :], tmp[:, 3, :], ALU.mult))
                if renormalise:
                    ch.then(nc.vector.tensor_reduce(tmp[:, 4, :], pr[:], AX_X, ALU.add))
                    ch.then(nc.vector.tensor_scalar(tmp[:, 4, :], tmp[:, 4, :], 1e-9, None, ALU.add))
                    ch.then(nc.vector.reciprocal(tmp[:, 5, :], tmp[:, 4, :]))
                    for j in range(2):
                        ch.step(nc.vector.tensor_tensor(pr[:, :, j], pr[:, :, j], tmp[:, 5, :], ALU.mult))
                    ch.wait()
                for t in range(TILES):
                    for j in range(2):
                        ch.step(nc.vector.tensor_scalar(comb[:, j, t, :], k.index16[0:NT, 0:E], idf[:, t, j:j + 1], pr[:, t, j:j + 1],
                                                        ALU.is_equal, ALU.mult))
                ch.wait()
                nc.vector.tensor_tensor(comb[:, 0, :, :], comb[:, 0, :, :], comb[:, 1, :, :], ALU.add).then_inc(b0, 1)


def experts_stage(k, w_dram, eb_dram, comb_dram, E):
    nc, ps = k.nc, k.ps
    wl = [k.sem(f"ex_weights{h}") for h in range(2)]
    cb = [k.sem(f"ex_comb{h}") for h in range(2)]
    done, out, scaled, eb_in = k.sem("ex_done"), k.sem("ex_out"), k.sem("ex_scaled"), k.sem("ex_bias_in")
    with ExitStack() as ctx:
        w = k.sb("ex_w", [P, 2, FC, P], ctx=ctx)
        cbs = k.sb("ex_comb", [P, 2, TP], ctx=ctx)
        tmp = k.sb("ex_tmp", [P, 2, TP], ctx=ctx)
        eb = k.sb("ex_eb", [E, D], ctx=ctx)
        ct = k.sb("ex_ct", [E, TP], ctx=ctx)
        with nc.Block(no_gpsimd_drain=True) as block:
            @block.sync
            def _(sp):
                sp.dma_start(eb[:], eb_dram).then_inc(eb_in, 16)
                sp.dma_start(ct[:], comb_dram[:, :]).then_inc(eb_in, 16)

                def expert_pair(i):
                    for j in range(2):
                        if not isinstance(i, int):
                            sp.wait_ge(out, FC * (2 * i + j - 1) + FC)
                        sp.dma_start(cbs[:, j, :], comb_dram[bass.ds(2 * i + j, 1), :].partition_broadcast(P) if False else
                                     comb_dram[bass.ds(2 * i + j, 1), :].broadcast_to([P, TP])).then_inc(cb[j], 16)
                        for o in range(FC):
                            if not (isinstance(i, int) and j == 0 and o < 2):
                                sp.wait_ge(done, FC * (2 * i + j + 1) + o - 1)
                            sp.dma_start(w[:, o % 2], w_dram[2 * i + j, o]).then_inc(wl[o % 2], 16)
                expert_pair(0)
                with sp.Fori(1, E // 2) as i:
                    expert_pair(i)

            @block.tensor
            def _(pe):
                pe.wait_ge(eb_in, 32)
                for o in range(FC):
                    if o >= 2:
                        pe.wait_ge(out, o - 1)
                    for c in range(CH):
                        mm = nc.tensor.matmul(ps[:, 3 * (o % 2) + c, 0:CW], eb[:, P * o:P * o + P], ct[:, cols(c)], start=True, stop=True)
                    mm.then_inc(done, 1)
                with pe.Fori(0, E) as i:
                    for o in range(FC):
                        pe.wait_ge(wl[o % 2], (i * 3 + o // 2 + 1) * 16)
                        pe.wait_ge(out, FC * i + FC + o - 1)
                        for f in range(FC):
                            for c in range(CH):
                                mm = nc.tensor.matmul(ps[:, 3 * (o % 2) + c, 0:CW], w[:, o % 2, f, :], k.nT[:, f, cols(c)],
                                                      start=(f == 0), stop=(f == FC - 1))
                        mm.then_inc(done, 1)

            @block.vector
            def _(dve):
                def three(a):
                    return a.rearrange("p (c n) -> p c n", c=CH)
                for o in range(FC):
                    dve.wait_ge(done, o + 1)
                    g = 3 * (o % 2)
                    nc.vector.tensor_tensor(three(k.xT[:, o, :]), three(k.xT[:, o, :]), ps[:, g:g + CH, 0:CW], ALU.add).then_inc(out, 1)
                with dve.Fori(0, E // 2) as i:
                    for j in range(2):
                        dve.wait_ge(cb[j], 16 * i + 16)
                        for o in range(FC):
                            n = FC * (2 * i + j) + o
                            g = 3 * (o % 2)
                            dve.wait_ge(done, n + FC + 1)
                            dve.wait_ge(out, n + FC)
                            nc.vector.tensor_tensor(three(tmp[:, o % 2, :]), ps[:, g:g + CH, 0:CW], three(cbs[:, j, :]),
                                                    ALU.mult).then_inc(scaled, 1)
                            dve.wait_ge(scaled, n + 1)
                            nc.vector.tensor_tensor(k.xT[:, o, :], k.xT[:, o, :], tmp[:, o % 2, :], ALU.add).then_inc(out, 1)


def flow_attention_stage(k, w_qk, b_qk, w_v, b_v):
    nc, ps = k.nc, k.ps
    H = 2 * FC
    E6 = 1e-6
    s = {n: k.sem("fa_" + n) for n in (
        "qk_done", "qk_out", "turned", "copied", "order", "dots1", "dots2", "flow1", "sums", "v_done", "v_out",
        "columns", "flow2", "exp", "total", "comp", "vscaled", "kv", "kv_out", "att", "att_out", "att_turned", "att_copied",
        "cols_in", "eps_made")}
    wl = [k.sem(f"fa_weights{h}") for h in range(2)]
    with ExitStack() as ctx:
        qT = k.sb("fa_qT", [P, FC, TP], ctx=ctx)
        kT = k.attT
        q_node = k.sb("fa_q_node", [NT, TILES, D], ctx=ctx)
        k_node = k.sb("fa_k_node", [NT, TILES, D], ctx=ctx)
        w = k.sb("fa_w", [P, 2, FC, HALF], ctx=ctx)
        ws = w[:].rearrange("p s f n -> p s (f n)")[:, :, 0:D].rearrange("p s (f n) -> p s f n", f=FC)
        bqk = k.sb("fa_bqk", [P, 2 * FC], ctx=ctx)
        part = k.sb("fa_part", [P, 2 * FC, CH], ctx=ctx)
        vec = k.sb("fa_vec", [P, 2 * FC], ctx=ctx)
        head2 = k.sb("fa_head2", [P, 2], ctx=ctx)
        cl = k.sb("fa_columns", [P, 2, 2, FC, 2], ctx=ctx)
        epsm = k.sb("fa_eps", [P, NT], ctx=ctx)
        epsr = k.sb("fa_eps_rows", [NT, 2, H], ctx=ctx)
        fl = k.sb("fa_flow", [NT, 5, TILES, H], ctx=ctx)
        tot = epsr
        kvb = k.sb("fa_kvb", [P, FC, P], ctx=ctx)
        v_node, mix_node = q_node, k_node
        with nc.Block(no_gpsimd_drain=True) as block:
            @block.sync
            def _(sp):
                sp.dma_start(bqk[:], b_qk).then_inc(s["cols_in"], 16)
                for j in range(2 * FC):
                    if j >= 2:
                        sp.wait_ge(s["qk_done"], CH * (j - 1))
                    sp.dma_start(ws[:, j % 2], w_qk[j]).then_inc(wl[j % 2], 16)

            @block.vector
            def _(dve):
                nc.vector.tensor_copy(head2[:], k.heads2[:, 0:P:64])
                nc.vector.memset(epsm[:], E6).then_inc(s["eps_made"], 1)
                nc.vector.memset(qT[:, :, T:TP], 0.0)
                nc.vector.memset(kT[:, :, T:TP], 0.0)
                for g in range(2 * FC):
                    for q in range(3):
                        n = 3 * g + q
                        m = min(4, TILES - 4 * q)
                        dst, c = (q_node, g) if g < FC else (k_node, g - FC)
                        dve.wait_ge(s["turned"], n + 1)
                        nc.vector.tensor_copy(dst[:, 4 * q:4 * q + m, P * c:P * c + P],
                                              ps[0:NT, 6 + n % 2, 0:m * P].rearrange("p (t d) -> p t d", t=m)).then_inc(s["copied"], 1)

            @block.scalar
            def _(act):
                act.wait_ge(s["cols_in"], 16)
                for j in range(2 * FC):
                    dst = (qT if j < FC else kT)[:, j % FC, :]
                    for c in range(CH):
                        n = j * CH + c
                        act.wait_ge(s["qk_done"], n + 1)
                        wd = min(CW, T - c * CW)
                        nc.scalar.activation(dst[:, c * CW:c * CW + wd], ps[:, n % 6, 0:wd], ACT.Sigmoid, bias=bqk[:, j:j + 1],
                                             accum_out=part[:, j, c:c + 1]).then_inc(s["qk_out"], 1)

            @block.tensor
            def _(pe):
                def turn(g):
                    src, c = (qT, g) if g < FC else (kT, g - FC)
                    pe.wait_ge(s["qk_out"], CH * (g + 1))
                    for q in range(3):
                        n = 3 * g + q
                        if n >= 2:
                            pe.wait_ge(s["copied"], n - 1)
                        for t in range(4 * q, min(4 * q + 4, TILES)):
                            mm = nc.tensor.transpose(ps[0:NT, 6 + n % 2, P * (t % 4):P * (t % 4) + P], src[:, c, tile_cols(t)],
                                                     k.ident[:])
                        mm.then_inc(s["turned"], 1)
                for j in range(2 * FC):
                    pe.wait_ge(wl[j % 2], 16 * (j // 2 + 1))
                    for c in range(CH):
                        n = j * CH + c
                        if n >= 6:
                            pe.wait_ge(s["qk_out"], n - 5)
                        for f in range(FC):
                            mm = nc.tensor.matmul(ps[:, n % 6, 0:CW], ws[:, j % 2, f, :], k.nT[:, f, cols(c)],
                                                  start=(f == 0), stop=(f == FC - 1))
                        mm.then_inc(s["qk_done"], 1)
                    if j >= 1:
                        turn(j - 1)
                turn(2 * FC - 1)

        b_in, v_in = k.sem("fa_vbias_in"), [k.sem(f"fa_v_in{h}") for h in range(2)]
        bv = k.sb("fa_bv", [NT, D], ctx=ctx)
        with nc.Block(no_gpsimd_drain=True) as block:
            @block.sync
            def _(sp):
                sp.dma_start(bv[:], b_v.partition_broadcast(NT)).then_inc(b_in, 16)
                for h in range(2):
                    sp.dma_start(w[:, h], w_v[h]).then_inc(v_in[h], 16)

            @block.tensor
            def _(pe):
                def dots(step, done):
                    for side, src in ((0, qT), (1, kT)):
                        for t in range(TILES):
                            for p in range(FC):
                                nc.tensor.matmul(ps[0:NT, side, H * t + 2 * p:H * t + 2 * p + 2], src[:, p, tile_cols(t)],
                                                 cl[:, step, side, p, :], start=True, stop=True)
                    for side in range(2):
                        for p in range(FC):
                            mm = nc.tensor.matmul(ps[0:NT, 2, H * side + 2 * p:H * side + 2 * p + 2], epsm[:],
                                                  cl[:, step, side, p, :], start=True, stop=True)
                    mm.then_inc(done, 1)
                pe.wait_ge(s["columns"], 1)
                dots(0, s["dots1"])
                pe.wait_ge(s["flow1"], 2)
                for side, src, wt in ((0, k_node, 1), (1, q_node, 0)):
                    for p in range(FC):
                        for t in range(TILES):
                            mm = nc.tensor.matmul(ps[:, 3 + side, 2 * p:2 * p + 2], src[:, t, P * p:P * p + P],
                                                  fl[:, wt, t, 2 * p:2 * p + 2], start=(t == 0), stop=(t == TILES - 1))
                mm.then_inc(s["sums"], 1)
                pe.wait_ge(s["columns"], 2)
                dots(1, s["dots2"])
                for h in range(2):
                    pe.wait_ge(v_in[h], 16)
                    for t in range(TILES):
                        n = h * TILES + t
                        if n >= 3:
                            pe.wait_ge(s["v_out"], n - 2)
                        for f in range(FC):
                            mm = nc.tensor.matmul(ps[0:NT, 5 + n % 3, 0:HALF], k.nT[:, f, tile_cols(t)], w[:, h, f, :],
                                                  start=(f == 0), stop=(f == FC - 1))
                        mm.then_inc(s["v_done"], 1)
                pe.wait_ge(s["exp"], 3)
                nc.tensor.matmul(ps[0:NT, 3, 0:H], k.ones[0:NT, 0:NT], tot[:, 0, :], start=True, stop=True).then_inc(s["total"], 1)
                pe.wait_ge(s["vscaled"], TILES)
                for p in range(FC):
                    for t in range(TILES):
                        mm = nc.tensor.matmul(ps[:, p % 2, 0:P], k_node[:, t, P * p:P * p + P], v_node[:, t, P * p:P * p + P],
                                              start=(t == 0), stop=(t == TILES - 1))
                    mm.then_inc(s["kv"], 1)
                    if p < FC - 1:
                        if p >= 1:
                            pe.wait_ge(s["kv_out"], p)
                pe.wait_ge(s["kv_out"], FC)
                for t in range(TILES):
                    for h in range(2):
                        n = 2 * t + h
                        if n >= 4:
                            pe.wait_ge(s["att_out"], n - 3)
                        for p in range(3):
                            mm = nc.tensor.matmul(ps[0:NT, n % 4, P * p:P * p + P], qT[:, 3 * h + p, tile_cols(t)],
                                                  kvb[:, 3 * h + p, :], start=True, stop=True)
                        mm.then_inc(s["att"], 1)
                for c in range(FC):
                    for q in range(3):
                        n = 3 * c + q
                        pe.wait_ge(s["att_out"], 2 * TILES)
                        if n >= 4:
                            pe.wait_ge(s["att_copied"], n - 3)
                        for t in range(4 * q, min(4 * q + 4, TILES)):
                            mm = nc.tensor.transpose(ps[:, 4 + n % 4, NT * (t % 4):NT * (t % 4) + NT],
                                                     mix_node[:, t, P * c:P * c + P], k.ident[0:NT, 0:NT])
                        mm.then_inc(s["att_turned"], 1)

            @block.scalar
            def _(act):
                act.wait_ge(s["flow2"], 1)
                nc.scalar.activation(fl[:, 2, :, :], fl[:, 2, :, :], ACT.Sigmoid).then_inc(s["exp"], 1)
                nc.scalar.activation(fl[:, 3, :, :], fl[:, 3, :, :], ACT.Exp).then_inc(s["exp"], 1)
                for c in range(FC):
                    for q in range(3):
                        n = 3 * c + q
                        m = min(4, TILES - 4 * q)
                        act.wait_ge(s["att_turned"], n + 1)
                        nc.scalar.activation(k.attT[:, c, 4 * NT * q:4 * NT * q + m * NT], ps[:, 4 + n % 4, 0:m * NT],
                                             ACT.Copy).then_inc(s["att_copied"], 1)

            @block.vector
            def _(dve):
                ch = Chain(dve, s["order"])

                def masked(step, side, values):
                    return nc.vector.scalar_tensor_tensor(out=cl[:, step, side], in0=values, scalar=E6,
                                                          in1=head2[:].unsqueeze(1).broadcast_to([P, FC, 2]), op0=ALU.add, op1=ALU.mult)
                ch.then(nc.vector.tensor_reduce(vec[:], part[:], AX_X, ALU.add))
                ch.then(masked(0, 0, vec[:, FC:].unsqueeze(2).broadcast_to([P, FC, 2])))
                masked(0, 1, vec[:, 0:FC].unsqueeze(2).broadcast_to([P, FC, 2])).then_inc(s["columns"], 1)

                def dots_out(step, sem, dst0, dst1):
                    dve.wait_ge(sem, 1)
                    ch.then(nc.vector.tensor_scalar(epsr[:], ps[0:NT, 2, 0:2 * H].rearrange("p (s h) -> p s h", s=2), E6, None, ALU.add))
                    for side, dst in ((0, dst0), (1, dst1)):
                        ch.step(nc.vector.tensor_tensor(dst, ps[0:NT, side, 0:TILES * H].rearrange("p (t h) -> p t h", h=H),
                                                        epsr[:, side, :].unsqueeze(1).broadcast_to([NT, TILES, H]), ALU.add))
                    ch.wait()
                dots_out(0, s["dots1"], fl[:, 2], fl[:, 3])
                nc.vector.reciprocal(fl[:, 0], fl[:, 2]).then_inc(s["flow1"], 1)
                nc.vector.reciprocal(fl[:, 1], fl[:, 3]).then_inc(s["flow1"], 1)
                dve.wait_ge(s["sums"], 1)
                ch.then(masked(1, 0, ps[:, 3, 0:H].rearrange("p (c h) -> p c h", h=2)))
                masked(1, 1, ps[:, 4, 0:H].rearrange("p (c h) -> p c h", h=2)).then_inc(s["columns"], 1)
                dots_out(1, s["dots2"], fl[:, 2], fl[:, 4])
                nc.vector.tensor_scalar(fl[:, 3], fl[:, 4], -1.0, 1.0, ALU.max, ALU.min).then_inc(s["flow2"], 1)
                dve.wait_ge(s["exp"], 2)
                nc.vector.tensor_reduce(tot[:, 0, :], fl[:, 3].rearrange("p t h -> p h t"), AX_X, ALU.add).then_inc(s["exp"], 1)
                ch.step(nc.vector.tensor_tensor(fl[:, 2], fl[:, 2], fl[:, 0], ALU.mult))
                dve.wait_ge(b_in, 16)
                for n in range(2 * TILES):
                    h, t = n // TILES, n % TILES
                    dve.wait_ge(s["v_done"], n + 1)
                    nc.vector.tensor_tensor(v_node[:, t, HALF * h:HALF * h + HALF], ps[0:NT, 5 + n % 3, 0:HALF],
                                            bv[:, HALF * h:HALF * h + HALF], ALU.add).then_inc(s["v_out"], 1)
                dve.wait_ge(s["total"], 1)
                ch.then(nc.vector.reciprocal(tot[:, 1, :], ps[0:NT, 3, 0:H]))
                ch.then(nc.vector.tensor_scalar(tot[:, 1, :], tot[:, 1, :], float(T), None, ALU.mult))
                ch.then(nc.vector.tensor_tensor(fl[:, 4], fl[:, 3], tot[:, 1, :].unsqueeze(1).broadcast_to([NT, TILES, H]), ALU.mult))
                dve.wait_ge(s["v_out"], 2 * TILES)
                for t in range(TILES):
                    v3 = v_node[:, t, :].rearrange("p (h e) -> p h e", h=H)
                    nc.vector.tensor_tensor(v3, v3, fl[:, 4, t, :].unsqueeze(2).broadcast_to([NT, H, D // H]),
                                            ALU.mult).then_inc(s["vscaled"], 1)
                for p in range(FC):
                    dve.wait_ge(s["kv"], p + 1)
                    nc.vector.tensor_tensor(kvb[:, p, :], ps[:, p % 2, 0:P], k.heads2[:], ALU.mult).then_inc(s["kv_out"], 1)
                for n in range(2 * TILES):
                    t, h = n // 2, n % 2
                    dve.wait_ge(s["att"], n + 1)
                    nc.vector.tensor_tensor(mix_node[:, t, HALF * h:HALF * h + HALF].rearrange("p (h e) -> p h e", h=FC),
                                            ps[0:NT, n % 4, 0:HALF].rearrange("p (h e) -> p h e", h=FC),
                                            fl[:, 2, t, FC * h:FC * h + FC].unsqueeze(2).broadcast_to([NT, FC, D // H]),
                                            ALU.mult).then_inc(s["att_out"], 1)


def flow_project_stage(k, w_dram, bias_dram):
    nc, ps = k.nc, k.ps
    wl = [k.sem(f"fp_weights{h}") for h in range(2)]
    done, gated, out, b_in, b2 = k.sem("fp_done"), k.sem("fp_gated"), k.sem("fp_out"), k.sem("fp_bias_in"), k.sem("fp_bias2")
    with ExitStack() as ctx:
        w = k.sb("fp_w", [P, 2, FC, P], ctx=ctx)
        g_sb = k.sb("fp_gate", [P, 2, TP], ctx=ctx)
        bias = k.sb("fp_bias", [P, FC], ctx=ctx)
        with nc.Block(no_gpsimd_drain=True) as block:
            @block.sync
            def _(sp):
                sp.dma_start(bias[:], bias_dram).then_inc(b_in, 16)
                for o in range(FC):
                    if o >= 2:
                        sp.wait_ge(done, o - 1)
                    sp.dma_start(w[:, o % 2], w_dram[o]).then_inc(wl[o % 2], 16)

            @block.tensor
            def _(pe):
                for o in range(FC):
                    pe.wait_ge(wl[o % 2], 16 * (o // 2 + 1))
                    if o >= 2:
                        pe.wait_ge(gated, o - 1)
                    for f in range(FC):
                        for c in range(CH):
                            mm = nc.tensor.matmul(ps[:, 3 * (o % 2) + c, 0:CW], w[:, o % 2, f, :], k.attT[:, f, cols(c)],
                                                  start=(f == 0), stop=(f == FC - 1))
                    mm.then_inc(done, 1)

            @block.scalar
            def _(act):
                act.wait_ge(b2, 1)
                for o in range(FC):
                    act.wait_ge(done, o + 1)
                    if o >= 2:
                        act.wait_ge(out, o - 1)
                    g = 3 * (o % 2)
                    nc.scalar.activation(g_sb[:, o % 2, :].rearrange("p (c n) -> p c n", c=CH), ps[:, g:g + CH, 0:CW],
                                         ACT.Sigmoid, bias=bias[:, o:o + 1], scale=2.0).then_inc(gated, 1)

            @block.vector
            def _(dve):
                dve.wait_ge(b_in, 16)
                nc.vector.tensor_scalar(bias[:], bias[:], 2.0, None, ALU.mult).then_inc(b2, 1)
                for o in range(FC):
                    dve.wait_ge(gated, o + 1)
                    nc.vector.tensor_tensor(k.xT[:, o, :], k.xT[:, o, :], g_sb[:, o % 2, :], ALU.add).then_inc(out, 1)


def graph_layer(k, name, heads, F, w_dram, att_dram, b_dram, wide, h1_dram=None):
    nc, ps = k.nc, k.ps
    NF = F // P
    DEN = NF
    HB = 2 if wide else 1
    s = {n: k.sem(f"{name}_{n}") for n in (
        "h_done", "h_out", "al", "order", "as_diag", "as_row", "as_out", "far_read", "r_diag", "r_row", "r_out",
        "low", "exped", "p_made", "summed", "agg", "inverse", "scaled", "clipped", "elu_exp", "result")}
    w_in, at_in, b_in = k.sem(f"{name}_w_in"), k.sem(f"{name}_att_in"), k.sem(f"{name}_b_in")
    far_in = [k.sem(f"{name}_far_in{h}") for h in range(2)]
    st_out = [k.sem(f"{name}_stored{h}") for h in range(2)] if wide else None
    LR = 0.2
    with ExitStack() as ctx:
        if wide:
            h_sb = k.sb(f"{name}_h", [NT, HB, TILES, F], ctx=ctx)
            w = k.sb(f"{name}_w", [P, FC, F], ctx=ctx)
        else:
            h_sb = k.h2[:, :].rearrange("p (a t f) -> p a t f", a=1, t=TILES)
        a_rows = k.sb(f"{name}_a", [NT, 2, F], ctx=ctx)
        al = k.sb(f"{name}_al", [NT, 2, 3, TILES], ctx=ctx)
        mx = k.sb(f"{name}_mx", [NT, 5, TILES], ctx=ctx)
        rows = k.sb(f"{name}_rows", [P, 2, TP], ctx=ctx)
        far = k.sb(f"{name}_far", [NT, 2, T], BF16, ctx=ctx)
        tt = k.sb(f"{name}_scratch", [NT, 6 * CW], ctx=ctx)
        t1, t2 = (tt[:, a * CW:b * CW].rearrange("p (s n) -> p s n", n=CW) for a, b in ((0, 4), (4, 6)))
        dg = tt[:, 0:T].rearrange("p (t n) -> p t n", n=NT)
        scr = tt[:, T:T + F]
        mscr = tt[:, T:T + T // 2].bitcast(BF16)
        pr = k.sb(f"{name}_p", [NT, 2, TILES, CW], ctx=ctx)
        sm = k.sb(f"{name}_sm", [NT, 2, CW], ctx=ctx)
        rden = k.sb(f"{name}_rden", [P, CW], ctx=ctx)
        o1 = k.sb(f"{name}_o1", [P, 2, CW], ctx=ctx)
        o2 = k.sb(f"{name}_o2", [P, 2, CW], ctx=ctx)
        bias = k.sb(f"{name}_bias", [P, heads * NF], ctx=ctx)
        NR = TILES * heads
        with nc.Block(no_gpsimd_drain=True) as block:
            @block.sync
            def _(sp):
                def head_in(i):
                    if i >= 1:
                        sp.wait_ge(s["al"], 2 * TILES * i)
                    for j in range(2):
                        sp.dma_start(a_rows[:, j, :], att_dram[j, i].partition_broadcast(NT)).then_inc(at_in, 16)
                    if wide:
                        if i >= 1:
                            sp.wait_ge(s["h_done"], TILES * i)
                        sp.dma_start(w[:], w_dram[i]).then_inc(w_in, 16)

                sp.dma_start(bias[:], b_dram).then_inc(b_in, 16)
                head_in(0)
                for i in range(heads):
                    if i + 1 < heads:
                        head_in(i + 1)
                    for t in range(TILES):
                        n = i * TILES + t
                        if n >= 2:
                            sp.wait_ge(s["far_read"], n - 1)
                        sp.dma_start(far[:, n % 2, :], k.far_dram[t]).then_inc(far_in[n % 2], 16)
                    if wide:
                        for m in range(NF * CH * i, NF * CH * (i + 1)):
                            c, f = m // NF % CH, m % NF
                            sp.wait_ge(s["result"], m + 1)
                            sp.dma_start(h1_dram[NF * i + f, :, cols(c)], o2[:, m % 2, :]).then_inc(st_out[m % 2], 16)
                if wide:
                    for h in range(2):
                        sp.wait_ge(st_out[h], 16 * (NF * CH * heads // 2))

            @block.tensor
            def _(pe):
                def project(i, ts):
                    if ts[0] == 0:
                        pe.wait_ge(w_in, 16 * (i + 1))
                    for t in ts:
                        n = i * TILES + t
                        if n >= 2:
                            pe.wait_ge(s["h_out"], n - 1)
                        if i >= 1 and t == 0:
                            pe.wait_ge(s["as_out"], 2 * i)
                        if t == 5 and i >= 1:
                            pe.wait_ge(s["r_out"], 4 * i)
                        for f in range(FC):
                            mm = nc.tensor.matmul(ps[0:NT, 5 + t % 2, 0:F], k.nT[:, f, tile_cols(t)], w[:, f, :],
                                                  start=(f == 0), stop=(f == FC - 1))
                        mm.then_inc(s["h_done"], 1)

                def lay(n_diag, sem_in, wait, sem_out):
                    pe.wait_ge(sem_in, n_diag)
                    pe.wait_ge(*wait)
                    for t in range(TILES):
                        b = 5 + t // 4
                        mm = nc.tensor.matmul(ps[:, b, NT * (t % 4):NT * (t % 4) + NT], k.ones[0:NT, :], dg[:, t, :],
                                              start=True, stop=True)
                    mm.then_inc(sem_out, 1)

                def a_row(i):
                    lay(TILES * (i + 1), s["as_diag"], (s["h_out"], TILES * (i + 1)) if wide else (s["al"], 1), s["as_row"])

                def r_rows(i):
                    for j in range(2):
                        wait = (s["as_out"], 2 * (i + 1)) if j == 0 else (s["r_out"], 2 * (2 * i + 1))
                        if wide and j == 0 and i + 1 < heads:
                            pe.wait_ge(s["h_out"], TILES * (i + 1) + 5)
                        lay(TILES * (2 * i + j + 1), s["r_diag"], wait, s["r_row"])

                def aggregate(i):
                    for c in range(CH):
                        n = CH * i + c
                        for f in range(NF):
                            if f == 0:
                                pe.wait_ge(s["p_made"], TILES * (n + 1))
                            if n >= 1:
                                pe.wait_ge(s["scaled"], NF * (n - 1) + f + 1)
                            for t in range(TILES):
                                mm = nc.tensor.matmul(ps[:, f, 0:CW], h_sb[:, i % HB, t, P * f:P * f + P], pr[:, n % 2, t, :],
                                                      start=(t == 0), stop=(t == TILES - 1))
                            mm.then_inc(s["agg"], 1)
                            if f == 0:
                                pe.wait_ge(s["summed"], TILES * (n + 1))
                                if n >= 1:
                                    pe.wait_ge(s["inverse"], n)
                                nc.tensor.matmul(ps[:, DEN, 0:CW], k.ones[0:NT, :], sm[:, n % 2, :], start=True, stop=True)\
                                    .then_inc(s["agg"], 1)

                if wide:
                    project(0, range(TILES))
                a_row(0)
                for i in range(heads):
                    if wide and i + 1 < heads:
                        project(i + 1, range(0, 5))
                    r_rows(i)
                    if wide and i + 1 < heads:
                        project(i + 1, range(5, TILES))
                    aggregate(i)
                    if i + 1 < heads:
                        a_row(i + 1)

            @block.scalar
            def _(act):
                nexp = [0]

                def h_copy(i, t):
                    act.wait_ge(s["h_done"], i * TILES + t + 1)
                    if i >= 2 and t == 0:
                        act.wait_ge(s["agg"], CH * (NF + 1) * (i - 1))
                    nc.scalar.activation(h_sb[:, i % HB, t, :], ps[0:NT, 5 + t % 2, 0:F], ACT.Copy).then_inc(s["h_out"], 1)

                def row_copy(j, sem):
                    nc.scalar.activation(rows[:, j, 0:1000].rearrange("p (b n) -> p b n", b=2), ps[:, 5:7, 0:500], ACT.Copy).then_inc(sem, 1)
                    nc.scalar.activation(rows[:, j, 1000:T], ps[:, 7, 0:250], ACT.Copy).then_inc(sem, 1)

                def exps(m):
                    for _ in range(m):
                        n = nexp[0]
                        nexp[0] += 1
                        act.wait_ge(s["low"], n + 1)
                        nc.scalar.activation(t1[:, n % 4, :], t1[:, n % 4, :], ACT.Exp).then_inc(s["exped"], 1)

                def elus(n):
                    if wide:
                        for f in range(NF):
                            act.wait_ge(s["clipped"], 2 * (NF * n + f + 1))
                            nc.scalar.activation(o1[:, (NF * n + f) % 2, :], o1[:, (NF * n + f) % 2, :], ACT.Exp).then_inc(s["elu_exp"], 1)
                if wide:
                    for t in range(TILES):
                        h_copy(0, t)
                act.wait_ge(s["as_row"], 1)
                row_copy(0, s["as_out"])
                for i in range(heads):
                    more = wide and i + 1 < heads
                    if more:
                        for t in range(5):
                            h_copy(i + 1, t)
                    for j in range(2):
                        act.wait_ge(s["r_row"], 2 * i + j + 1)
                        row_copy(j, s["r_out"])
                    for t in range(5):
                        exps(2)
                        if more:
                            h_copy(i + 1, 5 + t)
                    exps(TILES)
                    elus(CH * i)
                    exps(TILES)
                    elus(CH * i + 1)
                    elus(CH * i + 2)
                    if i + 1 < heads:
                        act.wait_ge(s["as_row"], i + 2)
                        row_copy(0, s["as_out"])

            @block.gpsimd
            def _(pool):
                for n in range(CH * heads):
                    for t in range(TILES):
                        m = n * TILES + t
                        pool.wait_ge(s["p_made"], m + 1)
                        if t == 0:
                            if n >= 2:
                                pool.wait_ge(s["inverse"], n - 1)
                            nc.gpsimd.tensor_copy(sm[:, n % 2, :], pr[:, n % 2, 0, :]).then_inc(s["summed"], 1)
                        else:
                            pool.wait_ge(s["summed"], m)
                            nc.gpsimd.tensor_tensor(sm[:, n % 2, :], sm[:, n % 2, :], pr[:, n % 2, t, :], ALU.add)\
                                .then_inc(s["summed"], 1)

            @block.vector
            def _(dve):
                ch = Chain(dve, s["order"])
                ch.step(nc.vector.memset(rows[:, :, T:TP], 0.0))
                made = [0]

                def logits(i):
                    dve.wait_ge(at_in, 32 * (i + 1))
                    for t in range(TILES):
                        if wide:
                            dve.wait_ge(s["h_out"], i * TILES + t + 1)
                        for j in range(2):
                            nc.vector.tensor_tensor_reduce(scr[:], h_sb[:, i % HB, t, :], a_rows[:, j, :], 1.0, 0.0, ALU.mult, ALU.add,
                                                           al[:, i % 2, j, t:t + 1]).then_inc(s["al"], 1)
                            dve.wait_ge(s["al"], 2 * (i * TILES + t) + j + 1)
                    ch.then(nc.vector.tensor_scalar(al[:, i % 2, 2, :], al[:, i % 2, 0, :], LR, None, ALU.mult))

                def as_diag(i):
                    if i >= 1:
                        dve.wait_ge(s["r_row"], 2 * i)
                    for t in range(TILES):
                        nc.vector.tensor_scalar(dg[:, t, :], k.ident[0:NT, 0:NT], al[:, i % 2, 0, t:t + 1], None,
                                                ALU.mult).then_inc(s["as_diag"], 1)

                def maxima(i):
                    dve.wait_ge(s["as_out"], 2 * (i + 1))
                    for t in range(TILES):
                        n = i * TILES + t
                        dve.wait_ge(far_in[n % 2], 16 * (n // 2 + 1))
                        nc.vector.tensor_tensor_reduce(mscr[:], rows[0:NT, 0, 0:T], far[:, n % 2, :], 1.0, 3 * BIG, ALU.add, ALU.max,
                                                       mx[:, 0, t:t + 1]).then_inc(s["far_read"], 1)
                        dve.wait_ge(s["far_read"], n + 1)
                    ch.then(nc.vector.tensor_tensor(mx[:, 0, :], mx[:, 0, :], al[:, i % 2, 1, :], ALU.add))
                    ch.then(nc.vector.tensor_scalar(mx[:, 2, :], mx[:, 0, :], LR, None, ALU.mult))
                    ch.then(nc.vector.tensor_tensor(mx[:, 1, :], mx[:, 0, :], mx[:, 2, :], ALU.max))
                    ch.step(nc.vector.tensor_tensor(mx[:, 3, :], al[:, i % 2, 1, :], mx[:, 1, :], ALU.subtract))
                    ch.then(nc.vector.scalar_tensor_tensor(out=mx[:, 4, :], in0=al[:, i % 2, 1, :], scalar=LR, in1=mx[:, 1, :],
                                                           op0=ALU.mult, op1=ALU.subtract))
                    for j in range(2):
                        if j == 0:
                            dve.wait_ge(s["as_row"], i + 1)
                        else:
                            dve.wait_ge(s["r_row"], 2 * i + 1)
                        for t in range(TILES):
                            nc.vector.tensor_scalar(dg[:, t, :], k.ident[0:NT, 0:NT], mx[:, 3 + j, t:t + 1], None,
                                                    ALU.mult).then_inc(s["r_diag"], 1)

                def weights(i, c):
                    n = CH * i + c
                    if c == 0:
                        dve.wait_ge(s["r_out"], 4 * (i + 1))
                    if n >= 2:
                        dve.wait_ge(s["agg"], (NF + 1) * (n - 1))
                        dve.wait_ge(s["summed"], TILES * (n - 1))
                    for t in range(TILES + 2):
                        if t < TILES:
                            m = n * TILES + t
                            ch.step(nc.vector.tensor_scalar(t1[:, m % 4, :], rows[0:NT, 0, cols(c)], al[:, i % 2, 0, t:t + 1], 0.0,
                                                            ALU.add, ALU.min))
                            ch.then(nc.vector.tensor_scalar(t2[:, m % 2, :], rows[0:NT, 1, cols(c)], al[:, i % 2, 2, t:t + 1], 0.0,
                                                            ALU.add, ALU.min))
                            nc.vector.tensor_tensor(t1[:, m % 4, :], t1[:, m % 4, :], t2[:, m % 2, :], ALU.max).then_inc(s["low"], 1)
                        if t >= 2:
                            m = n * TILES + t - 2
                            dve.wait_ge(s["exped"], m + 1)
                            nc.vector.tensor_tensor(pr[:, n % 2, t - 2, :], t1[:, m % 4, :], k.counts[:, t - 2, cols(c)],
                                                    ALU.mult).then_inc(s["p_made"], 1)
                            dve.wait_ge(s["p_made"], m + 1)

                def results(i, c):
                    n = CH * i + c
                    for f in range(NF):
                        m = NF * n + f
                        base = (NF + 1) * n
                        if f == 0:
                            dve.wait_ge(s["agg"], base + 2)
                            ch.then(nc.vector.tensor_scalar(rden[:], ps[:, DEN, 0:CW], 1e-16, None, ALU.add))
                            nc.vector.reciprocal(rden[:], rden[:]).then_inc(s["inverse"], 1)
                            dve.wait_ge(s["inverse"], n + 1)
                        dve.wait_ge(s["agg"], base + (1 if f == 0 else f + 2))
                        if wide:
                            if m >= 2:
                                dve.wait_ge(st_out[m % 2], 16 * (m // 2))
                            nc.vector.tensor_tensor(o1[:, m % 2, :], ps[:, f, 0:CW], rden[:], ALU.mult).then_inc(s["scaled"], 1)
                            dve.wait_ge(s["scaled"], m + 1)
                            b = bias[:, NF * i + f:NF * i + f + 1]
                            nc.vector.tensor_scalar(o2[:, m % 2, :], o1[:, m % 2, :], b, 0.0, ALU.add, ALU.max).then_inc(s["clipped"], 1)
                            dve.wait_ge(s["clipped"], 2 * m + 1)
                            nc.vector.tensor_scalar(o1[:, m % 2, :], o1[:, m % 2, :], b, 0.0, ALU.add, ALU.min).then_inc(s["clipped"], 1)
                            dve.wait_ge(s["elu_exp"], m + 1)
                            nc.vector.scalar_tensor_tensor(out=o2[:, m % 2, :], in0=o2[:, m % 2, :], scalar=-1.0, in1=o1[:, m % 2, :],
                                                           op0=ALU.add, op1=ALU.add).then_inc(s["result"], 1)
                        else:
                            if m >= 2:
                                dve.wait_ge(s["result"], m - 1)
                            nc.vector.tensor_tensor(o1[:, m % 2, :], ps[:, f, 0:CW], rden[:], ALU.mult).then_inc(s["scaled"], 1)
                            dve.wait_ge(s["scaled"], m + 1)
                            nc.vector.scalar_tensor_tensor(out=k.xT[:, f, cols(c)], in0=o1[:, m % 2, :], scalar=bias[:, f:f + 1],
                                                           in1=k.xT[:, f, cols(c)], op0=ALU.add, op1=ALU.add).then_inc(s["result"], 1)
                logits(0)
                as_diag(0)
                maxima(0)
                dve.wait_ge(b_in, 16)
                for i in range(heads):
                    weights(i, 0)
                    if i + 1 < heads:
                        logits(i + 1)
                    weights(i, 1)
                    results(i, 0)
                    weights(i, 2)
                    results(i, 1)
                    results(i, 2)
                    if i + 1 < heads:
                        as_diag(i + 1)
                        maxima(i + 1)



def project_wide_stage(k, w_dram, h1_dram):
    nc, ps = k.nc, k.ps
    KC = 16
    w_in, done, out = k.sem("w2_in"), k.sem("h2_done"), k.sem("h2_out")
    h_in = [k.sem(f"h1_in{h}") for h in range(2)]
    with ExitStack() as ctx:
        w = k.sb("w2_w", [P, KC, D], ctx=ctx)
        h1 = k.sb("h1_tile", [P, 2, KC, NT], ctx=ctx)
        with nc.Block(no_gpsimd_drain=True) as block:
            @block.sync
            def _(sp):
                sp.dma_start(w[:], w_dram).then_inc(w_in, 16)
                for t in range(TILES):
                    if t >= 2:
                        sp.wait_ge(done, 2 * (t - 1))
                    sp.dma_start(h1[:, t % 2], h1_dram[:, :, tile_cols(t)].rearrange("c p n -> p c n")).then_inc(h_in[t % 2], 16)

            @block.tensor
            def _(pe):
                pe.wait_ge(w_in, 16)
                for t in range(TILES):
                    pe.wait_ge(h_in[t % 2], 16 * (t // 2 + 1))
                    for h in range(2):
                        n = 2 * t + h
                        if n >= 4:
                            pe.wait_ge(out, n - 3)
                        for c in range(KC):
                            mm = nc.tensor.matmul(ps[0:NT, n % 4, 0:HALF], h1[:, t % 2, c, :], w[:, c, HALF * h:HALF * h + HALF],
                                                  start=(c == 0), stop=(c == KC - 1))
                        mm.then_inc(done, 1)

            @block.scalar
            def _(act):
                for n in range(2 * TILES):
                    act.wait_ge(done, n + 1)
                    nc.scalar.activation(k.h2[:, D * (n // 2) + HALF * (n % 2):D * (n // 2) + HALF * (n % 2) + HALF],
                                         ps[0:NT, n % 4, 0:HALF], ACT.Copy).then_inc(out, 1)


def gated_experts_stage(k, w13_dram, w2_dram, comb_dram, E):
    nc, ps = k.nc, k.ps
    s = {n: k.sem("ge_" + n) for n in ("h_done", "sig", "u1", "u2", "h_out", "y_done", "y_out")}
    wl, w2l, cb = ([k.sem(f"ge_{n}{h}") for h in range(2)] for n in ("w13", "w2", "comb"))
    U = 2 * CH
    Y = FC * CH
    with ExitStack() as ctx:
        w13 = k.sb("ge_w13", [P, 2, 2, 2, FC, P], ctx=ctx)
        w2 = k.sb("ge_w2", [P, 2, 2, D], ctx=ctx)
        comb = k.sb("ge_comb", [P, 2, TP], ctx=ctx)
        hid = k.sb("ge_hid", [P, 2, 2, TP], ctx=ctx)
        sg = k.sb("ge_sig", [P, 2, CW], ctx=ctx)
        with nc.Block(no_gpsimd_drain=True) as block:
            @block.sync
            def _(sp):
                def load(i, j):
                    e = 2 * i + j
                    if not isinstance(i, int):
                        sp.wait_ge(s["h_out"], U * (e - 1))
                    sp.dma_start(w13[:, j], w13_dram[e]).then_inc(wl[j], 16)
                    sp.dma_start(comb[:, j, :], comb_dram[bass.ds(e, 1), :].broadcast_to([P, TP])).then_inc(cb[j], 16)
                    if not isinstance(i, int):
                        sp.wait_ge(s["y_done"], Y * (e - 1))
                    sp.dma_start(w2[:, j], w2_dram[e]).then_inc(w2l[j], 16)
                for j in range(2):
                    load(0, j)
                with sp.Fori(1, E // 2) as i:
                    for j in range(2):
                        load(i, j)

            @block.tensor
            def _(pe):
                def hidden(i, j):
                    e = 2 * i + j
                    pe.wait_ge(wl[j], 16 * i + 16)
                    for u in range(U):
                        q, c = u // CH, u % CH
                        n = U * e + u
                        if not (isinstance(i, int) and n < 2):
                            pe.wait_ge(s["h_out"], n - 1)
                        for g in range(2):
                            for f in range(FC):
                                mm = nc.tensor.matmul(ps[:, 2 * (u % 2) + g, 0:CW], w13[:, j, q, g, f, :], k.nT[:, f, cols(c)],
                                                      start=(f == 0), stop=(f == FC - 1))
                        mm.then_inc(s["h_done"], 1)

                def outputs(i, j):
                    e = 2 * i + j
                    pe.wait_ge(w2l[j], 16 * i + 16)
                    pe.wait_ge(s["h_out"], U * (e + 1))
                    for y in range(Y):
                        o, c = y // CH, y % CH
                        n = Y * e + y
                        if not (isinstance(i, int) and n < 4):
                            pe.wait_ge(s["y_out"], n - 3)
                        for q in range(2):
                            mm = nc.tensor.matmul(ps[:, 4 + (Y * j + y) % 4, 0:CW], w2[:, j, q, P * o:P * o + P],
                                                  hid[:, j, q, cols(c)], start=(q == 0), stop=(q == 1))
                        mm.then_inc(s["y_done"], 1)
                hidden(0, 0)
                hidden(0, 1)
                outputs(0, 0)
                hidden(1, 0)
                outputs(0, 1)
                with pe.Fori(1, E // 2 - 1) as i:
                    hidden(i, 1)
                    outputs(i, 0)
                    hidden(i + 1, 0)
                    outputs(i, 1)
                hidden(E // 2 - 1, 1)
                outputs(E // 2 - 1, 0)
                outputs(E // 2 - 1, 1)

            @block.scalar
            def _(act):
                def unit(n, u, guard):
                    act.wait_ge(s["h_done"], n + 1)
                    if guard:
                        act.wait_ge(s["h_out"], n - 1)
                    nc.scalar.activation(sg[:, u % 2, :], ps[:, 2 * (u % 2), 0:CW], ACT.Sigmoid).then_inc(s["sig"], 1)
                for u in range(U):
                    unit(u, u, u >= 2)
                with act.Fori(1, E) as e:
                    for u in range(U):
                        unit(U * e + u, u, True)

            @block.vector
            def _(dve):
                def hidden(i, j):
                    e = 2 * i + j
                    dve.wait_ge(cb[j], 16 * i + 16)
                    if not isinstance(i, int):
                        dve.wait_ge(s["y_done"], Y * (e - 1))
                    for u in range(U):
                        q, c = u // CH, u % CH
                        n = U * e + u
                        h = hid[:, j, q, cols(c)]
                        dve.wait_ge(s["sig"], n + 1)
                        nc.vector.tensor_tensor(h, ps[:, 2 * (u % 2), 0:CW], sg[:, u % 2, :], ALU.mult).then_inc(s["u1"], 1)
                        dve.wait_ge(s["u1"], n + 1)
                        nc.vector.tensor_tensor(h, ps[:, 2 * (u % 2) + 1, 0:CW], h, ALU.mult).then_inc(s["u2"], 1)
                        dve.wait_ge(s["u2"], n + 1)
                        nc.vector.tensor_tensor(h, h, comb[:, j, cols(c)], ALU.mult).then_inc(s["h_out"], 1)

                def outputs(i, j):
                    for y in range(Y):
                        o, c = y // CH, y % CH
                        n = Y * (2 * i + j) + y
                        dve.wait_ge(s["y_done"], n + 1)
                        if not (isinstance(i, int) and n < Y):
                            dve.wait_ge(s["y_out"], n - Y + 1)
                        nc.vector.tensor_tensor(k.xT[:, o, cols(c)], ps[:, 4 + (Y * j + y) % 4, 0:CW], k.xT[:, o, cols(c)],
                                                ALU.add).then_inc(s["y_out"], 1)
                hidden(0, 0)
                hidden(0, 1)
                outputs(0, 0)
                hidden(1, 0)
                outputs(0, 1)
                with dve.Fori(1, E // 2 - 1) as i:
                    hidden(i, 1)
                    outputs(i, 0)
                    hidden(i + 1, 0)
                    outputs(i, 1)
                hidden(E // 2 - 1, 1)
                outputs(E // 2 - 1, 0)
                outputs(E // 2 - 1, 1)




def store_stage(k, src, out_dram):
    stored = k.sem("y_stored")
    with k.nc.Block(no_gpsimd_drain=True) as block:
        @block.sync
        def _(sp):
            sp.dma_start(out_dram, src[:, :, 0:T]).then_inc(stored, 16)
            sp.wait_ge(stored, 16)


STOP = 99


def program(nc, a, out):
    with ExitStack() as ctx:
        k = Kit(nc, ctx)
        k.ps = ctx.enter_context(nc.psum_tensor("ps", [P, 8, 512], F32))
        k.sem_ctx = layer0 = ctx.enter_context(ExitStack())
        ones_stage(k)
        nbuf = k.sb("normed", [P, TILES * D])
        k.nT = nbuf[:, 0:FC * TP].rearrange("p (c n) -> p c n", c=FC)
        k.h2 = nbuf[0:NT, :]
        k.dinv = k.sb("dinv", [NT, TILES])
        k.far_dram = nc.dram_tensor("far", (TILES, NT, T), BF16, kind="Internal").ap()
        k.counts_dram = nc.dram_tensor("counts_keep", (NT, TILES, TP), F32, kind="Internal").ap()
        x_park = nc.dram_tensor("x_park", (P, FC, TP), F32, kind="Internal").ap()
        comb0 = nc.dram_tensor("comb0", (8, TP), F32, kind="Internal").ap()
        comb1 = nc.dram_tensor("comb1", (18, TP), F32, kind="Internal").ap()
        h1_dram = nc.dram_tensor("h1", (16, P, TP), F32, kind="Internal").ap()
        out_f = out.rearrange("(c p) n -> p c n", p=P)

        def stop(n, src):
            if STOP == n:
                store_stage(k, src, out_f)
            return STOP == n

        with ExitStack() as first:
            k.x_node = k.sb("x_node", [NT, TILES, D], ctx=first)
            k.attT = k.sb("attT", [P, FC, TP], ctx=first)
            norm_nodes_stage(k, a["x"])
            if stop(1, k.nT):
                return
            linear_attention_stage(k, a["L0_kv"], a["L0_q"])
            if stop(2, k.attT):
                return
            k.counts = k.sb("counts", [NT, TILES, TP], ctx=first)
            counts_stage(k, a["src"], a["dst"])
            move_stage(k, "counts_kept", k.counts_dram[:, :, :], k.counts[:])
            aggregate_stage(k)
            if stop(3, k.nT):
                return
            k.xT = k.sb("x_first", [P, FC, TP], ctx=first)
            mix_project_stage(k, a["L0_out"], a["L0_bias"], a["xT"])
            move_stage(k, "x1_parked", x_park, k.xT[:])
        with ExitStack() as mid:
            k.xT = k.sb("x_mid", [P, FC, TP], ctx=mid)
            move_stage(k, "x1_back", k.xT[:], x_park)
            if stop(4, k.xT):
                return
            norm_stage(k, "ln1")
            if stop(5, k.nT):
                return
            router_stage(k, "r0", 8, a["L0_router_w"], a["L0_router_b"], True, comb0)
            experts_stage(k, a["L0_experts"], a["L0_expert_b"], comb0, 8)
            if stop(6, k.xT):
                return
            k.clear_sems()
            layer0.close()
            k.sem_ctx = layer1 = ctx.enter_context(ExitStack())
            norm_stage(k, "ln2")
            if stop(7, k.nT):
                return
            with ExitStack() as att:
                k.attT = k.sb("attT1", [P, FC, TP], ctx=att)
                flow_attention_stage(k, a["L1_qk"], a["L1_b_qk"], a["L1_v"], a["L1_b_v"])
                if stop(8, k.attT):
                    return
                flow_project_stage(k, a["L1_proj"], a["L1_b_proj"])
            if stop(9, k.xT):
                return
            move_stage(k, "x2_parked", x_park, k.xT[:])
        with ExitStack() as graph:
            k.counts = k.sb("counts1", [NT, TILES, TP], ctx=graph)
            move_stage(k, "counts_back", k.counts[:], k.counts_dram[:, :, :])
            graph_layer(k, "g1", 4, 512, a["L1_W1"], a["L1_att1"], a["L1_b1"], True, h1_dram)
            if STOP == 10:
                with ExitStack() as dbg:
                    d = k.sb("dbg", [P, FC, TP], ctx=dbg)
                    move_stage(k, "dbg_in", d[:], h1_dram[0:FC].rearrange("c p n -> p c n"))
                    store_stage(k, d, out_f)
                return
            k.clear_sems()
            layer1.close()
            k.sem_ctx = ctx.enter_context(ExitStack())
            project_wide_stage(k, a["L1_W2"], h1_dram)
            k.xT = k.sb("x_graph", [P, FC, TP], ctx=graph)
            move_stage(k, "x2_back", k.xT[:], x_park)
            graph_layer(k, "g2", 1, D, None, a["L1_att2"], a["L1_b2"], False)
            move_stage(k, "x3_parked", x_park, k.xT[:])
        k.xT = k.sb("x_last", [P, FC, TP])
        move_stage(k, "x3_back", k.xT[:], x_park)
        if stop(11, k.xT):
            return
        norm_stage(k, "ln3")
        router_stage(k, "r1", 16, a["L1_gate_w"], None, False, comb1, shared=2)
        gated_experts_stage(k, a["L1_w13"], a["L1_w2"], comb1, 18)
        store_stage(k, k.xT, out_f)


def move_stage(k, name, dst, src):
    moved = k.sem(name)
    with k.nc.Block(no_gpsimd_drain=True) as block:
        @block.sync
        def _(sp):
            sp.dma_start(dst, src).then_inc(moved, 16)
            sp.wait_ge(moved, 16)


def kernel(**inputs):
    import numpy as np
    import concourse.bacc as _bacc
    from concourse.bass_utils import run_bass_kernel_spmd as _run

    nc = _bacc.Bacc("TRN2", target_bir_lowering=False, num_devices=1)
    v = {n: np.asarray(x) for n, x in inputs.items()}

    def chunks(w):
        ni, no = w.shape[0] // P, w.shape[1] // P
        return w.reshape(ni, P, no, P).transpose(2, 1, 0, 3)

    def blocks(w, width):
        ni, nb = w.shape[0] // P, w.shape[1] // width
        return w.reshape(ni, P, nb, width).transpose(2, 1, 0, 3)

    def column(b):
        return b.reshape(-1, P).T

    def pairs(w1, w3):
        e = w1.shape[0]
        return np.stack([w1, w3], 1).reshape(e, 2, 2, P, FC, P).transpose(0, 5, 2, 1, 4, 3)

    def halves(w):
        return w.reshape(2, 256, D)

    w13 = np.concatenate([pairs(v["L1_ffn_w1"], v["L1_ffn_w3"]), pairs(halves(v["L1_ffn_sw1"]), halves(v["L1_ffn_sw3"]))])
    w2 = np.concatenate([v["L1_ffn_w2"].transpose(0, 2, 1), halves(v["L1_ffn_sw2"].T)])
    w2 = w2.reshape(18, 2, P, D).transpose(0, 2, 1, 3)
    host = {
        "x": v["x"], "xT": v["x"].T.reshape(FC, P, T).transpose(1, 0, 2),
        "src": v["src"].reshape(EC, NT).T, "dst": v["dst"].reshape(EC, NT).T,
        "L0_kv": blocks(v["L0_mix_w_qkv"][:, D:], HALF), "L0_q": chunks(v["L0_mix_w_qkv"][:, :D]),
        "L0_out": chunks(np.concatenate([v["L0_gnn_W"], v["L0_mix_w_proj"]], 0)),
        "L0_bias": np.stack([column(v["L0_gnn_b"]), column(v["L0_mix_b_proj"])]),
        "L0_router_w": v["L0_ffn_router_w"].T.reshape(FC, P, 8).transpose(1, 0, 2),
        "L0_router_b": v["L0_ffn_router_b"],
        "L0_experts": np.stack([chunks(w.T) for w in v["L0_ffn_expert_w"]]),
        "L0_expert_b": v["L0_ffn_expert_b"],
        "L1_qk": chunks(v["L1_mix_W_qkv"][:, :2 * D]), "L1_v": blocks(v["L1_mix_W_qkv"][:, 2 * D:], HALF),
        "L1_b_qk": column(v["L1_mix_b_qkv"][:2 * D]), "L1_b_v": v["L1_mix_b_qkv"][2 * D:],
        "L1_proj": chunks(v["L1_mix_W_proj"]), "L1_b_proj": column(v["L1_mix_b_proj"]),
        "L1_W1": blocks(v["L1_gnn_W1"], 512), "L1_att1": np.stack([v["L1_gnn_att_src1"], v["L1_gnn_att_dst1"]]),
        "L1_b1": column(v["L1_gnn_b1"]), "L1_W2": v["L1_gnn_W2"].reshape(16, P, D).transpose(1, 0, 2),
        "L1_att2": np.stack([v["L1_gnn_att_src2"], v["L1_gnn_att_dst2"]]), "L1_b2": column(v["L1_gnn_b2"]),
        "L1_gate_w": v["L1_ffn_gate_w"].T.reshape(FC, P, 16).transpose(1, 0, 2),
        "L1_w13": w13, "L1_w2": w2,
    }
    host = {n: np.ascontiguousarray(x) for n, x in host.items()}
    a = {n: nc.dram_tensor("in_" + n, x.shape, mybir.dt.from_np(x.dtype), kind="ExternalInput").ap() for n, x in host.items()}
    out = nc.dram_tensor("out_y", (D, T), F32, kind="ExternalOutput").ap()
    program(nc, a, out)
    r = _run(nc, [{"in_" + n: x for n, x in host.items()}], core_ids=[0])
    return np.ascontiguousarray(r.results[0]["out_y"].T)
```

```python
import concourse.bass as bass
from concourse import mybir
from contextlib import ExitStack

F32 = mybir.dt.float32
F16 = mybir.dt.float16
F32R = mybir.dt.float32r
BF16 = mybir.dt.bfloat16
I32 = mybir.dt.int32
U32 = mybir.dt.uint32
ACT = mybir.ActivationFunctionType
ALU = mybir.AluOpType
AX_X = mybir.AxisListType.X

P = 128
T = 1250
NT = 125
TILES = T // NT
CW = 418
CH = 3
TP = CW * CH
D = 768
FC = D // P
HALF = D // 2
EC = 160
EPS = 1e-5
NB0 = (2 * T // P + 8 + 1) // 2 * 2
NB1 = (2 * T // P + 16 + 1) // 2 * 2
BIG = -1.0e30


class Chain:

    def __init__(self, eng, sem, start=0):
        self.eng, self.sem, self.n = eng, sem, start

    def step(self, ins):
        self.n = self.n + 1
        return ins.then_inc(self.sem, 1)

    def wait(self):
        self.eng.wait_ge(self.sem, self.n)

    def then(self, ins):
        self.step(ins)
        self.wait()


class Kit:

    def __init__(self, nc, ctx):
        self.nc, self.ctx, self.sems, self.sem_ctx = nc, ctx, [], ctx

    def sb(self, name, shape, dt=F32, ctx=None):
        return (ctx or self.ctx).enter_context(self.nc.sbuf_tensor(name, shape, dt))

    def sem(self, name):
        handle = self.sem_ctx.enter_context(self.nc.semaphore(name))
        self.sems.append(handle)
        return handle

    def soft_sem(self, name):
        return self.ctx.enter_context(self.nc.semaphore(name))

    def clear_sems(self):
        with self.nc.Block(no_gpsimd_drain=True) as block:
            @block.gpsimd
            def _(pool):
                for handle in self.sems:
                    pool.sem_clear(handle)
        self.sems = []


def cols(c):
    return slice(c * CW, (c + 1) * CW)


def tile_cols(t):
    return slice(t * NT, (t + 1) * NT)


def ones_stage(k):
    nc = k.nc
    k.ident = k.sb("ident", [P, P])
    k.ones = k.sb("ones", [P, P])
    k.avg = k.sb("avg", [P, P])
    k.heads2 = k.sb("heads2", [P, P])
    k.index16 = k.sb("index16", [P, 16])
    made, zeroed = k.sem("const_made"), k.sem("const_zeroed")
    with nc.Block(no_gpsimd_drain=True) as block:
        @block.gpsimd
        def _(pool):
            nc.gpsimd.memset(k.ident[:], 0.0).then_inc(zeroed, 1)
            pool.wait_ge(zeroed, 1)
            nc.gpsimd.affine_select(out=k.ident[:], in_=k.ident[:], compare_op=ALU.not_equal, fill=1.0, base=0,
                                    pattern=[[-1, P]], channel_multiplier=1).then_inc(zeroed, 1)
            pool.wait_ge(zeroed, 2)
            nc.gpsimd.iota(k.index16[:], [[1, 16]], base=0, channel_multiplier=0,
                           allow_small_or_imprecise_dtypes=True).then_inc(zeroed, 1)

        @block.vector
        def _(dve):
            nc.vector.memset(k.heads2[:], 0.0).then_inc(made, 1)
            nc.vector.memset(k.ones[:], 1.0).then_inc(made, 1)
            nc.vector.memset(k.avg[:], 1.0 / D).then_inc(made, 1)
            dve.wait_ge(made, 1)
            nc.vector.memset(k.heads2[0:64, 0:64], 1.0).then_inc(made, 1)
            nc.vector.memset(k.heads2[64:128, 64:128], 1.0).then_inc(made, 1)


def norm_nodes_stage(k, x_dram):
    nc, ps = k.nc, k.ps
    loaded = [k.sem(f"x_loaded{g}") for g in range(2)]
    order, stats, rooted, normed = k.sem("ln0_order"), k.sem("ln0_var"), k.sem("ln0_std"), k.sem("ln0_normed")
    turned, copied = k.sem("ln0_turned"), k.sem("ln0_copied")
    with ExitStack() as ctx:
        six = k.sb("ln0_six", [NT, TILES, 12], ctx=ctx)
        mv = k.sb("ln0_mv", [NT, TILES, 2], ctx=ctx)
        rstd = k.sb("ln0_rstd", [NT, TILES], ctx=ctx)
        with nc.Block(no_gpsimd_drain=True) as block:
            @block.sync
            def _(sp):
                for g in range(2):
                    sp.dma_start(k.x_node[:, 5 * g:5 * g + 5, :],
                                 x_dram[625 * g:625 * g + 625, :].rearrange("(t p) d -> p t d", p=NT)).then_inc(loaded[g], 16)

            @block.vector
            def _(dve):
                ch = Chain(dve, order)
                ch.step(nc.vector.memset(k.nT[:, :, T:TP], 0.0))
                for t in range(TILES):
                    dve.wait_ge(loaded[t // 5], 16)
                    for h in range(2):
                        ch.step(nc.vector.bn_stats(six[:, t, 6 * h:6 * h + 6], k.x_node[:, t, h * HALF:(h + 1) * HALF]))
                ch.wait()
                for t in range(TILES):
                    ch.step(nc.vector.bn_aggr(mv[:, t, :], six[:, t, :]))
                ch.wait()
                nc.vector.tensor_scalar(rstd[:], mv[:, :, 1], EPS, None, ALU.add).then_inc(stats, 1)
                dve.wait_ge(rooted, 1)
                ch.then(nc.vector.reciprocal(rstd[:], rstd[:]))
                for t in range(TILES):
                    nc.vector.tensor_scalar(k.x_node[:, t, :], k.x_node[:, t, :], mv[:, t, 0:1], rstd[:, t:t + 1],
                                            ALU.subtract, ALU.mult).then_inc(normed, 1)

            @block.tensor
            def _(pe):
                for c in range(FC):
                    if c >= 2:
                        pe.wait_ge(copied, c - 1)
                    for t in range(TILES):
                        if c == 0:
                            pe.wait_ge(normed, t + 1)
                        mm = nc.tensor.transpose(ps[:, 3 * (c % 2) + t // 4, NT * (t % 4):NT * (t % 4) + NT],
                                                 k.x_node[:, t, P * c:P * c + P], k.ident[0:NT, 0:NT])
                    mm.then_inc(turned, 1)

            @block.scalar
            def _(act):
                act.wait_ge(stats, 1)
                nc.scalar.activation(rstd[:], rstd[:], ACT.Sqrt).then_inc(rooted, 1)
                for c in range(FC):
                    g = 3 * (c % 2)
                    act.wait_ge(turned, c + 1)
                    nc.scalar.activation(k.nT[:, c, 0:8 * NT].rearrange("p (b n) -> p b n", b=2), ps[:, g:g + 2, 0:4 * NT], ACT.Copy)
                    nc.scalar.activation(k.nT[:, c, 8 * NT:T], ps[:, g + 2, 0:2 * NT], ACT.Copy).then_inc(copied, 1)


def linear_attention_stage(k, w_kv, w_q):
    nc, ps = k.nc, k.ps
    wl = [k.sem(f"la_weights{h}") for h in range(2)]
    kv_done, kv_low, kv_exp, kv_out = k.sem("la_kv_done"), k.sem("la_kv_low"), k.sem("la_kv_exp"), k.sem("la_kv_out")
    with ExitStack() as ctx:
        kv = k.sb("la_kv", [NT, TILES, 2 * D], ctx=ctx)
        kvb = k.sb("la_kvb", [P, FC, 2 * P], ctx=ctx)
        wk = k.sb("la_w", [P, 2, FC, HALF], ctx=ctx)
        low = k.sb("la_low", [NT, 2, HALF], ctx=ctx)
        with nc.Block(no_gpsimd_drain=True) as block:
            @block.sync
            def _(sp):
                for j in range(4):
                    if j >= 2:
                        sp.wait_ge(kv_done, TILES * (j - 1))
                    sp.dma_start(wk[:, j % 2, :, :], w_kv[j]).then_inc(wl[j % 2], 16)

            @block.tensor
            def _(pe):
                for j in range(4):
                    pe.wait_ge(wl[j % 2], 16 * (j // 2 + 1))
                    for t in range(TILES):
                        n = j * TILES + t
                        if n >= 8:
                            pe.wait_ge(kv_out, n - 7)
                        for c in range(FC):
                            mm = nc.tensor.matmul(ps[0:NT, n % 8, 0:HALF], k.nT[:, c, tile_cols(t)], wk[:, j % 2, c, :],
                                                  start=(c == 0), stop=(c == FC - 1))
                        mm.then_inc(kv_done, 1)

            @block.vector
            def _(dve):
                for n in range(2 * TILES):
                    j, t = n // TILES, n % TILES
                    dve.wait_ge(kv_done, n + 1)
                    if n >= 2:
                        dve.wait_ge(kv_out, n - 1)
                    nc.vector.tensor_scalar(low[:, n % 2, :], ps[0:NT, n % 8, 0:HALF], 0.0, None, ALU.min).then_inc(kv_low, 1)
                    dve.wait_ge(kv_exp, n + 1)
                    nc.vector.scalar_tensor_tensor(out=kv[:, t, HALF * j:HALF * j + HALF], in0=ps[0:NT, n % 8, 0:HALF], scalar=0.0,
                                                   in1=low[:, n % 2, :], op0=ALU.max, op1=ALU.add).then_inc(kv_out, 1)
                for n in range(2 * TILES, 4 * TILES):
                    j, t = n // TILES, n % TILES
                    dve.wait_ge(kv_done, n + 1)
                    nc.vector.tensor_copy(kv[:, t, HALF * j:HALF * j + HALF], ps[0:NT, n % 8, 0:HALF]).then_inc(kv_out, 1)

            @block.scalar
            def _(act):
                for n in range(2 * TILES):
                    act.wait_ge(kv_low, n + 1)
                    nc.scalar.activation(low[:, n % 2, :], low[:, n % 2, :], ACT.Exp).then_inc(kv_exp, 1)

        state, masked = k.sem("la_state"), k.sem("la_masked")
        with nc.Block(no_gpsimd_drain=True) as block:
            @block.tensor
            def _(pe):
                for p in range(FC):
                    for t in range(TILES):
                        nc.tensor.matmul(ps[:, p, 0:P], kv[:, t, P * p:P * p + P], kv[:, t, D + P * p:D + P * p + P],
                                         start=(t == 0), stop=(t == TILES - 1))
                    for t in range(TILES):
                        mm = nc.tensor.matmul(ps[:, p, P:2 * P], kv[:, t, P * p:P * p + P], k.ones[0:NT, :],
                                              start=(t == 0), stop=(t == TILES - 1))
                    mm.then_inc(state, 1)

            @block.vector
            def _(dve):
                for p in range(FC):
                    dve.wait_ge(state, p + 1)
                    for h in range(2):
                        nc.vector.tensor_tensor(kvb[:, p, h * P:h * P + P], ps[:, p, h * P:h * P + P], k.heads2[:],
                                                ALU.mult).then_inc(masked, 1)

        wq = wk[:, :, 0:2, :].rearrange("p s a (b n) -> p s (a b) n", b=3)
        q_in = [k.sem(f"la_qweights{h}") for h in range(2)]
        q_done, q_low, q_exp, q_out = k.sem("la_q_done"), k.sem("la_q_low"), k.sem("la_q_exp"), k.sem("la_q_out")
        nd_done, inverted, nd_out = k.sem("la_numden"), k.sem("la_inverted"), k.sem("la_out")
        q = kv[:, 0:2, 0:TP]
        with ExitStack() as ctx2:
            q = k.sb("la_q", [P, 2, TP], ctx=ctx2)
            qlow = k.sb("la_qlow", [P, TP], ctx=ctx2)
            rec = k.sb("la_rec", [P, 2, CW], ctx=ctx2)
            with nc.Block(no_gpsimd_drain=True) as block:
                @block.sync
                def _(sp):
                    for p in range(FC):
                        if p >= 2:
                            sp.wait_ge(q_done, p - 1)
                        sp.dma_start(wq[:, p % 2], w_q[p]).then_inc(q_in[p % 2], 16)

                @block.tensor
                def _(pe):
                    for p in range(FC + 1):
                        if p < FC:
                            pe.wait_ge(q_in[p % 2], 16 * (p // 2 + 1))
                            if p >= 1:
                                pe.wait_ge(q_out, p)
                            for c in range(CH):
                                for f in range(FC):
                                    mm = nc.tensor.matmul(ps[:, c, 0:CW], wq[:, p % 2, f, :], k.nT[:, f, cols(c)],
                                                          start=(f == 0), stop=(f == FC - 1))
                            mm.then_inc(q_done, 1)
                        if p >= 1:
                            pe.wait_ge(q_out, p)
                            for c in range(CH):
                                n = (p - 1) * CH + c
                                if n >= 2:
                                    pe.wait_ge(nd_out, n - 1)
                                for h in range(2):
                                    mm = nc.tensor.matmul(ps[:, 3 + 2 * h + n % 2, 0:CW], kvb[:, p - 1, h * P:h * P + P],
                                                          q[:, (p - 1) % 2, cols(c)], start=True, stop=True)
                                mm.then_inc(nd_done, 1)

                @block.vector
                def _(dve):
                    for p in range(FC + 1):
                        if p < FC:
                            dve.wait_ge(q_done, p + 1)
                            if p >= 1:
                                dve.wait_ge(q_out, p)
                            nc.vector.tensor_scalar(qlow[:].rearrange("p (c n) -> p c n", c=CH), ps[:, 0:CH, 0:CW], 0.0, None,
                                                    ALU.min).then_inc(q_low, 1)
                            dve.wait_ge(q_exp, p + 1)
                            if p >= 2:
                                dve.wait_ge(nd_done, CH * (p - 1))
                            nc.vector.scalar_tensor_tensor(out=q[:, p % 2, :].rearrange("p (c n) -> p c n", c=CH),
                                                           in0=ps[:, 0:CH, 0:CW], scalar=0.0,
                                                           in1=qlow[:].rearrange("p (c n) -> p c n", c=CH),
                                                           op0=ALU.max, op1=ALU.add).then_inc(q_out, 1)
                        if p >= 1:
                            for c in range(CH):
                                n = (p - 1) * CH + c
                                dve.wait_ge(nd_done, n + 1)
                                if n >= 2:
                                    dve.wait_ge(nd_out, n - 1)
                                nc.vector.reciprocal(rec[:, n % 2, :], ps[:, 5 + n % 2, 0:CW]).then_inc(inverted, 1)
                                dve.wait_ge(inverted, n + 1)
                                nc.vector.tensor_tensor(k.attT[:, p - 1, cols(c)], ps[:, 3 + n % 2, 0:CW], rec[:, n % 2, :],
                                                        ALU.mult).then_inc(nd_out, 1)

                @block.scalar
                def _(act):
                    for p in range(FC):
                        act.wait_ge(q_low, p + 1)
                        nc.scalar.activation(qlow[:], qlow[:], ACT.Exp).then_inc(q_exp, 1)


def counts_stage(k, src_dram, dst_dram, dst_groups_dram):
    nc, ps = k.nc, k.ps
    U = 4
    NG = EC // U
    PASSES = TILES // 2
    SPAN = 2 * NT
    e_in, e_f, row, g_in = k.sem("edges_in"), k.sem("edges_float"), k.sem("index_row"), k.sem("groups_in")
    order, ext, laid, bounds = k.sem("range_order"), k.sem("range_extrema"), k.sem("range_row"), k.sem("range_found")
    hot, free = [k.sem(f"onehot_made{g}") for g in range(PASSES)], [k.sem(f"onehot_free{g}") for g in range(PASSES)]
    fin, staged, diag, summed = k.sem("counts_done"), k.sem("counts_staged"), k.sem("counts_diag"), k.sem("counts_summed")
    turned, placed, far_out = k.sem("counts_turned"), k.sem("counts_placed"), [k.sem(f"far_stored{h}") for h in range(2)]
    with ExitStack() as ctx:
        ei = k.sb("edge_int", [NT, 2, EC], I32, ctx=ctx)
        ef = k.sb("edge_float", [NT, 2, EC], F32, ctx=ctx)
        gi = k.sb("group_int", [NG, U * NT], I32, ctx=ctx)
        ge = k.sb("group_extrema", [NG, 2], F32, ctx=ctx)
        gf = k.sb("group_float", [NG, U * NT], F32, ctx=ctx)
        gx = k.sb("group_index", [1, NG], F32, ctx=ctx)
        rg = k.sb("group_rows", [1, 4, NG], F32, ctx=ctx)
        ac = k.sb("group_active", [1, 3, PASSES, NG], F32, ctx=ctx)
        lim = k.sb("pass_limits", [1, 2, PASSES], F32, ctx=ctx)
        limi = k.sb("pass_limits_int", [1, 2, PASSES], I32, ctx=ctx)
        idx = k.sb("index_row", [NT, TP], F16, ctx=ctx)
        zero = k.sb("zero_weights", [NT, NT], F16, ctx=ctx)
        hs = k.sb("hot_src", [NT, U, TP], F16, ctx=ctx)
        hd = k.sb("hot_dst", [NT, U, SPAN], F16, ctx=ctx)
        st = k.sb("counts_rows", [NT, 2, TP], F32, ctx=ctx)
        far = k.sb("far_rows", [NT, TP], BF16, ctx=ctx)
        with nc.Block(no_gpsimd_drain=True) as block:
            @block.sync
            def _(sp):
                sp.dma_start(gi[:], dst_groups_dram).then_inc(g_in, 16)
                sp.dma_start(ei[:, 0, :], src_dram).then_inc(e_in, 16)
                sp.dma_start(ei[:, 1, :], dst_dram).then_inc(e_in, 16)
                for t in range(TILES):
                    sp.wait_ge(summed, 2 * t + 2)
                    sp.dma_start(k.far_dram[t], far[:, 0:T]).then_inc(far_out[t % 2], 16)
                for h in range(2):
                    sp.wait_ge(far_out[h], 16 * (TILES // 2))

            @block.gpsimd
            def _(pool):
                nc.gpsimd.memset(zero[:], 0.0).then_inc(row, 1)
                nc.gpsimd.iota(idx[:], [[1, TP]], base=0, channel_multiplier=0,
                               allow_small_or_imprecise_dtypes=True).then_inc(row, 1)
                pool.wait_ge(row, 2)
                nc.gpsimd.iota(gx[:], [[1, NG]], base=0, channel_multiplier=0,
                               allow_small_or_imprecise_dtypes=True).then_inc(row, 1)

            @block.vector
            def _(dve):
                ch = Chain(dve, order)
                nc.vector.memset(k.counts[:, :, T:TP], 0.0)
                dve.wait_ge(g_in, 16)
                ch.then(nc.vector.tensor_copy(gf[:], gi[:]))
                nc.vector.tensor_reduce(ge[:, 0:1], gf[:], AX_X, ALU.min).then_inc(ext, 1)
                nc.vector.tensor_reduce(ge[:, 1:2], gf[:], AX_X, ALU.max).then_inc(ext, 1)
                dve.wait_ge(e_in, 32)
                nc.vector.tensor_copy(ef[:], ei[:]).then_inc(e_f, 1)
                dve.wait_ge(row, 3)
                ch.step(nc.vector.tensor_scalar(rg[:, 2, :], gx[:], -64.0, None, ALU.add))
                ch.step(nc.vector.tensor_scalar(rg[:, 3, :], gx[:], 1.0, None, ALU.add))
                dve.wait_ge(laid, 1)
                ch.then(nc.vector.tensor_copy(rg[:, 0:2, :], ps[0:1, 7, 0:2 * NG].rearrange("p (a n) -> p a n", a=2)))
                for g in range(PASSES):
                    ch.step(nc.vector.tensor_scalar(ac[:, 0, g, :], rg[:, 1, :], float(SPAN * g), None, ALU.is_ge))
                ch.wait()
                for g in range(PASSES):
                    ch.step(nc.vector.scalar_tensor_tensor(out=ac[:, 1, g, :], in0=rg[:, 0, :], scalar=float(SPAN * (g + 1)),
                                                           in1=ac[:, 0, g, :], op0=ALU.is_lt, op1=ALU.mult))
                ch.wait()
                for g in range(PASSES):
                    ch.step(nc.vector.tensor_tensor(ac[:, 2, g, :], ac[:, 1, g, :], rg[:, 2, :], ALU.mult))
                    ch.step(nc.vector.tensor_tensor(ac[:, 0, g, :], ac[:, 1, g, :], rg[:, 3, :], ALU.mult))
                ch.wait()
                ch.step(nc.vector.tensor_reduce(lim[:, 0, :], ac[:, 2], AX_X, ALU.min))
                ch.then(nc.vector.tensor_reduce(lim[:, 1, :], ac[:, 0], AX_X, ALU.max))
                ch.then(nc.vector.tensor_scalar(lim[:, 0, :], lim[:, 0, :], 64.0, float(NG - 1), ALU.add, ALU.min))
                ch.then(nc.vector.tensor_tensor(lim[:, 1, :], lim[:, 1, :], lim[:, 0, :], ALU.subtract))
                ch.then(nc.vector.tensor_scalar(lim[:, 1, :], lim[:, 1, :], 1.0, None, ALU.max))
                nc.vector.tensor_copy(limi[:], lim[:]).then_inc(bounds, 1)
                dve.wait_ge(bounds, 1)
                dve.wait_ge(e_f, 1)

                def make(g, first, i):
                    for u in range(U):
                        e = nc.s_assert_within((first + i) * U + u, 0, EC - 1,
                                               skip_runtime_bounds_check_because="first + groups is at most NG")
                        dve.wait_ge(free[g], i * U + u + 1)
                        nc.vector.tensor_scalar(hs[:, u, :], idx[:], ef[:, 0, bass.ds(e, 1)], None, ALU.is_equal)
                        nc.vector.tensor_scalar(hd[:, u, :], idx[:, SPAN * g:SPAN * (g + 1)], ef[:, 1, bass.ds(e, 1)],
                                                None, ALU.is_equal).then_inc(hot[g], 1)

                for g in range(PASSES):
                    first = dve.value_load(limi[0:1, 0, g:g + 1], min_val=0, max_val=NG - 1)
                    groups = dve.value_load(limi[0:1, 1, g:g + 1], min_val=1, max_val=NG)
                    with dve.Fori(0, groups) as i:
                        make(g, first, i)
                    for h in range(2):
                        t = 2 * g + h
                        dve.wait_ge(staged, t + 1)
                        nc.vector.tensor_tensor(st[:, h, tile_cols(t)], st[:, h, tile_cols(t)], k.ident[0:NT, 0:NT],
                                                ALU.add).then_inc(diag, 1)
                        dve.wait_ge(diag, t + 1)
                        if t >= 1:
                            dve.wait_ge(far_out[(t - 1) % 2], 16 * ((t - 1) // 2 + 1))
                        nc.vector.tensor_reduce(k.dinv[:, t:t + 1], st[:, h, 0:T], AX_X, ALU.add).then_inc(summed, 1)
                        nc.vector.tensor_scalar(far[:], st[:, h, :], 0.0, BIG, ALU.is_equal, ALU.mult).then_inc(summed, 1)

            @block.tensor
            def _(pe):
                pe.wait_ge(ext, 2)
                for j in range(2):
                    mm = nc.tensor.matmul(ps[0:1, 7, NG * j:NG * j + NG], ge[:, j:j + 1], k.ident[0:NG, 0:NG], start=True, stop=True)
                mm.then_inc(laid, 1)
                pe.wait_ge(row, 2)
                pe.wait_ge(bounds, 1)
                for g in range(PASSES):
                    groups = pe.value_load(limi[0:1, 1, g:g + 1], min_val=1, max_val=NG)
                    if g >= 1:
                        pe.wait_ge(staged, 2 * g)
                    for h in range(2):
                        for c in range(CH):
                            mm = nc.tensor.matmul(ps[0:NT, 3 * h + c, 0:CW], zero[:], idx[:, cols(c)], start=True, stop=False,
                                                  skip_group_check=True)
                            if 3 * h + c < U:
                                mm.then_inc(free[g], 1)
                    with pe.Fori(0, groups) as i:
                        for u in range(U):
                            pe.wait_ge(hot[g], i * U + u + 1)
                            for h in range(2):
                                for c in range(CH):
                                    mm = nc.tensor.matmul(ps[0:NT, 3 * h + c, 0:CW], hd[:, u, h * NT:(h + 1) * NT],
                                                          hs[:, u, cols(c)], start=False, stop=False, skip_group_check=True)
                            mm.then_inc(free[g], 1)
                    for h in range(2):
                        for c in range(CH):
                            mm = nc.tensor.matmul(ps[0:NT, 3 * h + c, 0:CW], zero[:], idx[:, cols(c)], start=False, stop=True,
                                                  skip_group_check=True)
                    mm.then_inc(fin, 1)
                    for h in range(2):
                        t = 2 * g + h
                        pe.wait_ge(diag, t + 1)
                        for q in range(3):
                            n = 3 * t + q
                            if n >= 2:
                                pe.wait_ge(placed, n - 1)
                            for s in range(4 * q, min(4 * q + 4, TILES)):
                                mm = nc.tensor.transpose(ps[0:NT, 6 + n % 2, NT * (s % 4):NT * (s % 4) + NT],
                                                         st[:, h, tile_cols(s)], k.ident[0:NT, 0:NT])
                            mm.then_inc(turned, 1)

            @block.scalar
            def _(act):
                for g in range(PASSES):
                    act.wait_ge(fin, g + 1)
                    for h in range(2):
                        t = 2 * g + h
                        if g >= 1:
                            act.wait_ge(summed, 2 * (t - 1))
                        nc.scalar.activation(st[:, h, :].rearrange("p (c n) -> p c n", c=CH), ps[0:NT, 3 * h:3 * h + CH, 0:CW],
                                             ACT.Copy).then_inc(staged, 1)
                    for h in range(2):
                        t = 2 * g + h
                        for q in range(3):
                            n = 3 * t + q
                            m = min(4, TILES - 4 * q)
                            act.wait_ge(turned, n + 1)
                            nc.scalar.activation(k.counts[:, 4 * q:4 * q + m, tile_cols(t)],
                                                 ps[0:NT, 6 + n % 2, 0:m * NT].rearrange("p (s n) -> p s n", s=m),
                                                 ACT.Copy).then_inc(placed, 1)


def aggregate_stage(k):
    nc, ps = k.nc, k.ps
    rooted, inv, scaled, dg = k.sem("deg_root"), k.sem("deg_inverse"), k.sem("agg_scaled"), k.sem("agg_diag")
    rowd, rows_out, done, out = k.sem("agg_row"), k.sem("agg_row_out"), k.sem("agg_done"), k.sem("agg_out")
    with ExitStack() as ctx:
        dg_sb = k.sb("agg_diag", [NT, TILES, NT], ctx=ctx)
        dinvb = k.sb("dinv_rows", [P, TP], ctx=ctx)
        with nc.Block(no_gpsimd_drain=True) as block:
            @block.scalar
            def _(act):
                nc.scalar.activation(k.dinv[:], k.dinv[:], ACT.Sqrt).then_inc(rooted, 1)
                act.wait_ge(rowd, 1)
                nc.scalar.activation(dinvb[:, 0:1000].rearrange("p (b n) -> p b n", b=2), ps[:, 6:8, 0:500], ACT.Copy)
                nc.scalar.activation(dinvb[:, 1000:T], ps[:, 5, 0:250], ACT.Copy).then_inc(rows_out, 1)

            @block.vector
            def _(dve):
                nc.vector.memset(dinvb[:, T:TP], 0.0)
                dve.wait_ge(rooted, 1)
                nc.vector.reciprocal(k.dinv[:], k.dinv[:]).then_inc(inv, 1)
                dve.wait_ge(inv, 1)
                for t in range(TILES):
                    nc.vector.tensor_scalar(k.x_node[:, t, :], k.x_node[:, t, :], k.dinv[:, t:t + 1], None,
                                            ALU.mult).then_inc(scaled, 1)
                for t in range(TILES):
                    nc.vector.tensor_scalar(dg_sb[:, t, :], k.ident[0:NT, 0:NT], k.dinv[:, t:t + 1], None, ALU.mult).then_inc(dg, 1)
                dve.wait_ge(rows_out, 1)
                for f in range(FC):
                    dve.wait_ge(done, f + 1)
                    g = 3 * (f % 2) if f else 0
                    nc.vector.tensor_tensor(k.nT[:, f, :].rearrange("p (c n) -> p c n", c=CH), ps[:, g:g + CH, 0:CW],
                                            dinvb[:].rearrange("p (c n) -> p c n", c=CH), ALU.mult).then_inc(out, 1)

            @block.tensor
            def _(pe):
                pe.wait_ge(dg, TILES)
                for t in range(TILES):
                    b = (6, 7, 5)[t // 4]
                    mm = nc.tensor.matmul(ps[:, b, NT * (t % 4):NT * (t % 4) + NT], k.ones[0:NT, :], dg_sb[:, t, :],
                                          start=True, stop=True)
                mm.then_inc(rowd, 1)
                pe.wait_ge(scaled, TILES)
                for f in range(FC):
                    if f == 1:
                        pe.wait_ge(rows_out, 1)
                    if f >= 2:
                        pe.wait_ge(out, f - 1)
                    for t in range(TILES):
                        for c in range(CH):
                            mm = nc.tensor.matmul(ps[:, 3 * (f % 2) + c, 0:CW], k.x_node[:, t, P * f:P * f + P],
                                                  k.counts[:, t, cols(c)], start=(t == 0), stop=(t == TILES - 1))
                    mm.then_inc(done, 1)


def project_stage(k, name, ins, w_dram, evacuate, extra_in=None):
    nc, ps = k.nc, k.ps
    nk = sum(n for _, n in ins)
    wl = [k.sem(f"{name}_weights{h}") for h in range(2)]
    done, out = k.sem(f"{name}_done"), k.sem(f"{name}_out")
    with ExitStack() as ctx:
        w = k.sb(f"{name}_w", [P, 2, nk, P], ctx=ctx)
        with nc.Block(no_gpsimd_drain=True) as block:
            @block.sync
            def _(sp):
                if extra_in:
                    extra_in(sp)
                for o in range(FC):
                    if o >= 2:
                        sp.wait_ge(done, o - 1)
                    sp.dma_start(w[:, o % 2], w_dram[o]).then_inc(wl[o % 2], 16)

            @block.tensor
            def _(pe):
                def pair(i):
                    for h in range(2):
                        pe.wait_ge(wl[h], 16 * i + 16)
                        if not isinstance(i, int):
                            pe.wait_ge(out, 2 * i + h - 1)
                        n = 0
                        for src, m in ins:
                            for f in range(m):
                                for c in range(CH):
                                    mm = nc.tensor.matmul(ps[:, 3 * h + c, 0:CW], w[:, h, n, :], src[:, f, cols(c)],
                                                          start=(n == 0), stop=(n == nk - 1))
                                n += 1
                        mm.then_inc(done, 1)
                pair(0)
                with pe.Fori(1, FC // 2) as i:
                    pair(i)

            @block.vector
            def _(dve):
                evacuate(dve, done, out)


def mix_project_stage(k, w_dram, bias_dram, x_dram):
    nc, ps = k.nc, k.ps
    x_in, b_in, badd = k.sem("x1_x"), k.sem("x1_bias"), k.sem("x1_bias_sum")
    with ExitStack() as ctx:
        bias = k.sb("x1_bias", [P, 2, FC], ctx=ctx)

        def loads(sp):
            for j in range(2):
                sp.dma_start(bias[:, j, :], bias_dram[j]).then_inc(b_in, 16)
            sp.dma_start(k.xT[:, :, 0:T], x_dram).then_inc(x_in, 16)

        def evacuate(dve, done, out):
            nc.vector.memset(k.xT[:, :, T:TP], 0.0).then_inc(badd, 1)
            dve.wait_ge(b_in, 32)
            nc.vector.tensor_tensor(bias[:, 0, :], bias[:, 0, :], bias[:, 1, :], ALU.add).then_inc(badd, 1)
            dve.wait_ge(badd, 2)
            dve.wait_ge(x_in, 16)
            for o in range(FC):
                dve.wait_ge(done, o + 1)
                g = 3 * (o % 2)
                xo = k.xT[:, o, :].rearrange("p (c n) -> p c n", c=CH)
                nc.vector.scalar_tensor_tensor(out=xo, in0=ps[:, g:g + CH, 0:CW], scalar=bias[:, 0, o:o + 1], in1=xo,
                                               op0=ALU.add, op1=ALU.add).then_inc(out, 1)
        project_stage(k, "x1", [(k.nT, FC), (k.attT, FC)], w_dram, evacuate, loads)


def norm_stage(k, name):
    nc, ps = k.nc, k.ps
    mean, cen, sq, var, eps, root, rec = (k.sem(f"{name}_{x}") for x in
                                          ("mean", "centred", "squared", "var", "eps", "root", "inverse"))
    with ExitStack() as ctx:
        s = k.sb(f"{name}_sq", [P, 2, TP], ctx=ctx)
        r = k.sb(f"{name}_r", [P, TP], ctx=ctx)
        r3 = r[:].rearrange("p (c n) -> p c n", c=CH)
        with nc.Block(no_gpsimd_drain=True) as block:
            @block.tensor
            def _(pe):
                for f in range(FC):
                    for c in range(CH):
                        mm = nc.tensor.matmul(ps[:, c, 0:CW], k.avg[:], k.xT[:, f, cols(c)], start=(f == 0), stop=(f == FC - 1))
                mm.then_inc(mean, 1)
                for f in range(FC):
                    pe.wait_ge(sq, f + 1)
                    for c in range(CH):
                        mm = nc.tensor.matmul(ps[:, 3 + c, 0:CW], k.avg[:], s[:, f % 2, cols(c)], start=(f == 0), stop=(f == FC - 1))
                    mm.then_inc(var, 1)

            @block.vector
            def _(dve):
                dve.wait_ge(mean, 1)
                for f in range(FC):
                    nc.vector.tensor_tensor(k.nT[:, f, :].rearrange("p (c n) -> p c n", c=CH),
                                            k.xT[:, f, :].rearrange("p (c n) -> p c n", c=CH), ps[:, 0:CH, 0:CW],
                                            ALU.subtract).then_inc(cen, 1)
                dve.wait_ge(var, FC)
                nc.vector.tensor_scalar(r3, ps[:, 3:6, 0:CW], EPS, None, ALU.add).then_inc(eps, 1)
                dve.wait_ge(root, 1)
                nc.vector.reciprocal(r[:], r[:]).then_inc(rec, 1)
                dve.wait_ge(rec, 1)
                for f in range(FC):
                    nc.vector.tensor_tensor(k.nT[:, f, :], k.nT[:, f, :], r[:], ALU.mult)

            @block.scalar
            def _(act):
                for f in range(FC):
                    act.wait_ge(cen, f + 1)
                    if f >= 2:
                        act.wait_ge(var, f - 1)
                    nc.scalar.activation(s[:, f % 2, :], k.nT[:, f, :], ACT.Square).then_inc(sq, 1)
                act.wait_ge(eps, 1)
                nc.scalar.activation(r[:], r[:], ACT.Sqrt).then_inc(root, 1)


def router_stage(k, name, E, rw_dram, rb_dram, renormalise, comb_dram, NB):
    nc, ps = k.nc, k.ps
    w_in, b_in, done, order, ex, turned, laid, stored = (k.sem(f"{name}_{x}") for x in (
        "w_in", "b_in", "scores", "order", "exp", "turned", "laid", "stored"))
    b0, cum, counted, consts = (k.sem(f"{name}_{x}") for x in ("neg", "one_hot", "counted", "consts"))
    with ExitStack() as ctx:
        w = k.sb(f"{name}_w", [P, FC, E], ctx=ctx)
        rb = k.sb(f"{name}_b", [NT, E], ctx=ctx)
        sc = k.sb(f"{name}_sc", [NT, TILES, E], ctx=ctx)
        ex_sb = k.sb(f"{name}_ex", [NT, TILES, E], ctx=ctx)
        top = k.sb(f"{name}_top", [NT, TILES, 8], ctx=ctx)
        idx = k.sb(f"{name}_idx", [NT, TILES, 8], U32, ctx=ctx)
        idf = k.sb(f"{name}_idf", [NT, TILES, 8], ctx=ctx)
        tmp = k.sb(f"{name}_tmp", [NT, 6, TILES], ctx=ctx)
        pr = k.sb(f"{name}_pr", [NT, TILES, 2], ctx=ctx)
        comb = k.sb(f"{name}_comb", [NT, 2, TILES, E], ctx=ctx)
        combT = k.sb(f"{name}_combT", [E, TP], ctx=ctx)
        hot = k.sb(f"{name}_hot", [NT, 3, TILES, E], ctx=ctx)
        before = k.sb(f"{name}_before", [NT, NT], ctx=ctx)
        thr = k.sb(f"{name}_thr", [NT, TILES], ctx=ctx)
        bidx = k.sb(f"{name}_bidx", [NT, NB], ctx=ctx)
        pos = k.sb(f"{name}_pos", [NT, TILES, E], ctx=ctx)
        carry = k.sb(f"{name}_carry", [NT, TILES + 1, E], ctx=ctx)
        over = k.sb(f"{name}_over", [NT, E, TILES], ctx=ctx)
        start = k.sb(f"{name}_start", [NT, E + 1], ctx=ctx)
        nblk = k.sb(f"{name}_nblk", [NT, E], ctx=ctx)
        row = k.sb(f"{name}_row", [NT, 2, TILES], ctx=ctx)
        past = k.sb(f"{name}_past", [1, NB, E], ctx=ctx)
        bex = k.sb(f"{name}_bex", [1, NB], ctx=ctx)
        with nc.Block(no_gpsimd_drain=True) as block:
            @block.sync
            def _(sp):
                sp.dma_start(w[:], rw_dram).then_inc(w_in, 16)
                if rb_dram is not None:
                    sp.dma_start(rb[:], rb_dram.partition_broadcast(NT)).then_inc(b_in, 16)
                sp.wait_ge(laid, 1)
                sp.dma_start(comb_dram[0:E, :], combT[:]).then_inc(stored, 16)
                sp.wait_ge(stored, 16)

            @block.gpsimd
            def _(pool):
                nc.gpsimd.memset(before[:], 0.0).then_inc(consts, 1)
                pool.wait_ge(consts, 1)
                nc.gpsimd.affine_select(out=before[:], in_=before[:], compare_op=ALU.is_ge, fill=1.0, base=0,
                                        pattern=[[-1, NT]], channel_multiplier=1).then_inc(consts, 1)
                pool.wait_ge(consts, 2)
                nc.gpsimd.iota(thr[:], [[P, TILES]], base=0, channel_multiplier=0,
                               allow_small_or_imprecise_dtypes=True).then_inc(consts, 1)
                pool.wait_ge(consts, 3)
                nc.gpsimd.iota(bidx[:], [[1, NB]], base=0, channel_multiplier=0,
                               allow_small_or_imprecise_dtypes=True).then_inc(consts, 1)

            @block.tensor
            def _(pe):
                pe.wait_ge(w_in, 16)
                for t in range(TILES):
                    for f in range(FC):
                        mm = nc.tensor.matmul(ps[0:NT, 0, E * t:E * t + E], k.nT[:, f, tile_cols(t)], w[:, f, :],
                                              start=(f == 0), stop=(f == FC - 1))
                mm.then_inc(done, 1)
                pe.wait_ge(b0, 2)
                for t in range(TILES):
                    mm = nc.tensor.transpose(ps[0:E, 1 + t // 4, NT * (t % 4):NT * (t % 4) + NT], comb[:, 0, t, :],
                                             k.ident[0:NT, 0:NT])
                mm.then_inc(turned, 1)
                pe.wait_ge(cum, 1)
                pe.wait_ge(consts, 4)
                both = hot[:, 2].rearrange("p t e -> p (t e)")
                nc.tensor.matmul(ps[0:NT, 5, 0:TILES * E], before[:], both, start=True, stop=True)
                nc.tensor.matmul(ps[0:NT, 6, 0:TILES * E], k.ones[0:NT, 0:NT], both, start=True, stop=True).then_inc(counted, 1)

            @block.scalar
            def _(act):
                act.wait_ge(b0, 1)
                nc.scalar.activation(ex_sb[:], ex_sb[:], ACT.Exp)
                nc.scalar.activation(tmp[:, 1, :], tmp[:, 0, :], ACT.Exp).then_inc(ex, 1)
                act.wait_ge(turned, 1)
                nc.scalar.activation(combT[:, 0:1000].rearrange("p (b n) -> p b n", b=2), ps[0:E, 1:3, 0:500], ACT.Copy)
                nc.scalar.activation(combT[:, 1000:T], ps[0:E, 3, 0:250], ACT.Copy).then_inc(laid, 1)

            @block.vector
            def _(dve):
                ch = Chain(dve, order)
                ch.step(nc.vector.memset(combT[:, T:TP], 0.0))
                dve.wait_ge(done, 1)
                s3 = ps[0:NT, 0, 0:TILES * E].rearrange("p (t e) -> p t e", t=TILES)
                if rb_dram is not None:
                    dve.wait_ge(b_in, 16)
                    ch.then(nc.vector.tensor_tensor(sc[:], s3, rb[:].unsqueeze(1).broadcast_to([NT, TILES, E]), ALU.add))
                else:
                    ch.then(nc.vector.tensor_copy(sc[:], s3))
                for t in range(TILES):
                    ch.step(nc.vector.max(top[:, t, :], sc[:, t, :]))
                ch.wait()
                for t in range(TILES):
                    ch.step(nc.vector.max_index(idx[:, t, :], top[:, t, :], sc[:, t, :]))
                    ch.step(nc.vector.tensor_scalar(ex_sb[:, t, :], sc[:, t, :], top[:, t, 0:1], None, ALU.subtract))
                ch.wait()
                nc.vector.tensor_tensor(tmp[:, 0, :], top[:, :, 1], top[:, :, 0], ALU.subtract).then_inc(b0, 1)
                ch.step(nc.vector.tensor_copy(idf[:], idx[:]))
                dve.wait_ge(ex, 1)
                ch.then(nc.vector.tensor_reduce(tmp[:, 2, :], ex_sb[:], AX_X, ALU.add))
                ch.then(nc.vector.reciprocal(tmp[:, 3, :], tmp[:, 2, :]))
                ch.step(nc.vector.tensor_copy(pr[:, :, 0], tmp[:, 3, :]))
                ch.then(nc.vector.tensor_tensor(pr[:, :, 1], tmp[:, 1, :], tmp[:, 3, :], ALU.mult))
                if renormalise:
                    ch.then(nc.vector.tensor_reduce(tmp[:, 4, :], pr[:], AX_X, ALU.add))
                    ch.then(nc.vector.tensor_scalar(tmp[:, 4, :], tmp[:, 4, :], 1e-9, None, ALU.add))
                    ch.then(nc.vector.reciprocal(tmp[:, 5, :], tmp[:, 4, :]))
                    for j in range(2):
                        ch.step(nc.vector.tensor_tensor(pr[:, :, j], pr[:, :, j], tmp[:, 5, :], ALU.mult))
                    ch.wait()
                for t in range(TILES):
                    for j in range(2):
                        ch.step(nc.vector.tensor_scalar(comb[:, j, t, :], k.index16[0:NT, 0:E], idf[:, t, j:j + 1], pr[:, t, j:j + 1],
                                                        ALU.is_equal, ALU.mult))
                        ch.step(nc.vector.tensor_scalar(hot[:, j, t, :], k.index16[0:NT, 0:E], idf[:, t, j:j + 1], None, ALU.is_equal))
                ch.step(nc.vector.tensor_copy(k.weight[:], pr[:]))
                ch.wait()
                nc.vector.tensor_tensor(comb[:, 0, :, :], comb[:, 0, :, :], comb[:, 1, :, :], ALU.add).then_inc(b0, 1)
                nc.vector.tensor_tensor(hot[:, 2], hot[:, 0], hot[:, 1], ALU.add).then_inc(cum, 1)
                ch.step(nc.vector.memset(carry[:, 0, :], 0.0))
                ch.step(nc.vector.memset(start[:, 0:1], 0.0))
                dve.wait_ge(counted, 1)
                ch.wait()
                for t in range(TILES):
                    ch.then(nc.vector.tensor_tensor(carry[:, t + 1, :], carry[:, t, :], ps[0:NT, 6, E * t:E * t + E], ALU.add))
                ch.step(nc.vector.tensor_tensor(over[:], carry[:, TILES, :].unsqueeze(2).broadcast_to([NT, E, TILES]),
                                                thr[:].unsqueeze(1).broadcast_to([NT, E, TILES]), ALU.is_gt))
                ch.then(nc.vector.tensor_tensor(pos[:], ps[0:NT, 5, 0:TILES * E].rearrange("p (t e) -> p t e", e=E),
                                                carry[:, 0:TILES, :], ALU.add))
                ch.then(nc.vector.tensor_reduce(nblk[:], over[:], AX_X, ALU.add))
                for e in range(E):
                    ch.then(nc.vector.tensor_tensor(start[:, e + 1:e + 2], start[:, e:e + 1], nblk[:, e:e + 1], ALU.add))
                ch.step(nc.vector.tensor_tensor(past[:], bidx[0:1, :].unsqueeze(2).broadcast_to([1, NB, E]),
                                                start[0:1, 1:E + 1].unsqueeze(1).broadcast_to([1, NB, E]), ALU.is_ge))
                ch.then(nc.vector.tensor_scalar(nblk[:], start[:, 0:E], float(P), None, ALU.mult))
                ch.step(nc.vector.tensor_reduce(bex[:], past[:], AX_X, ALU.add))
                ch.then(nc.vector.tensor_tensor(pos[:], pos[:], nblk[:].unsqueeze(1).broadcast_to([NT, TILES, E]), ALU.add))
                ch.step(nc.vector.tensor_scalar(k.block_expert[:, 0:NB], bex[:], float(E - 1), None, ALU.min))
                for j in range(2):
                    ch.step(nc.vector.tensor_tensor(hot[:, j], hot[:, j], pos[:], ALU.mult))
                ch.wait()
                for j in range(2):
                    ch.step(nc.vector.tensor_reduce(row[:, j, :], hot[:, j], AX_X, ALU.add))
                ch.wait()
                ch.step(nc.vector.tensor_copy(k.slot[:], row[:]))


def scatter_stage(k, name, rows_dram):
    nc, ps = k.nc, k.ps
    turned, copied, sent = k.sem(f"{name}_turned"), k.sem(f"{name}_copied"), k.soft_sem(f"{name}_sent")
    with ExitStack() as ctx:
        node = k.sb(f"{name}_node", [NT, TILES, D], ctx=ctx)
        with nc.Block() as block:
            @block.tensor
            def _(pe):
                for t in range(TILES):
                    for h in range(2):
                        n = 2 * t + h
                        if n >= 8:
                            pe.wait_ge(copied, n - 7)
                        for f in range(3):
                            mm = nc.tensor.transpose(ps[0:NT, n % 8, P * f:P * f + P], k.nT[:, 3 * h + f, tile_cols(t)], k.ident[:])
                        mm.then_inc(turned, 1)

            @block.scalar
            def _(act):
                for n in range(2 * TILES):
                    act.wait_ge(turned, n + 1)
                    nc.scalar.activation(node[:, n // 2, HALF * (n % 2):HALF * (n % 2) + HALF], ps[0:NT, n % 8, 0:HALF],
                                         ACT.Copy).then_inc(copied, 1)

            @block.gpsimd
            def _(pool):
                for t in range(TILES):
                    pool.wait_ge(copied, 2 * t + 2)
                    for j in range(2):
                        pool.indirect_dma_start(rows_dram, bass.IndirectOffsetOnAxis(ap=k.slot[:, j, t:t + 1], axis=0),
                                                node[:, t, :], None).then_inc(sent, 16)
                pool.wait_ge(sent, 16 * 2 * TILES)


def combine_stage(k, name, rows_dram):
    nc, ps = k.nc, k.ps
    got = [k.soft_sem(f"{name}_got{h}") for h in range(4)]
    mixed, both, turned, added = (k.sem(f"{name}_{x}") for x in ("mixed", "both", "turned", "added"))
    with ExitStack() as ctx:
        y = k.sb(f"{name}_y", [NT, 4, 2, D], ctx=ctx)
        with nc.Block() as block:
            @block.gpsimd
            def _(pool):
                for t in range(TILES):
                    if t >= 4:
                        pool.wait_ge(turned, 2 * (t - 3))
                    for j in range(2):
                        pool.indirect_dma_start(y[:, t % 4, j, :], None, rows_dram,
                                                bass.IndirectOffsetOnAxis(ap=k.slot[:, j, t:t + 1], axis=0)).then_inc(got[t % 4], 16)

            @block.vector
            def _(dve):
                def add(t):
                    for h in range(2):
                        n = 2 * t + h
                        dve.wait_ge(turned, n + 1)
                        nc.vector.tensor_tensor(k.xT[:, 3 * h:3 * h + 3, tile_cols(t)], k.xT[:, 3 * h:3 * h + 3, tile_cols(t)],
                                                ps[:, n % 8, 0:3 * NT].rearrange("p (f n) -> p f n", f=3), ALU.add).then_inc(added, 1)
                for t in range(TILES):
                    dve.wait_ge(got[t % 4], 32 * (t // 4 + 1))
                    nc.vector.tensor_scalar(y[:, t % 4, 0, :], y[:, t % 4, 0, :], k.weight[:, t, 0:1], None, ALU.mult).then_inc(mixed, 1)
                    dve.wait_ge(mixed, t + 1)
                    nc.vector.scalar_tensor_tensor(out=y[:, t % 4, 0, :], in0=y[:, t % 4, 1, :], scalar=k.weight[:, t, 1:2],
                                                   in1=y[:, t % 4, 0, :], op0=ALU.mult, op1=ALU.add).then_inc(both, 1)
                    if t >= 1:
                        add(t - 1)
                add(TILES - 1)

            @block.tensor
            def _(pe):
                for t in range(TILES):
                    pe.wait_ge(both, t + 1)
                    for h in range(2):
                        n = 2 * t + h
                        if n >= 8:
                            pe.wait_ge(added, n - 7)
                        for f in range(3):
                            mm = nc.tensor.transpose(ps[:, n % 8, NT * f:NT * f + NT], y[:, t % 4, 0, P * (3 * h + f):P * (3 * h + f) + P],
                                                     k.ident[0:NT, 0:NT])
                        mm.then_inc(turned, 1)


def block_stage(k, name, NB, E, w_dram, x_rows, y_rows, gated):
    nc, ps = k.nc, k.ps
    WC = FC * D
    W1 = FC * 512 if gated else WC
    KH = 2
    s = {n: k.sem(f"{name}_{n}") for n in (
        "x_turned", "x_high", "x_split", "w_high", "w_split", "v_high", "v_split", "h_done", "sig", "u1", "hidden", "h_turned",
        "h_high", "h_split", "y_done", "y_out")}
    xl, wl, vl, st = ([k.sem(f"{name}_{n}{h}") for h in range(2)] for n in ("x_in", "w_in", "v_in", "stored"))
    with ExitStack() as ctx:
        w = k.sb(f"{name}_w", [P, 2, WC], ctx=ctx)
        whi = k.sb(f"{name}_wh", [P, 2, WC], F32R, ctx=ctx)
        wlo = k.sb(f"{name}_wl", [P, 2, WC], F32R, ctx=ctx)
        x = k.sb(f"{name}_x", [P, 2, D], ctx=ctx)
        xhi = k.sb(f"{name}_xh", [P, 2, FC, P], F32R, ctx=ctx)
        xlo = k.sb(f"{name}_xl", [P, 2, FC, P], F32R, ctx=ctx)
        y = k.sb(f"{name}_y", [P, 2, D], ctx=ctx)
        if gated:
            sg = k.sb(f"{name}_sg", [P, 256], ctx=ctx)
            hid = k.sb(f"{name}_hid", [P, 2, 256], ctx=ctx)
            hhi = k.sb(f"{name}_hh", [P, KH, P], F32R, ctx=ctx)
            hlo = k.sb(f"{name}_hl", [P, KH, P], F32R, ctx=ctx)

        def run(eng, step):
            for j in range(4):
                step(j, j % 2, False)
            with eng.Fori(2, NB // 2 - 1) as i:
                for h in range(2):
                    step(2 * i + h, h, False)
            for h in range(2):
                step(NB - 2 + h, h, h == 1)

        def ge(eng, sem, value):
            if not isinstance(value, int) or value > 0:
                eng.wait_ge(sem, value)

        def count(j, h):
            return (j - h) * 8 + 16

        with nc.Block(no_gpsimd_drain=True) as block:
            @block.sync
            def _(sp):
                def step(j, h, last):
                    ge(sp, s["x_turned"], j - 1)
                    sp.dma_start(x[:, h, :], x_rows[bass.ds(j * P, P), :]).then_inc(xl[h], 16)
                    e = sp.value_load(k.block_expert[0:1, bass.ds(j, 1)], min_val=0, max_val=E - 1)
                    ge(sp, s["w_split"], j - 1)
                    sp.dma_start(w[:, h, 0:W1], w_dram[bass.ds(e, 1), :, 0:W1].rearrange("e p n -> (e p) n")).then_inc(wl[h], 16)
                    if gated:
                        ge(sp, s["v_split"], j - 1)
                        sp.dma_start(w[:, h, W1:], w_dram[bass.ds(e, 1), :, W1:].rearrange("e p n -> (e p) n")).then_inc(vl[h], 16)
                run(sp, step)

            @block.tensor
            def _(pe):
                def three(out, lhs, rhs, f, n):
                    for m, (a, b) in enumerate(((0, 0), (0, 1), (1, 0))):
                        mm = nc.tensor.matmul(out, lhs[a], rhs[b], start=(f == 0 and m == 0), stop=(f == n - 1 and m == 2))
                    return mm

                def turn_x(j, h):
                    pe.wait_ge(xl[h], count(j, h))
                    ge(pe, s["x_split"], j)
                    for f in range(FC):
                        mm = nc.tensor.transpose(ps[:, f // 3, P * (f % 3):P * (f % 3) + P], x[:, h, P * f:P * f + P], k.ident[:])
                    mm.then_inc(s["x_turned"], 1)

                def product(j, h):
                    pe.wait_ge(s["x_split"], j + 1)
                    pe.wait_ge(s["w_split"], j + 1)
                    if gated:
                        ge(pe, s["hidden"], j - 1)
                        for f in range(FC):
                            mm = three(ps[:, 2 + h, :], (xhi[:, h, f, :], xlo[:, h, f, :]),
                                       (whi[:, h, 512 * f:512 * f + 512], wlo[:, h, 512 * f:512 * f + 512]), f, FC)
                        mm.then_inc(s["h_done"], 1)
                    else:
                        ge(pe, s["y_out"], j - 1)
                        for f in range(FC):
                            for q in range(2):
                                c0 = D * f + HALF * q
                                mm = three(ps[:, 2 + 2 * h + q, 0:HALF], (xhi[:, h, f, :], xlo[:, h, f, :]),
                                           (whi[:, h, c0:c0 + HALF], wlo[:, h, c0:c0 + HALF]), f, FC)
                        mm.then_inc(s["y_done"], 1)

                def turn_hidden(j, h):
                    pe.wait_ge(s["hidden"], j + 1)
                    ge(pe, s["h_split"], j)
                    for f in range(KH):
                        mm = nc.tensor.transpose(ps[:, 4, P * f:P * f + P], hid[:, h, P * f:P * f + P], k.ident[:])
                    mm.then_inc(s["h_turned"], 1)

                def result(j, h):
                    pe.wait_ge(s["h_split"], j + 1)
                    pe.wait_ge(s["v_split"], j + 1)
                    ge(pe, s["y_out"], j)
                    for f in range(KH):
                        for q in range(2):
                            c0 = W1 + D * f + HALF * q
                            mm = three(ps[:, 5 + q, 0:HALF], (hhi[:, f, :], hlo[:, f, :]),
                                       (whi[:, h, c0:c0 + HALF], wlo[:, h, c0:c0 + HALF]), f, KH)
                    mm.then_inc(s["y_done"], 1)

                def step(j, h, last):
                    product(j, h)
                    if gated and not (isinstance(j, int) and j == 0):
                        result(j - 1, 1 - h)
                    if not last:
                        turn_x(j + 1, 1 - h)
                    if gated:
                        turn_hidden(j, h)
                turn_x(0, 0)
                run(pe, step)
                if gated:
                    result(NB - 1, 1)

            @block.scalar
            def _(act):
                def weights_high(j, h):
                    act.wait_ge(wl[h], count(j, h))
                    ge(act, s["h_done" if gated else "y_done"], j - 1)
                    nc.scalar.activation(whi[:, h, 0:W1], w[:, h, 0:W1], ACT.Copy).then_inc(s["w_high"], 1)

                def rest_high(j, h):
                    act.wait_ge(vl[h], count(j, h))
                    ge(act, s["y_done"], j - 1)
                    nc.scalar.activation(whi[:, h, W1:], w[:, h, W1:], ACT.Copy).then_inc(s["v_high"], 1)

                def x_high(j, h):
                    act.wait_ge(s["x_turned"], j + 1)
                    ge(act, s["h_done" if gated else "y_done"], j - 1)
                    nc.scalar.activation(xhi[:, h, :, :].rearrange("p (b f) n -> p b (f n)", b=2), ps[:, 0:2, 0:3 * P],
                                         ACT.Copy).then_inc(s["x_high"], 1)

                def y_out(j, h):
                    act.wait_ge(s["y_done"], j + 1)
                    ge(act, st[h], count(j, h) - 16)
                    b = 5 if gated else 2 + 2 * h
                    nc.scalar.activation(y[:, h, :].rearrange("p (b n) -> p b n", b=2), ps[:, b:b + 2, 0:HALF],
                                         ACT.Copy).then_inc(s["y_out"], 1)
                    act.wait_ge(s["y_out"], j + 1)
                    act.dma_start(y_rows[bass.ds(j * P, P), :], y[:, h, :]).then_inc(st[h], 16)

                def step(j, h, last):
                    if not last:
                        weights_high(j + 1, 1 - h)
                    if gated:
                        act.wait_ge(s["h_done"], j + 1)
                        ge(act, s["u1"], j)
                        nc.scalar.activation(sg[:], ps[:, 2 + h, 0:256], ACT.Sigmoid).then_inc(s["sig"], 1)
                        if not (isinstance(j, int) and j == 0):
                            y_out(j - 1, 1 - h)
                    if not last:
                        x_high(j + 1, 1 - h)
                        if gated:
                            rest_high(j + 1, 1 - h)
                    if gated:
                        act.wait_ge(s["h_turned"], j + 1)
                        ge(act, s["y_done"], j)
                        nc.scalar.activation(hhi[:].rearrange("p f n -> p (f n)"), ps[:, 4, 0:256], ACT.Copy).then_inc(s["h_high"], 1)
                    else:
                        y_out(j, h)
                weights_high(0, 0)
                x_high(0, 0)
                if gated:
                    rest_high(0, 0)
                run(act, step)
                if gated:
                    y_out(NB - 1, 1)
                for h in range(2):
                    act.wait_ge(st[h], 16 * (NB // 2))

            @block.vector
            def _(dve):
                def weights_low(j, h):
                    dve.wait_ge(s["w_high"], j + 1)
                    nc.vector.tensor_tensor(wlo[:, h, 0:W1], w[:, h, 0:W1], whi[:, h, 0:W1].bitcast(F32), ALU.subtract)\
                        .then_inc(s["w_split"], 1)

                def rest_low(j, h):
                    dve.wait_ge(s["v_high"], j + 1)
                    nc.vector.tensor_tensor(wlo[:, h, W1:], w[:, h, W1:], whi[:, h, W1:].bitcast(F32), ALU.subtract)\
                        .then_inc(s["v_split"], 1)

                def x_low(j, h):
                    dve.wait_ge(s["x_high"], j + 1)
                    nc.vector.tensor_tensor(xlo[:, h, :, :].rearrange("p (b f) n -> p b (f n)", b=2), ps[:, 0:2, 0:3 * P],
                                            xhi[:, h, :, :].rearrange("p (b f) n -> p b (f n)", b=2).bitcast(F32),
                                            ALU.subtract).then_inc(s["x_split"], 1)

                def step(j, h, last):
                    if not last:
                        weights_low(j + 1, 1 - h)
                    if gated:
                        dve.wait_ge(s["sig"], j + 1)
                        nc.vector.tensor_tensor(hid[:, h, :], ps[:, 2 + h, 0:256], sg[:], ALU.mult).then_inc(s["u1"], 1)
                        dve.wait_ge(s["u1"], j + 1)
                        nc.vector.tensor_tensor(hid[:, h, :], ps[:, 2 + h, 256:512], hid[:, h, :], ALU.mult).then_inc(s["hidden"], 1)
                    if not last:
                        x_low(j + 1, 1 - h)
                        if gated:
                            rest_low(j + 1, 1 - h)
                    if gated:
                        dve.wait_ge(s["h_high"], j + 1)
                        nc.vector.tensor_tensor(hlo[:].rearrange("p f n -> p (f n)"), ps[:, 4, 0:256],
                                                hhi[:].rearrange("p f n -> p (f n)").bitcast(F32), ALU.subtract).then_inc(s["h_split"], 1)
                weights_low(0, 0)
                x_low(0, 0)
                if gated:
                    rest_low(0, 0)
                run(dve, step)


def routed_bias_stage(k, eb_dram, comb_dram, E):
    nc, ps = k.nc, k.ps
    done, eb_in, out = k.sem("rb_done"), k.sem("rb_in"), k.sem("rb_out")
    with ExitStack() as ctx:
        eb = k.sb("rb_b", [E, D], ctx=ctx)
        ct = k.sb("rb_comb", [E, TP], ctx=ctx)
        with nc.Block(no_gpsimd_drain=True) as block:
            @block.sync
            def _(sp):
                sp.dma_start(eb[:], eb_dram).then_inc(eb_in, 16)
                sp.dma_start(ct[:], comb_dram[:, :]).then_inc(eb_in, 16)

            @block.tensor
            def _(pe):
                pe.wait_ge(eb_in, 32)
                for o in range(FC):
                    if o >= 2:
                        pe.wait_ge(out, o - 1)
                    for c in range(CH):
                        mm = nc.tensor.matmul(ps[:, 3 * (o % 2) + c, 0:CW], eb[:, P * o:P * o + P], ct[:, cols(c)], start=True, stop=True)
                    mm.then_inc(done, 1)

            @block.vector
            def _(dve):
                for o in range(FC):
                    dve.wait_ge(done, o + 1)
                    g = 3 * (o % 2)
                    xo = k.xT[:, o, :].rearrange("p (c n) -> p c n", c=CH)
                    nc.vector.tensor_tensor(xo, xo, ps[:, g:g + CH, 0:CW], ALU.add).then_inc(out, 1)


def flow_attention_stage(k, w_qk, b_qk, w_v, b_v):
    nc, ps = k.nc, k.ps
    H = 2 * FC
    E6 = 1e-6
    s = {n: k.sem("fa_" + n) for n in (
        "qk_done", "qk_out", "turned", "copied", "order", "dots1", "dots2", "flow1", "sums", "v_done", "v_out",
        "columns", "flow2", "exp", "total", "comp", "vscaled", "kv", "kv_out", "att", "att_out", "att_turned", "att_copied",
        "cols_in", "eps_made")}
    wl = [k.sem(f"fa_weights{h}") for h in range(2)]
    with ExitStack() as ctx:
        qT = k.sb("fa_qT", [P, FC, TP], ctx=ctx)
        kT = k.attT
        q_node = k.sb("fa_q_node", [NT, TILES, D], ctx=ctx)
        k_node = k.sb("fa_k_node", [NT, TILES, D], ctx=ctx)
        w = k.sb("fa_w", [P, 2, FC, HALF], ctx=ctx)
        ws = w[:].rearrange("p s f n -> p s (f n)")[:, :, 0:D].rearrange("p s (f n) -> p s f n", f=FC)
        bqk = k.sb("fa_bqk", [P, 2 * FC], ctx=ctx)
        part = k.sb("fa_part", [P, 2 * FC, CH], ctx=ctx)
        vec = k.sb("fa_vec", [P, 2 * FC], ctx=ctx)
        head2 = k.sb("fa_head2", [P, 2], ctx=ctx)
        cl = k.sb("fa_columns", [P, 2, 2, FC, 2], ctx=ctx)
        epsr = k.sb("fa_eps_rows", [NT, 2, H], ctx=ctx)
        fl = k.sb("fa_flow", [NT, 5, TILES, H], ctx=ctx)
        tot = epsr
        kvb = k.sb("fa_kvb", [P, FC, P], ctx=ctx)
        epsm = kvb[:, 0, 0:NT]
        v_node, mix_node = q_node, k_node
        with nc.Block(no_gpsimd_drain=True) as block:
            @block.sync
            def _(sp):
                sp.dma_start(bqk[:], b_qk).then_inc(s["cols_in"], 16)
                for j in range(2 * FC):
                    if j >= 2:
                        sp.wait_ge(s["qk_done"], CH * (j - 1))
                    sp.dma_start(ws[:, j % 2], w_qk[j]).then_inc(wl[j % 2], 16)

            @block.vector
            def _(dve):
                nc.vector.tensor_copy(head2[:], k.heads2[:, 0:P:64])
                nc.vector.memset(epsm, E6).then_inc(s["eps_made"], 1)
                nc.vector.memset(qT[:, :, T:TP], 0.0)
                nc.vector.memset(kT[:, :, T:TP], 0.0)
                for g in range(2 * FC):
                    for q in range(3):
                        n = 3 * g + q
                        m = min(4, TILES - 4 * q)
                        dst, c = (q_node, g) if g < FC else (k_node, g - FC)
                        dve.wait_ge(s["turned"], n + 1)
                        nc.vector.tensor_copy(dst[:, 4 * q:4 * q + m, P * c:P * c + P],
                                              ps[0:NT, 6 + n % 2, 0:m * P].rearrange("p (t d) -> p t d", t=m)).then_inc(s["copied"], 1)

            @block.scalar
            def _(act):
                act.wait_ge(s["cols_in"], 16)
                for j in range(2 * FC):
                    dst = (qT if j < FC else kT)[:, j % FC, :]
                    for c in range(CH):
                        n = j * CH + c
                        act.wait_ge(s["qk_done"], n + 1)
                        wd = min(CW, T - c * CW)
                        nc.scalar.activation(dst[:, c * CW:c * CW + wd], ps[:, n % 6, 0:wd], ACT.Sigmoid, bias=bqk[:, j:j + 1],
                                             accum_out=part[:, j, c:c + 1]).then_inc(s["qk_out"], 1)

            @block.tensor
            def _(pe):
                def turn(g):
                    src, c = (qT, g) if g < FC else (kT, g - FC)
                    pe.wait_ge(s["qk_out"], CH * (g + 1))
                    for q in range(3):
                        n = 3 * g + q
                        if n >= 2:
                            pe.wait_ge(s["copied"], n - 1)
                        for t in range(4 * q, min(4 * q + 4, TILES)):
                            mm = nc.tensor.transpose(ps[0:NT, 6 + n % 2, P * (t % 4):P * (t % 4) + P], src[:, c, tile_cols(t)],
                                                     k.ident[:])
                        mm.then_inc(s["turned"], 1)
                for j in range(2 * FC):
                    pe.wait_ge(wl[j % 2], 16 * (j // 2 + 1))
                    for c in range(CH):
                        n = j * CH + c
                        if n >= 6:
                            pe.wait_ge(s["qk_out"], n - 5)
                        for f in range(FC):
                            mm = nc.tensor.matmul(ps[:, n % 6, 0:CW], ws[:, j % 2, f, :], k.nT[:, f, cols(c)],
                                                  start=(f == 0), stop=(f == FC - 1))
                        mm.then_inc(s["qk_done"], 1)
                    if j >= 1:
                        turn(j - 1)
                turn(2 * FC - 1)

        b_in, v_in = k.sem("fa_vbias_in"), [k.sem(f"fa_v_in{h}") for h in range(2)]
        bv = k.sb("fa_bv", [NT, D], ctx=ctx)
        with nc.Block(no_gpsimd_drain=True) as block:
            @block.sync
            def _(sp):
                sp.dma_start(bv[:], b_v.partition_broadcast(NT)).then_inc(b_in, 16)
                for h in range(2):
                    sp.dma_start(w[:, h], w_v[h]).then_inc(v_in[h], 16)

            @block.tensor
            def _(pe):
                def dots(step, done):
                    for side, src in ((0, qT), (1, kT)):
                        for t in range(TILES):
                            for p in range(FC):
                                nc.tensor.matmul(ps[0:NT, side, H * t + 2 * p:H * t + 2 * p + 2], src[:, p, tile_cols(t)],
                                                 cl[:, step, side, p, :], start=True, stop=True)
                    for side in range(2):
                        for p in range(FC):
                            mm = nc.tensor.matmul(ps[0:NT, 2, H * side + 2 * p:H * side + 2 * p + 2], epsm,
                                                  cl[:, step, side, p, :], start=True, stop=True)
                    mm.then_inc(done, 1)
                pe.wait_ge(s["columns"], 1)
                dots(0, s["dots1"])
                pe.wait_ge(s["flow1"], 2)
                for side, src, wt in ((0, k_node, 1), (1, q_node, 0)):
                    for p in range(FC):
                        for t in range(TILES):
                            mm = nc.tensor.matmul(ps[:, 3 + side, 2 * p:2 * p + 2], src[:, t, P * p:P * p + P],
                                                  fl[:, wt, t, 2 * p:2 * p + 2], start=(t == 0), stop=(t == TILES - 1))
                mm.then_inc(s["sums"], 1)
                pe.wait_ge(s["columns"], 2)
                dots(1, s["dots2"])
                for h in range(2):
                    pe.wait_ge(v_in[h], 16)
                    for t in range(TILES):
                        n = h * TILES + t
                        if n >= 3:
                            pe.wait_ge(s["v_out"], n - 2)
                        for f in range(FC):
                            mm = nc.tensor.matmul(ps[0:NT, 5 + n % 3, 0:HALF], k.nT[:, f, tile_cols(t)], w[:, h, f, :],
                                                  start=(f == 0), stop=(f == FC - 1))
                        mm.then_inc(s["v_done"], 1)
                pe.wait_ge(s["exp"], 3)
                nc.tensor.matmul(ps[0:NT, 3, 0:H], k.ones[0:NT, 0:NT], tot[:, 0, :], start=True, stop=True).then_inc(s["total"], 1)
                pe.wait_ge(s["vscaled"], TILES)
                for p in range(FC):
                    for t in range(TILES):
                        mm = nc.tensor.matmul(ps[:, p % 2, 0:P], k_node[:, t, P * p:P * p + P], v_node[:, t, P * p:P * p + P],
                                              start=(t == 0), stop=(t == TILES - 1))
                    mm.then_inc(s["kv"], 1)
                    if p < FC - 1:
                        if p >= 1:
                            pe.wait_ge(s["kv_out"], p)
                pe.wait_ge(s["kv_out"], FC)
                for t in range(TILES):
                    for h in range(2):
                        n = 2 * t + h
                        if n >= 4:
                            pe.wait_ge(s["att_out"], n - 3)
                        for p in range(3):
                            mm = nc.tensor.matmul(ps[0:NT, n % 4, P * p:P * p + P], qT[:, 3 * h + p, tile_cols(t)],
                                                  kvb[:, 3 * h + p, :], start=True, stop=True)
                        mm.then_inc(s["att"], 1)
                for c in range(FC):
                    for q in range(3):
                        n = 3 * c + q
                        pe.wait_ge(s["att_out"], 2 * TILES)
                        if n >= 4:
                            pe.wait_ge(s["att_copied"], n - 3)
                        for t in range(4 * q, min(4 * q + 4, TILES)):
                            mm = nc.tensor.transpose(ps[:, 4 + n % 4, NT * (t % 4):NT * (t % 4) + NT],
                                                     mix_node[:, t, P * c:P * c + P], k.ident[0:NT, 0:NT])
                        mm.then_inc(s["att_turned"], 1)

            @block.scalar
            def _(act):
                act.wait_ge(s["flow2"], 1)
                nc.scalar.activation(fl[:, 2, :, :], fl[:, 2, :, :], ACT.Sigmoid).then_inc(s["exp"], 1)
                nc.scalar.activation(fl[:, 3, :, :], fl[:, 3, :, :], ACT.Exp).then_inc(s["exp"], 1)
                for c in range(FC):
                    for q in range(3):
                        n = 3 * c + q
                        m = min(4, TILES - 4 * q)
                        act.wait_ge(s["att_turned"], n + 1)
                        nc.scalar.activation(k.attT[:, c, 4 * NT * q:4 * NT * q + m * NT], ps[:, 4 + n % 4, 0:m * NT],
                                             ACT.Copy).then_inc(s["att_copied"], 1)

            @block.vector
            def _(dve):
                ch = Chain(dve, s["order"])

                def masked(step, side, values):
                    return nc.vector.scalar_tensor_tensor(out=cl[:, step, side], in0=values, scalar=E6,
                                                          in1=head2[:].unsqueeze(1).broadcast_to([P, FC, 2]), op0=ALU.add, op1=ALU.mult)
                ch.then(nc.vector.tensor_reduce(vec[:], part[:], AX_X, ALU.add))
                ch.then(masked(0, 0, vec[:, FC:].unsqueeze(2).broadcast_to([P, FC, 2])))
                masked(0, 1, vec[:, 0:FC].unsqueeze(2).broadcast_to([P, FC, 2])).then_inc(s["columns"], 1)

                def dots_out(step, sem, dst0, dst1):
                    dve.wait_ge(sem, 1)
                    ch.then(nc.vector.tensor_scalar(epsr[:], ps[0:NT, 2, 0:2 * H].rearrange("p (s h) -> p s h", s=2), E6, None, ALU.add))
                    for side, dst in ((0, dst0), (1, dst1)):
                        ch.step(nc.vector.tensor_tensor(dst, ps[0:NT, side, 0:TILES * H].rearrange("p (t h) -> p t h", h=H),
                                                        epsr[:, side, :].unsqueeze(1).broadcast_to([NT, TILES, H]), ALU.add))
                    ch.wait()
                dots_out(0, s["dots1"], fl[:, 2], fl[:, 3])
                nc.vector.reciprocal(fl[:, 0], fl[:, 2]).then_inc(s["flow1"], 1)
                nc.vector.reciprocal(fl[:, 1], fl[:, 3]).then_inc(s["flow1"], 1)
                dve.wait_ge(s["sums"], 1)
                ch.then(masked(1, 0, ps[:, 3, 0:H].rearrange("p (c h) -> p c h", h=2)))
                masked(1, 1, ps[:, 4, 0:H].rearrange("p (c h) -> p c h", h=2)).then_inc(s["columns"], 1)
                dots_out(1, s["dots2"], fl[:, 2], fl[:, 4])
                nc.vector.tensor_scalar(fl[:, 3], fl[:, 4], -1.0, 1.0, ALU.max, ALU.min).then_inc(s["flow2"], 1)
                dve.wait_ge(s["exp"], 2)
                nc.vector.tensor_reduce(tot[:, 0, :], fl[:, 3].rearrange("p t h -> p h t"), AX_X, ALU.add).then_inc(s["exp"], 1)
                ch.step(nc.vector.tensor_tensor(fl[:, 2], fl[:, 2], fl[:, 0], ALU.mult))
                dve.wait_ge(b_in, 16)
                for n in range(2 * TILES):
                    h, t = n // TILES, n % TILES
                    dve.wait_ge(s["v_done"], n + 1)
                    nc.vector.tensor_tensor(v_node[:, t, HALF * h:HALF * h + HALF], ps[0:NT, 5 + n % 3, 0:HALF],
                                            bv[:, HALF * h:HALF * h + HALF], ALU.add).then_inc(s["v_out"], 1)
                dve.wait_ge(s["total"], 1)
                ch.then(nc.vector.reciprocal(tot[:, 1, :], ps[0:NT, 3, 0:H]))
                ch.then(nc.vector.tensor_scalar(tot[:, 1, :], tot[:, 1, :], float(T), None, ALU.mult))
                ch.then(nc.vector.tensor_tensor(fl[:, 4], fl[:, 3], tot[:, 1, :].unsqueeze(1).broadcast_to([NT, TILES, H]), ALU.mult))
                dve.wait_ge(s["v_out"], 2 * TILES)
                for t in range(TILES):
                    v3 = v_node[:, t, :].rearrange("p (h e) -> p h e", h=H)
                    nc.vector.tensor_tensor(v3, v3, fl[:, 4, t, :].unsqueeze(2).broadcast_to([NT, H, D // H]),
                                            ALU.mult).then_inc(s["vscaled"], 1)
                for p in range(FC):
                    dve.wait_ge(s["kv"], p + 1)
                    nc.vector.tensor_tensor(kvb[:, p, :], ps[:, p % 2, 0:P], k.heads2[:], ALU.mult).then_inc(s["kv_out"], 1)
                for n in range(2 * TILES):
                    t, h = n // 2, n % 2
                    dve.wait_ge(s["att"], n + 1)
                    nc.vector.tensor_tensor(mix_node[:, t, HALF * h:HALF * h + HALF].rearrange("p (h e) -> p h e", h=FC),
                                            ps[0:NT, n % 4, 0:HALF].rearrange("p (h e) -> p h e", h=FC),
                                            fl[:, 2, t, FC * h:FC * h + FC].unsqueeze(2).broadcast_to([NT, FC, D // H]),
                                            ALU.mult).then_inc(s["att_out"], 1)


def flow_project_stage(k, w_dram, bias_dram):
    nc, ps = k.nc, k.ps
    wl = [k.sem(f"fp_weights{h}") for h in range(2)]
    done, gated, out, b_in, b2 = k.sem("fp_done"), k.sem("fp_gated"), k.sem("fp_out"), k.sem("fp_bias_in"), k.sem("fp_bias2")
    with ExitStack() as ctx:
        w = k.sb("fp_w", [P, 2, FC, P], ctx=ctx)
        g_sb = k.sb("fp_gate", [P, 2, TP], ctx=ctx)
        bias = k.sb("fp_bias", [P, FC], ctx=ctx)
        with nc.Block(no_gpsimd_drain=True) as block:
            @block.sync
            def _(sp):
                sp.dma_start(bias[:], bias_dram).then_inc(b_in, 16)
                for o in range(FC):
                    if o >= 2:
                        sp.wait_ge(done, o - 1)
                    sp.dma_start(w[:, o % 2], w_dram[o]).then_inc(wl[o % 2], 16)

            @block.tensor
            def _(pe):
                for o in range(FC):
                    pe.wait_ge(wl[o % 2], 16 * (o // 2 + 1))
                    if o >= 2:
                        pe.wait_ge(gated, o - 1)
                    for f in range(FC):
                        for c in range(CH):
                            mm = nc.tensor.matmul(ps[:, 3 * (o % 2) + c, 0:CW], w[:, o % 2, f, :], k.attT[:, f, cols(c)],
                                                  start=(f == 0), stop=(f == FC - 1))
                    mm.then_inc(done, 1)

            @block.scalar
            def _(act):
                act.wait_ge(b2, 1)
                for o in range(FC):
                    act.wait_ge(done, o + 1)
                    if o >= 2:
                        act.wait_ge(out, o - 1)
                    g = 3 * (o % 2)
                    nc.scalar.activation(g_sb[:, o % 2, :].rearrange("p (c n) -> p c n", c=CH), ps[:, g:g + CH, 0:CW],
                                         ACT.Sigmoid, bias=bias[:, o:o + 1], scale=2.0).then_inc(gated, 1)

            @block.vector
            def _(dve):
                dve.wait_ge(b_in, 16)
                nc.vector.tensor_scalar(bias[:], bias[:], 2.0, None, ALU.mult).then_inc(b2, 1)
                for o in range(FC):
                    dve.wait_ge(gated, o + 1)
                    nc.vector.tensor_tensor(k.xT[:, o, :], k.xT[:, o, :], g_sb[:, o % 2, :], ALU.add).then_inc(out, 1)


def graph_layer(k, name, heads, F, w_dram, att_dram, b_dram, wide, h1_dram=None):
    nc, ps = k.nc, k.ps
    NF = F // P
    DEN = NF
    HB = 2 if wide else 1
    s = {n: k.sem(f"{name}_{n}") for n in (
        "h_done", "h_out", "al", "order", "as_diag", "as_row", "as_out", "far_read", "r_diag", "r_row", "r_out",
        "low", "exped", "p_made", "summed", "agg", "inverse", "scaled", "clipped", "elu_exp", "result")}
    w_in, at_in, b_in = k.sem(f"{name}_w_in"), k.sem(f"{name}_att_in"), k.sem(f"{name}_b_in")
    far_in = [k.sem(f"{name}_far_in{h}") for h in range(2)]
    st_out = [k.sem(f"{name}_stored{h}") for h in range(2)] if wide else None
    LR = 0.2
    with ExitStack() as ctx:
        if wide:
            h_sb = k.sb(f"{name}_h", [NT, HB, TILES, F], ctx=ctx)
            w = k.sb(f"{name}_w", [P, FC, F], ctx=ctx)
        else:
            h_sb = k.h2[:, :].rearrange("p (a t f) -> p a t f", a=1, t=TILES)
        a_rows = k.sb(f"{name}_a", [NT, 2, F], ctx=ctx)
        al = k.sb(f"{name}_al", [NT, 2, 3, TILES], ctx=ctx)
        mx = k.sb(f"{name}_mx", [NT, 5, TILES], ctx=ctx)
        rows = k.sb(f"{name}_rows", [P, 2, TP], ctx=ctx)
        far = k.sb(f"{name}_far", [NT, 2, T], BF16, ctx=ctx)
        tt = k.sb(f"{name}_scratch", [NT, 6 * CW], ctx=ctx)
        t1, t2 = (tt[:, a * CW:b * CW].rearrange("p (s n) -> p s n", n=CW) for a, b in ((0, 4), (4, 6)))
        dg = tt[:, 0:T].rearrange("p (t n) -> p t n", n=NT)
        scr = tt[:, T:T + F]
        mscr = tt[:, T:T + T // 2].bitcast(BF16)
        pr = k.sb(f"{name}_p", [NT, 2, TILES, CW], ctx=ctx)
        sm = k.sb(f"{name}_sm", [NT, 2, CW], ctx=ctx)
        rden = k.sb(f"{name}_rden", [P, CW], ctx=ctx)
        o1 = k.sb(f"{name}_o1", [P, 2, CW], ctx=ctx)
        o2 = k.sb(f"{name}_o2", [P, 2, CW], ctx=ctx)
        bias = k.sb(f"{name}_bias", [P, heads * NF], ctx=ctx)
        NR = TILES * heads
        with nc.Block(no_gpsimd_drain=True) as block:
            @block.sync
            def _(sp):
                def head_in(i):
                    if i >= 1:
                        sp.wait_ge(s["al"], 2 * TILES * i)
                    for j in range(2):
                        sp.dma_start(a_rows[:, j, :], att_dram[j, i].partition_broadcast(NT)).then_inc(at_in, 16)
                    if wide:
                        if i >= 1:
                            sp.wait_ge(s["h_done"], TILES * i)
                        sp.dma_start(w[:], w_dram[i]).then_inc(w_in, 16)

                sp.dma_start(bias[:], b_dram).then_inc(b_in, 16)
                head_in(0)
                for i in range(heads):
                    if i + 1 < heads:
                        head_in(i + 1)
                    for t in range(TILES):
                        n = i * TILES + t
                        if n >= 2:
                            sp.wait_ge(s["far_read"], n - 1)
                        sp.dma_start(far[:, n % 2, :], k.far_dram[t]).then_inc(far_in[n % 2], 16)
                    if wide:
                        for m in range(NF * CH * i, NF * CH * (i + 1)):
                            c, f = m // NF % CH, m % NF
                            sp.wait_ge(s["result"], m + 1)
                            sp.dma_start(h1_dram[NF * i + f, :, cols(c)], o2[:, m % 2, :]).then_inc(st_out[m % 2], 16)
                if wide:
                    for h in range(2):
                        sp.wait_ge(st_out[h], 16 * (NF * CH * heads // 2))

            @block.tensor
            def _(pe):
                def project(i, ts):
                    if ts[0] == 0:
                        pe.wait_ge(w_in, 16 * (i + 1))
                    for t in ts:
                        n = i * TILES + t
                        if n >= 2:
                            pe.wait_ge(s["h_out"], n - 1)
                        if i >= 1 and t == 0:
                            pe.wait_ge(s["as_out"], 2 * i)
                        if t == 5 and i >= 1:
                            pe.wait_ge(s["r_out"], 4 * i)
                        for f in range(FC):
                            mm = nc.tensor.matmul(ps[0:NT, 5 + t % 2, 0:F], k.nT[:, f, tile_cols(t)], w[:, f, :],
                                                  start=(f == 0), stop=(f == FC - 1))
                        mm.then_inc(s["h_done"], 1)

                def lay(n_diag, sem_in, wait, sem_out):
                    pe.wait_ge(sem_in, n_diag)
                    pe.wait_ge(*wait)
                    for t in range(TILES):
                        b = 5 + t // 4
                        mm = nc.tensor.matmul(ps[:, b, NT * (t % 4):NT * (t % 4) + NT], k.ones[0:NT, :], dg[:, t, :],
                                              start=True, stop=True)
                    mm.then_inc(sem_out, 1)

                def a_row(i):
                    lay(TILES * (i + 1), s["as_diag"], (s["h_out"], TILES * (i + 1)) if wide else (s["al"], 1), s["as_row"])

                def r_rows(i):
                    for j in range(2):
                        wait = (s["as_out"], 2 * (i + 1)) if j == 0 else (s["r_out"], 2 * (2 * i + 1))
                        if wide and j == 0 and i + 1 < heads:
                            pe.wait_ge(s["h_out"], TILES * (i + 1) + 5)
                        lay(TILES * (2 * i + j + 1), s["r_diag"], wait, s["r_row"])

                def aggregate(i):
                    for c in range(CH):
                        n = CH * i + c
                        for f in range(NF):
                            if f == 0:
                                pe.wait_ge(s["p_made"], TILES * (n + 1))
                            if n >= 1:
                                pe.wait_ge(s["scaled"], NF * (n - 1) + f + 1)
                            for t in range(TILES):
                                mm = nc.tensor.matmul(ps[:, f, 0:CW], h_sb[:, i % HB, t, P * f:P * f + P], pr[:, n % 2, t, :],
                                                      start=(t == 0), stop=(t == TILES - 1))
                            mm.then_inc(s["agg"], 1)
                            if f == 0:
                                pe.wait_ge(s["summed"], TILES * (n + 1))
                                if n >= 1:
                                    pe.wait_ge(s["inverse"], n)
                                nc.tensor.matmul(ps[:, DEN, 0:CW], k.ones[0:NT, :], sm[:, n % 2, :], start=True, stop=True)\
                                    .then_inc(s["agg"], 1)

                if wide:
                    project(0, range(TILES))
                a_row(0)
                for i in range(heads):
                    if wide and i + 1 < heads:
                        project(i + 1, range(0, 5))
                    r_rows(i)
                    if wide and i + 1 < heads:
                        project(i + 1, range(5, TILES))
                    aggregate(i)
                    if i + 1 < heads:
                        a_row(i + 1)

            @block.scalar
            def _(act):
                nexp = [0]

                def h_copy(i, t):
                    act.wait_ge(s["h_done"], i * TILES + t + 1)
                    if i >= 2 and t == 0:
                        act.wait_ge(s["agg"], CH * (NF + 1) * (i - 1))
                    nc.scalar.activation(h_sb[:, i % HB, t, :], ps[0:NT, 5 + t % 2, 0:F], ACT.Copy).then_inc(s["h_out"], 1)

                def row_copy(j, sem):
                    nc.scalar.activation(rows[:, j, 0:1000].rearrange("p (b n) -> p b n", b=2), ps[:, 5:7, 0:500], ACT.Copy).then_inc(sem, 1)
                    nc.scalar.activation(rows[:, j, 1000:T], ps[:, 7, 0:250], ACT.Copy).then_inc(sem, 1)

                def exps(m):
                    for _ in range(m):
                        n = nexp[0]
                        nexp[0] += 1
                        act.wait_ge(s["low"], n + 1)
                        nc.scalar.activation(t1[:, n % 4, :], t1[:, n % 4, :], ACT.Exp).then_inc(s["exped"], 1)

                def elus(n):
                    if wide:
                        for f in range(NF):
                            act.wait_ge(s["clipped"], 2 * (NF * n + f + 1))
                            nc.scalar.activation(o1[:, (NF * n + f) % 2, :], o1[:, (NF * n + f) % 2, :], ACT.Exp).then_inc(s["elu_exp"], 1)
                if wide:
                    for t in range(TILES):
                        h_copy(0, t)
                act.wait_ge(s["as_row"], 1)
                row_copy(0, s["as_out"])
                for i in range(heads):
                    more = wide and i + 1 < heads
                    if more:
                        for t in range(5):
                            h_copy(i + 1, t)
                    for j in range(2):
                        act.wait_ge(s["r_row"], 2 * i + j + 1)
                        row_copy(j, s["r_out"])
                    for t in range(5):
                        exps(2)
                        if more:
                            h_copy(i + 1, 5 + t)
                    exps(TILES)
                    elus(CH * i)
                    exps(TILES)
                    elus(CH * i + 1)
                    elus(CH * i + 2)
                    if i + 1 < heads:
                        act.wait_ge(s["as_row"], i + 2)
                        row_copy(0, s["as_out"])

            @block.gpsimd
            def _(pool):
                for n in range(CH * heads):
                    for t in range(TILES):
                        m = n * TILES + t
                        pool.wait_ge(s["p_made"], m + 1)
                        if t == 0:
                            if n >= 2:
                                pool.wait_ge(s["inverse"], n - 1)
                            nc.gpsimd.tensor_copy(sm[:, n % 2, :], pr[:, n % 2, 0, :]).then_inc(s["summed"], 1)
                        else:
                            pool.wait_ge(s["summed"], m)
                            nc.gpsimd.tensor_tensor(sm[:, n % 2, :], sm[:, n % 2, :], pr[:, n % 2, t, :], ALU.add)\
                                .then_inc(s["summed"], 1)

            @block.vector
            def _(dve):
                ch = Chain(dve, s["order"])
                ch.step(nc.vector.memset(rows[:, :, T:TP], 0.0))
                made = [0]

                def logits(i):
                    dve.wait_ge(at_in, 32 * (i + 1))
                    for t in range(TILES):
                        if wide:
                            dve.wait_ge(s["h_out"], i * TILES + t + 1)
                        for j in range(2):
                            nc.vector.tensor_tensor_reduce(scr[:], h_sb[:, i % HB, t, :], a_rows[:, j, :], 1.0, 0.0, ALU.mult, ALU.add,
                                                           al[:, i % 2, j, t:t + 1]).then_inc(s["al"], 1)
                            dve.wait_ge(s["al"], 2 * (i * TILES + t) + j + 1)
                    ch.then(nc.vector.tensor_scalar(al[:, i % 2, 2, :], al[:, i % 2, 0, :], LR, None, ALU.mult))

                def as_diag(i):
                    if i >= 1:
                        dve.wait_ge(s["r_row"], 2 * i)
                    for t in range(TILES):
                        nc.vector.tensor_scalar(dg[:, t, :], k.ident[0:NT, 0:NT], al[:, i % 2, 0, t:t + 1], None,
                                                ALU.mult).then_inc(s["as_diag"], 1)

                def maxima(i):
                    dve.wait_ge(s["as_out"], 2 * (i + 1))
                    for t in range(TILES):
                        n = i * TILES + t
                        dve.wait_ge(far_in[n % 2], 16 * (n // 2 + 1))
                        nc.vector.tensor_tensor_reduce(mscr[:], rows[0:NT, 0, 0:T], far[:, n % 2, :], 1.0, 3 * BIG, ALU.add, ALU.max,
                                                       mx[:, 0, t:t + 1]).then_inc(s["far_read"], 1)
                        dve.wait_ge(s["far_read"], n + 1)
                    ch.then(nc.vector.tensor_tensor(mx[:, 0, :], mx[:, 0, :], al[:, i % 2, 1, :], ALU.add))
                    ch.then(nc.vector.tensor_scalar(mx[:, 2, :], mx[:, 0, :], LR, None, ALU.mult))
                    ch.then(nc.vector.tensor_tensor(mx[:, 1, :], mx[:, 0, :], mx[:, 2, :], ALU.max))
                    ch.step(nc.vector.tensor_tensor(mx[:, 3, :], al[:, i % 2, 1, :], mx[:, 1, :], ALU.subtract))
                    ch.then(nc.vector.scalar_tensor_tensor(out=mx[:, 4, :], in0=al[:, i % 2, 1, :], scalar=LR, in1=mx[:, 1, :],
                                                           op0=ALU.mult, op1=ALU.subtract))
                    for j in range(2):
                        if j == 0:
                            dve.wait_ge(s["as_row"], i + 1)
                        else:
                            dve.wait_ge(s["r_row"], 2 * i + 1)
                        for t in range(TILES):
                            nc.vector.tensor_scalar(dg[:, t, :], k.ident[0:NT, 0:NT], mx[:, 3 + j, t:t + 1], None,
                                                    ALU.mult).then_inc(s["r_diag"], 1)

                def weights(i, c):
                    n = CH * i + c
                    if c == 0:
                        dve.wait_ge(s["r_out"], 4 * (i + 1))
                    if n >= 2:
                        dve.wait_ge(s["agg"], (NF + 1) * (n - 1))
                        dve.wait_ge(s["summed"], TILES * (n - 1))
                    for t in range(TILES + 2):
                        if t < TILES:
                            m = n * TILES + t
                            ch.step(nc.vector.tensor_scalar(t1[:, m % 4, :], rows[0:NT, 0, cols(c)], al[:, i % 2, 0, t:t + 1], 0.0,
                                                            ALU.add, ALU.min))
                            ch.then(nc.vector.tensor_scalar(t2[:, m % 2, :], rows[0:NT, 1, cols(c)], al[:, i % 2, 2, t:t + 1], 0.0,
                                                            ALU.add, ALU.min))
                            nc.vector.tensor_tensor(t1[:, m % 4, :], t1[:, m % 4, :], t2[:, m % 2, :], ALU.max).then_inc(s["low"], 1)
                        if t >= 2:
                            m = n * TILES + t - 2
                            dve.wait_ge(s["exped"], m + 1)
                            nc.vector.tensor_tensor(pr[:, n % 2, t - 2, :], t1[:, m % 4, :], k.counts[:, t - 2, cols(c)],
                                                    ALU.mult).then_inc(s["p_made"], 1)
                            dve.wait_ge(s["p_made"], m + 1)

                def results(i, c):
                    n = CH * i + c
                    for f in range(NF):
                        m = NF * n + f
                        base = (NF + 1) * n
                        if f == 0:
                            dve.wait_ge(s["agg"], base + 2)
                            ch.then(nc.vector.tensor_scalar(rden[:], ps[:, DEN, 0:CW], 1e-16, None, ALU.add))
                            nc.vector.reciprocal(rden[:], rden[:]).then_inc(s["inverse"], 1)
                            dve.wait_ge(s["inverse"], n + 1)
                        dve.wait_ge(s["agg"], base + (1 if f == 0 else f + 2))
                        if wide:
                            if m >= 2:
                                dve.wait_ge(st_out[m % 2], 16 * (m // 2))
                            nc.vector.tensor_tensor(o1[:, m % 2, :], ps[:, f, 0:CW], rden[:], ALU.mult).then_inc(s["scaled"], 1)
                            dve.wait_ge(s["scaled"], m + 1)
                            b = bias[:, NF * i + f:NF * i + f + 1]
                            nc.vector.tensor_scalar(o2[:, m % 2, :], o1[:, m % 2, :], b, 0.0, ALU.add, ALU.max).then_inc(s["clipped"], 1)
                            dve.wait_ge(s["clipped"], 2 * m + 1)
                            nc.vector.tensor_scalar(o1[:, m % 2, :], o1[:, m % 2, :], b, 0.0, ALU.add, ALU.min).then_inc(s["clipped"], 1)
                            dve.wait_ge(s["elu_exp"], m + 1)
                            nc.vector.scalar_tensor_tensor(out=o2[:, m % 2, :], in0=o2[:, m % 2, :], scalar=-1.0, in1=o1[:, m % 2, :],
                                                           op0=ALU.add, op1=ALU.add).then_inc(s["result"], 1)
                        else:
                            if m >= 2:
                                dve.wait_ge(s["result"], m - 1)
                            nc.vector.tensor_tensor(o1[:, m % 2, :], ps[:, f, 0:CW], rden[:], ALU.mult).then_inc(s["scaled"], 1)
                            dve.wait_ge(s["scaled"], m + 1)
                            nc.vector.scalar_tensor_tensor(out=k.xT[:, f, cols(c)], in0=o1[:, m % 2, :], scalar=bias[:, f:f + 1],
                                                           in1=k.xT[:, f, cols(c)], op0=ALU.add, op1=ALU.add).then_inc(s["result"], 1)
                logits(0)
                as_diag(0)
                maxima(0)
                dve.wait_ge(b_in, 16)
                for i in range(heads):
                    weights(i, 0)
                    if i + 1 < heads:
                        logits(i + 1)
                    weights(i, 1)
                    results(i, 0)
                    weights(i, 2)
                    results(i, 1)
                    results(i, 2)
                    if i + 1 < heads:
                        as_diag(i + 1)
                        maxima(i + 1)



def project_wide_stage(k, w_dram, h1_dram):
    nc, ps = k.nc, k.ps
    KC = 16
    w_in, done, out = k.sem("w2_in"), k.sem("h2_done"), k.sem("h2_out")
    h_in = [k.sem(f"h1_in{h}") for h in range(2)]
    with ExitStack() as ctx:
        w = k.sb("w2_w", [P, KC, D], ctx=ctx)
        h1 = k.sb("h1_tile", [P, 2, KC, NT], ctx=ctx)
        with nc.Block(no_gpsimd_drain=True) as block:
            @block.sync
            def _(sp):
                sp.dma_start(w[:], w_dram).then_inc(w_in, 16)
                for t in range(TILES):
                    if t >= 2:
                        sp.wait_ge(done, 2 * (t - 1))
                    sp.dma_start(h1[:, t % 2], h1_dram[:, :, tile_cols(t)].rearrange("c p n -> p c n")).then_inc(h_in[t % 2], 16)

            @block.tensor
            def _(pe):
                pe.wait_ge(w_in, 16)
                for t in range(TILES):
                    pe.wait_ge(h_in[t % 2], 16 * (t // 2 + 1))
                    for h in range(2):
                        n = 2 * t + h
                        if n >= 4:
                            pe.wait_ge(out, n - 3)
                        for c in range(KC):
                            mm = nc.tensor.matmul(ps[0:NT, n % 4, 0:HALF], h1[:, t % 2, c, :], w[:, c, HALF * h:HALF * h + HALF],
                                                  start=(c == 0), stop=(c == KC - 1))
                        mm.then_inc(done, 1)

            @block.scalar
            def _(act):
                for n in range(2 * TILES):
                    act.wait_ge(done, n + 1)
                    nc.scalar.activation(k.h2[:, D * (n // 2) + HALF * (n % 2):D * (n // 2) + HALF * (n % 2) + HALF],
                                         ps[0:NT, n % 4, 0:HALF], ACT.Copy).then_inc(out, 1)


def shared_expert_stage(k, w13_dram, w2_dram, E):
    nc, ps = k.nc, k.ps
    s = {n: k.sem("ge_" + n) for n in ("h_done", "sig", "u1", "h_out", "y_done", "y_out")}
    wl, w2l = ([k.sem(f"ge_{n}{h}") for h in range(2)] for n in ("w13", "w2"))
    U = 2 * CH
    Y = FC * CH
    with ExitStack() as ctx:
        w13 = k.sb("ge_w13", [P, 2, 2, 2, FC, P], ctx=ctx)
        w2 = k.sb("ge_w2", [P, 2, 2, D], ctx=ctx)
        hid = k.sb("ge_hid", [P, 2, 2, TP], ctx=ctx)
        sg = k.sb("ge_sig", [P, 2, CW], ctx=ctx)
        with nc.Block(no_gpsimd_drain=True) as block:
            @block.sync
            def _(sp):
                def load(i, j):
                    e = 2 * i + j
                    if not isinstance(i, int):
                        sp.wait_ge(s["h_out"], U * (e - 1))
                    sp.dma_start(w13[:, j], w13_dram[e]).then_inc(wl[j], 16)
                    if not isinstance(i, int):
                        sp.wait_ge(s["y_done"], Y * (e - 1))
                    sp.dma_start(w2[:, j], w2_dram[e]).then_inc(w2l[j], 16)
                for j in range(2):
                    load(0, j)

            @block.tensor
            def _(pe):
                def hidden(i, j):
                    e = 2 * i + j
                    pe.wait_ge(wl[j], 16 * i + 16)
                    for u in range(U):
                        q, c = u // CH, u % CH
                        n = U * e + u
                        if not (isinstance(i, int) and n < 2):
                            pe.wait_ge(s["h_out"], n - 1)
                        for g in range(2):
                            for f in range(FC):
                                mm = nc.tensor.matmul(ps[:, 2 * (u % 2) + g, 0:CW], w13[:, j, q, g, f, :], k.nT[:, f, cols(c)],
                                                      start=(f == 0), stop=(f == FC - 1))
                        mm.then_inc(s["h_done"], 1)

                def outputs(i, j):
                    e = 2 * i + j
                    pe.wait_ge(w2l[j], 16 * i + 16)
                    pe.wait_ge(s["h_out"], U * (e + 1))
                    for y in range(Y):
                        o, c = y // CH, y % CH
                        n = Y * e + y
                        if not (isinstance(i, int) and n < 4):
                            pe.wait_ge(s["y_out"], n - 3)
                        for q in range(2):
                            mm = nc.tensor.matmul(ps[:, 4 + (Y * j + y) % 4, 0:CW], w2[:, j, q, P * o:P * o + P],
                                                  hid[:, j, q, cols(c)], start=(q == 0), stop=(q == 1))
                        mm.then_inc(s["y_done"], 1)
                hidden(0, 0)
                hidden(0, 1)
                outputs(0, 0)
                outputs(0, 1)

            @block.scalar
            def _(act):
                def unit(n, u, guard):
                    act.wait_ge(s["h_done"], n + 1)
                    if guard:
                        act.wait_ge(s["h_out"], n - 1)
                    nc.scalar.activation(sg[:, u % 2, :], ps[:, 2 * (u % 2), 0:CW], ACT.Sigmoid).then_inc(s["sig"], 1)
                for u in range(U):
                    unit(u, u, u >= 2)
                for u in range(U):
                    unit(U + u, u, True)

            @block.vector
            def _(dve):
                def hidden(i, j):
                    e = 2 * i + j
                    if not isinstance(i, int):
                        dve.wait_ge(s["y_done"], Y * (e - 1))
                    for u in range(U):
                        q, c = u // CH, u % CH
                        n = U * e + u
                        h = hid[:, j, q, cols(c)]
                        dve.wait_ge(s["sig"], n + 1)
                        nc.vector.tensor_tensor(h, ps[:, 2 * (u % 2), 0:CW], sg[:, u % 2, :], ALU.mult).then_inc(s["u1"], 1)
                        dve.wait_ge(s["u1"], n + 1)
                        nc.vector.tensor_tensor(h, ps[:, 2 * (u % 2) + 1, 0:CW], h, ALU.mult).then_inc(s["h_out"], 1)

                def outputs(i, j):
                    for y in range(Y):
                        o, c = y // CH, y % CH
                        n = Y * (2 * i + j) + y
                        dve.wait_ge(s["y_done"], n + 1)
                        if not (isinstance(i, int) and n < Y):
                            dve.wait_ge(s["y_out"], n - Y + 1)
                        nc.vector.tensor_tensor(k.xT[:, o, cols(c)], ps[:, 4 + (Y * j + y) % 4, 0:CW], k.xT[:, o, cols(c)],
                                                ALU.add).then_inc(s["y_out"], 1)
                hidden(0, 0)
                hidden(0, 1)
                outputs(0, 0)
                outputs(0, 1)




def store_stage(k, src, out_dram):
    stored = k.sem("y_stored")
    with k.nc.Block(no_gpsimd_drain=True) as block:
        @block.sync
        def _(sp):
            sp.dma_start(out_dram, src[:, :, 0:T]).then_inc(stored, 16)
            sp.wait_ge(stored, 16)


STOP = 99


def program(nc, a, out):
    with ExitStack() as ctx:
        k = Kit(nc, ctx)
        k.ps = ctx.enter_context(nc.psum_tensor("ps", [P, 8, 512], F32))
        k.sem_ctx = layer0 = ctx.enter_context(ExitStack())
        ones_stage(k)
        nbuf = k.sb("normed", [P, TILES * D])
        k.nT = nbuf[:, 0:FC * TP].rearrange("p (c n) -> p c n", c=FC)
        k.h2 = nbuf[0:NT, :]
        k.dinv = k.sb("dinv", [NT, TILES])
        k.slot = k.sb("slot", [NT, 2, TILES], U32)
        k.weight = k.sb("choice_weight", [NT, TILES, 2])
        k.block_expert = k.sb("block_expert", [1, NB1], I32)
        x_rows = nc.dram_tensor("x_rows", (NB1 * P, D), F32, kind="Internal").ap()
        y_rows0 = nc.dram_tensor("y_rows0", (NB0 * P, D), F32, kind="Internal").ap()
        y_rows1 = nc.dram_tensor("y_rows1", (NB1 * P, D), F32, kind="Internal").ap()
        k.far_dram = nc.dram_tensor("far", (TILES, NT, T), BF16, kind="Internal").ap()
        k.counts_dram = nc.dram_tensor("counts_keep", (NT, TILES, TP), F32, kind="Internal").ap()
        x_park = nc.dram_tensor("x_park", (P, FC, TP), F32, kind="Internal").ap()
        comb0 = nc.dram_tensor("comb0", (8, TP), F32, kind="Internal").ap()
        comb1 = nc.dram_tensor("comb1", (16, TP), F32, kind="Internal").ap()
        h1_dram = nc.dram_tensor("h1", (16, P, TP), F32, kind="Internal").ap()
        out_f = out.rearrange("(c p) n -> p c n", p=P)

        def stop(n, src):
            if STOP == n:
                store_stage(k, src, out_f)
            return STOP == n

        with ExitStack() as first:
            k.x_node = k.sb("x_node", [NT, TILES, D], ctx=first)
            k.attT = k.sb("attT", [P, FC, TP], ctx=first)
            clear_rows_stage(k, x_rows)
            norm_nodes_stage(k, a["x"])
            if stop(1, k.nT):
                return
            linear_attention_stage(k, a["L0_kv"], a["L0_q"])
            if stop(2, k.attT):
                return
            k.counts = k.sb("counts", [NT, TILES, TP], ctx=first)
            counts_stage(k, a["src"], a["dst"], a["dst_groups"])
            move_stage(k, "counts_kept", k.counts_dram[:, :, :], k.counts[:])
            aggregate_stage(k)
            if stop(3, k.nT):
                return
            k.xT = k.sb("x_first", [P, FC, TP], ctx=first)
            mix_project_stage(k, a["L0_out"], a["L0_bias"], a["xT"])
            move_stage(k, "x1_parked", x_park, k.xT[:])
        with ExitStack() as mid:
            k.xT = k.sb("x_mid", [P, FC, TP], ctx=mid)
            move_stage(k, "x1_back", k.xT[:], x_park)
            if stop(4, k.xT):
                return
            norm_stage(k, "ln1")
            if stop(5, k.nT):
                return
            router_stage(k, "r0", 8, a["L0_router_w"], a["L0_router_b"], True, comb0, NB0)
            scatter_stage(k, "s0", x_rows)
            block_stage(k, "e0", NB0, 8, a["L0_experts"], x_rows, y_rows0, False)
            combine_stage(k, "c0", y_rows0)
            routed_bias_stage(k, a["L0_expert_b"], comb0, 8)
            if stop(6, k.xT):
                return
            k.clear_sems()
            layer0.close()
            k.sem_ctx = layer1 = ctx.enter_context(ExitStack())
            norm_stage(k, "ln2")
            if stop(7, k.nT):
                return
            with ExitStack() as att:
                k.attT = k.sb("attT1", [P, FC, TP], ctx=att)
                flow_attention_stage(k, a["L1_qk"], a["L1_b_qk"], a["L1_v"], a["L1_b_v"])
                if stop(8, k.attT):
                    return
                flow_project_stage(k, a["L1_proj"], a["L1_b_proj"])
            if stop(9, k.xT):
                return
            move_stage(k, "x2_parked", x_park, k.xT[:])
        with ExitStack() as graph:
            k.counts = k.sb("counts1", [NT, TILES, TP], ctx=graph)
            move_stage(k, "counts_back", k.counts[:], k.counts_dram[:, :, :])
            graph_layer(k, "g1", 4, 512, a["L1_W1"], a["L1_att1"], a["L1_b1"], True, h1_dram)
            if STOP == 10:
                with ExitStack() as dbg:
                    d = k.sb("dbg", [P, FC, TP], ctx=dbg)
                    move_stage(k, "dbg_in", d[:], h1_dram[0:FC].rearrange("c p n -> p c n"))
                    store_stage(k, d, out_f)
                return
            k.clear_sems()
            layer1.close()
            k.sem_ctx = ctx.enter_context(ExitStack())
            project_wide_stage(k, a["L1_W2"], h1_dram)
            k.xT = k.sb("x_graph", [P, FC, TP], ctx=graph)
            move_stage(k, "x2_back", k.xT[:], x_park)
            graph_layer(k, "g2", 1, D, None, a["L1_att2"], a["L1_b2"], False)
            move_stage(k, "x3_parked", x_park, k.xT[:])
        k.xT = k.sb("x_last", [P, FC, TP])
        move_stage(k, "x3_back", k.xT[:], x_park)
        if stop(11, k.xT):
            return
        norm_stage(k, "ln3")
        router_stage(k, "r1", 16, a["L1_gate_w"], None, False, comb1, NB1)
        shared_expert_stage(k, a["L1_sw13"], a["L1_sw2"], 2)
        scatter_stage(k, "s1", x_rows)
        block_stage(k, "e1", NB1, 16, a["L1_experts"], x_rows, y_rows1, True)
        combine_stage(k, "c1", y_rows1)
        store_stage(k, k.xT, out_f)


def clear_rows_stage(k, rows_dram):
    nc = k.nc
    cleared, zeroed = k.sem("rows_clear"), k.sem("rows_zeroed")
    with nc.Block(no_gpsimd_drain=True) as block:
        @block.vector
        def _(dve):
            nc.vector.memset(k.attT[:, 0, 0:D], 0.0).then_inc(zeroed, 1)

        @block.sync
        def _(sp):
            sp.wait_ge(zeroed, 1)
            for b in range(NB1):
                sp.dma_start(rows_dram[b * P:(b + 1) * P, :], k.attT[:, 0, 0:D]).then_inc(cleared, 16)
            sp.wait_ge(cleared, 16 * NB1)


def move_stage(k, name, dst, src):
    moved = k.sem(name)
    with k.nc.Block(no_gpsimd_drain=True) as block:
        @block.sync
        def _(sp):
            sp.dma_start(dst, src).then_inc(moved, 16)
            sp.wait_ge(moved, 16)


def kernel(**inputs):
    import numpy as np
    import concourse.bacc as _bacc
    from concourse.bass_utils import run_bass_kernel_spmd as _run

    nc = _bacc.Bacc("TRN2", target_bir_lowering=False, num_devices=1)
    v = {n: np.asarray(x) for n, x in inputs.items()}

    def chunks(w):
        ni, no = w.shape[0] // P, w.shape[1] // P
        return w.reshape(ni, P, no, P).transpose(2, 1, 0, 3)

    def blocks(w, width):
        ni, nb = w.shape[0] // P, w.shape[1] // width
        return w.reshape(ni, P, nb, width).transpose(2, 1, 0, 3)

    def column(b):
        return b.reshape(-1, P).T

    def moving(w):
        e, ni, no = w.shape
        return w.reshape(e, ni // P, P, no).transpose(0, 2, 1, 3).reshape(e, P, -1)

    def pairs(w1, w3):
        e = w1.shape[0]
        return np.stack([w1, w3], 1).reshape(e, 2, 2, P, FC, P).transpose(0, 5, 2, 1, 4, 3)

    def halves(w):
        return w.reshape(2, 256, D)

    w13 = moving(np.concatenate([v["L1_ffn_w1"], v["L1_ffn_w3"]], 1).transpose(0, 2, 1))
    experts1 = np.concatenate([w13, moving(v["L1_ffn_w2"].transpose(0, 2, 1))], 2)
    host = {
        "x": v["x"], "xT": v["x"].T.reshape(FC, P, T).transpose(1, 0, 2),
        "src": v["src"].reshape(EC, NT).T, "dst": v["dst"].reshape(EC, NT).T, "dst_groups": v["dst"].reshape(EC // 4, 4 * NT),
        "L0_kv": blocks(v["L0_mix_w_qkv"][:, D:], HALF), "L0_q": chunks(v["L0_mix_w_qkv"][:, :D]),
        "L0_out": chunks(np.concatenate([v["L0_gnn_W"], v["L0_mix_w_proj"]], 0)),
        "L0_bias": np.stack([column(v["L0_gnn_b"]), column(v["L0_mix_b_proj"])]),
        "L0_router_w": v["L0_ffn_router_w"].T.reshape(FC, P, 8).transpose(1, 0, 2),
        "L0_router_b": v["L0_ffn_router_b"],
        "L0_experts": moving(v["L0_ffn_expert_w"].transpose(0, 2, 1)),
        "L0_expert_b": v["L0_ffn_expert_b"],
        "L1_qk": chunks(v["L1_mix_W_qkv"][:, :2 * D]), "L1_v": blocks(v["L1_mix_W_qkv"][:, 2 * D:], HALF),
        "L1_b_qk": column(v["L1_mix_b_qkv"][:2 * D]), "L1_b_v": v["L1_mix_b_qkv"][2 * D:],
        "L1_proj": chunks(v["L1_mix_W_proj"]), "L1_b_proj": column(v["L1_mix_b_proj"]),
        "L1_W1": blocks(v["L1_gnn_W1"], 512), "L1_att1": np.stack([v["L1_gnn_att_src1"], v["L1_gnn_att_dst1"]]),
        "L1_b1": column(v["L1_gnn_b1"]), "L1_W2": v["L1_gnn_W2"].reshape(16, P, D).transpose(1, 0, 2),
        "L1_att2": np.stack([v["L1_gnn_att_src2"], v["L1_gnn_att_dst2"]]), "L1_b2": column(v["L1_gnn_b2"]),
        "L1_gate_w": v["L1_ffn_gate_w"].T.reshape(FC, P, 16).transpose(1, 0, 2),
        "L1_sw13": pairs(halves(v["L1_ffn_sw1"]), halves(v["L1_ffn_sw3"])),
        "L1_sw2": halves(v["L1_ffn_sw2"].T).reshape(2, 2, P, D).transpose(0, 2, 1, 3),
        "L1_experts": experts1,
    }
    host = {n: np.ascontiguousarray(x) for n, x in host.items()}
    a = {n: nc.dram_tensor("in_" + n, x.shape, mybir.dt.from_np(x.dtype), kind="ExternalInput").ap() for n, x in host.items()}
    out = nc.dram_tensor("out_y", (D, T), F32, kind="ExternalOutput").ap()
    program(nc, a, out)
    r = _run(nc, [{"in_" + n: x for n, x in host.items()}], core_ids=[0])
    return np.ascontiguousarray(r.results[0]["out_y"].T)
```

```python
import concourse.bass as bass
from concourse import mybir
from contextlib import ExitStack

F32 = mybir.dt.float32
F16 = mybir.dt.float16
F32R = mybir.dt.float32r
BF16 = mybir.dt.bfloat16
I32 = mybir.dt.int32
I16 = mybir.dt.int16
U32 = mybir.dt.uint32
ACT = mybir.ActivationFunctionType
ALU = mybir.AluOpType
AX_X = mybir.AxisListType.X

P = 128
T = 1250
NT = 125
TILES = T // NT
CW = 418
CH = 3
TP = CW * CH
D = 768
FC = D // P
HALF = D // 2
EC = 160
EPS = 1e-5
GROUP = 2 * P
NG0 = (2 * T // GROUP + 8 + 1) // 2 * 2
NG1 = (2 * T // GROUP + 16 + 1) // 2 * 2
BIG = -1.0e30


class Chain:

    def __init__(self, eng, sem, start=0):
        self.eng, self.sem, self.n = eng, sem, start

    def step(self, ins):
        self.n = self.n + 1
        return ins.then_inc(self.sem, 1)

    def wait(self):
        self.eng.wait_ge(self.sem, self.n)

    def then(self, ins):
        self.step(ins)
        self.wait()


class Kit:

    def __init__(self, nc, ctx):
        self.nc, self.ctx, self.sems, self.sem_ctx = nc, ctx, [], ctx

    def sb(self, name, shape, dt=F32, ctx=None):
        return (ctx or self.ctx).enter_context(self.nc.sbuf_tensor(name, shape, dt))

    def sem(self, name):
        handle = self.sem_ctx.enter_context(self.nc.semaphore(name))
        self.sems.append(handle)
        return handle

    def soft_sem(self, name):
        return self.ctx.enter_context(self.nc.semaphore(name))

    def clear_sems(self):
        with self.nc.Block(no_gpsimd_drain=True) as block:
            @block.gpsimd
            def _(pool):
                for handle in self.sems:
                    pool.sem_clear(handle)
        self.sems = []


def cols(c):
    return slice(c * CW, (c + 1) * CW)


def tile_cols(t):
    return slice(t * NT, (t + 1) * NT)


def three_passes(nc, out, lhs, rhs, start, stop):
    for m, (a, b) in enumerate(((0, 0), (0, 1), (1, 0))):
        mm = nc.tensor.matmul(out, lhs[a], rhs[b], start=(start and m == 0), stop=(stop and m == 2))
    return mm


def ones_stage(k):
    nc = k.nc
    k.ident = k.sb("ident", [P, P])
    k.ones = k.sb("ones", [P, P])
    k.avg = k.sb("avg", [P, P])
    k.heads2 = k.sb("heads2", [P, P])
    k.index16 = k.sb("index16", [P, 16])
    made, zeroed = k.sem("const_made"), k.sem("const_zeroed")
    with nc.Block(no_gpsimd_drain=True) as block:
        @block.gpsimd
        def _(pool):
            nc.gpsimd.memset(k.ident[:], 0.0).then_inc(zeroed, 1)
            pool.wait_ge(zeroed, 1)
            nc.gpsimd.affine_select(out=k.ident[:], in_=k.ident[:], compare_op=ALU.not_equal, fill=1.0, base=0,
                                    pattern=[[-1, P]], channel_multiplier=1).then_inc(zeroed, 1)
            pool.wait_ge(zeroed, 2)
            nc.gpsimd.iota(k.index16[:], [[1, 16]], base=0, channel_multiplier=0,
                           allow_small_or_imprecise_dtypes=True).then_inc(zeroed, 1)

        @block.vector
        def _(dve):
            nc.vector.memset(k.heads2[:], 0.0).then_inc(made, 1)
            nc.vector.memset(k.ones[:], 1.0).then_inc(made, 1)
            nc.vector.memset(k.avg[:], 1.0 / D).then_inc(made, 1)
            dve.wait_ge(made, 1)
            nc.vector.memset(k.heads2[0:64, 0:64], 1.0).then_inc(made, 1)
            nc.vector.memset(k.heads2[64:128, 64:128], 1.0).then_inc(made, 1)


def norm_nodes_stage(k, x_dram):
    nc, ps = k.nc, k.ps
    loaded = [k.sem(f"x_loaded{g}") for g in range(2)]
    order, stats, rooted, normed = k.sem("ln0_order"), k.sem("ln0_var"), k.sem("ln0_std"), k.sem("ln0_normed")
    turned, copied = k.sem("ln0_turned"), k.sem("ln0_copied")
    with ExitStack() as ctx:
        six = k.sb("ln0_six", [NT, TILES, 12], ctx=ctx)
        mv = k.sb("ln0_mv", [NT, TILES, 2], ctx=ctx)
        rstd = k.sb("ln0_rstd", [NT, TILES], ctx=ctx)
        with nc.Block(no_gpsimd_drain=True) as block:
            @block.sync
            def _(sp):
                for g in range(2):
                    sp.dma_start(k.x_node[:, 5 * g:5 * g + 5, :],
                                 x_dram[625 * g:625 * g + 625, :].rearrange("(t p) d -> p t d", p=NT)).then_inc(loaded[g], 16)

            @block.vector
            def _(dve):
                ch = Chain(dve, order)
                ch.step(nc.vector.memset(k.nT[:, :, T:TP], 0.0))
                for t in range(TILES):
                    dve.wait_ge(loaded[t // 5], 16)
                    for h in range(2):
                        ch.step(nc.vector.bn_stats(six[:, t, 6 * h:6 * h + 6], k.x_node[:, t, h * HALF:(h + 1) * HALF]))
                ch.wait()
                for t in range(TILES):
                    ch.step(nc.vector.bn_aggr(mv[:, t, :], six[:, t, :]))
                ch.wait()
                nc.vector.tensor_scalar(rstd[:], mv[:, :, 1], EPS, None, ALU.add).then_inc(stats, 1)
                dve.wait_ge(rooted, 1)
                ch.then(nc.vector.reciprocal(rstd[:], rstd[:]))
                for t in range(TILES):
                    nc.vector.tensor_scalar(k.x_node[:, t, :], k.x_node[:, t, :], mv[:, t, 0:1], rstd[:, t:t + 1],
                                            ALU.subtract, ALU.mult).then_inc(normed, 1)

            @block.tensor
            def _(pe):
                for c in range(FC):
                    if c >= 2:
                        pe.wait_ge(copied, c - 1)
                    for t in range(TILES):
                        if c == 0:
                            pe.wait_ge(normed, t + 1)
                        mm = nc.tensor.transpose(ps[:, 3 * (c % 2) + t // 4, NT * (t % 4):NT * (t % 4) + NT],
                                                 k.x_node[:, t, P * c:P * c + P], k.ident[0:NT, 0:NT])
                    mm.then_inc(turned, 1)

            @block.scalar
            def _(act):
                act.wait_ge(stats, 1)
                nc.scalar.activation(rstd[:], rstd[:], ACT.Sqrt).then_inc(rooted, 1)
                for c in range(FC):
                    g = 3 * (c % 2)
                    act.wait_ge(turned, c + 1)
                    nc.scalar.activation(k.nT[:, c, 0:8 * NT].rearrange("p (b n) -> p b n", b=2), ps[:, g:g + 2, 0:4 * NT], ACT.Copy)
                    nc.scalar.activation(k.nT[:, c, 8 * NT:T], ps[:, g + 2, 0:2 * NT], ACT.Copy).then_inc(copied, 1)


def linear_attention_stage(k, w_kv, w_q, rows_dram):
    nc, ps = k.nc, k.ps
    wl = [k.sem(f"la_weights{h}") for h in range(2)]
    cleared, zeroed = k.sem("rows_cleared"), k.sem("la_zeroed")
    blocks = rows_dram.rearrange("(b p) n -> p b n", p=P)
    kv_done, kv_low, kv_exp, kv_out = k.sem("la_kv_done"), k.sem("la_kv_low"), k.sem("la_kv_exp"), k.sem("la_kv_out")
    with ExitStack() as ctx:
        kv = k.sb("la_kv", [NT, TILES, 2 * D], ctx=ctx)
        kvb = k.sb("la_kvb", [P, FC, 2 * P], ctx=ctx)
        wk = k.sb("la_w", [P, 2, FC, HALF], ctx=ctx)
        low = k.sb("la_low", [NT, 2, HALF], ctx=ctx)
        zeros = k.attT[:].rearrange("p f n -> p (f n)")[:, 0:4 * D].rearrange("p (b n) -> p b n", b=4)
        with nc.Block(no_gpsimd_drain=True) as block:
            @block.sync
            def _(sp):
                for j in range(4):
                    if j >= 2:
                        sp.wait_ge(kv_done, TILES * (j - 1))
                    sp.dma_start(wk[:, j % 2, :, :], w_kv[j]).then_inc(wl[j % 2], 16)

            @block.tensor
            def _(pe):
                for j in range(4):
                    pe.wait_ge(wl[j % 2], 16 * (j // 2 + 1))
                    for t in range(TILES):
                        n = j * TILES + t
                        if n >= 8:
                            pe.wait_ge(kv_out, n - 7)
                        for c in range(FC):
                            mm = nc.tensor.matmul(ps[0:NT, n % 8, 0:HALF], k.nT[:, c, tile_cols(t)], wk[:, j % 2, c, :],
                                                  start=(c == 0), stop=(c == FC - 1))
                        mm.then_inc(kv_done, 1)

            @block.vector
            def _(dve):
                nc.vector.memset(zeros, 0.0).then_inc(zeroed, 1)
                for n in range(2 * TILES):
                    j, t = n // TILES, n % TILES
                    dve.wait_ge(kv_done, n + 1)
                    if n >= 2:
                        dve.wait_ge(kv_out, n - 1)
                    nc.vector.tensor_scalar(low[:, n % 2, :], ps[0:NT, n % 8, 0:HALF], 0.0, None, ALU.min).then_inc(kv_low, 1)
                    dve.wait_ge(kv_exp, n + 1)
                    nc.vector.scalar_tensor_tensor(out=kv[:, t, HALF * j:HALF * j + HALF], in0=ps[0:NT, n % 8, 0:HALF], scalar=0.0,
                                                   in1=low[:, n % 2, :], op0=ALU.max, op1=ALU.add).then_inc(kv_out, 1)
                for n in range(2 * TILES, 4 * TILES):
                    j, t = n // TILES, n % TILES
                    dve.wait_ge(kv_done, n + 1)
                    nc.vector.tensor_copy(kv[:, t, HALF * j:HALF * j + HALF], ps[0:NT, n % 8, 0:HALF]).then_inc(kv_out, 1)

            @block.scalar
            def _(act):
                act.wait_ge(zeroed, 1)
                for n in range(2 * TILES):
                    act.wait_ge(kv_low, n + 1)
                    nc.scalar.activation(low[:, n % 2, :], low[:, n % 2, :], ACT.Exp).then_inc(kv_exp, 1)
                    if n < NG1 // 2:
                        act.dma_start(blocks[:, 4 * n:4 * n + 4, :], zeros).then_inc(cleared, 16)
                act.wait_ge(cleared, 16 * (NG1 // 2))

        state, masked = k.sem("la_state"), k.sem("la_masked")
        with nc.Block(no_gpsimd_drain=True) as block:
            @block.tensor
            def _(pe):
                for p in range(FC):
                    for t in range(TILES):
                        nc.tensor.matmul(ps[:, p, 0:P], kv[:, t, P * p:P * p + P], kv[:, t, D + P * p:D + P * p + P],
                                         start=(t == 0), stop=(t == TILES - 1))
                    for t in range(TILES):
                        mm = nc.tensor.matmul(ps[:, p, P:2 * P], kv[:, t, P * p:P * p + P], k.ones[0:NT, :],
                                              start=(t == 0), stop=(t == TILES - 1))
                    mm.then_inc(state, 1)

            @block.vector
            def _(dve):
                for p in range(FC):
                    dve.wait_ge(state, p + 1)
                    for h in range(2):
                        nc.vector.tensor_tensor(kvb[:, p, h * P:h * P + P], ps[:, p, h * P:h * P + P], k.heads2[:],
                                                ALU.mult).then_inc(masked, 1)

        wq = wk[:, :, 0:2, :].rearrange("p s a (b n) -> p s (a b) n", b=3)
        q_in = [k.sem(f"la_qweights{h}") for h in range(2)]
        q_done, q_low, q_exp, q_out = k.sem("la_q_done"), k.sem("la_q_low"), k.sem("la_q_exp"), k.sem("la_q_out")
        nd_done, inverted, nd_out = k.sem("la_numden"), k.sem("la_inverted"), k.sem("la_out")
        with ExitStack() as ctx2:
            q = k.sb("la_q", [P, 2, TP], ctx=ctx2)
            qlow = k.sb("la_qlow", [P, TP], ctx=ctx2)
            rec = k.sb("la_rec", [P, 2, CW], ctx=ctx2)
            with nc.Block(no_gpsimd_drain=True) as block:
                @block.sync
                def _(sp):
                    for p in range(FC):
                        if p >= 2:
                            sp.wait_ge(q_done, p - 1)
                        sp.dma_start(wq[:, p % 2], w_q[p]).then_inc(q_in[p % 2], 16)

                @block.tensor
                def _(pe):
                    for p in range(FC + 1):
                        if p < FC:
                            pe.wait_ge(q_in[p % 2], 16 * (p // 2 + 1))
                            if p >= 1:
                                pe.wait_ge(q_out, p)
                            for c in range(CH):
                                for f in range(FC):
                                    mm = nc.tensor.matmul(ps[:, c, 0:CW], wq[:, p % 2, f, :], k.nT[:, f, cols(c)],
                                                          start=(f == 0), stop=(f == FC - 1))
                            mm.then_inc(q_done, 1)
                        if p >= 1:
                            pe.wait_ge(q_out, p)
                            for c in range(CH):
                                n = (p - 1) * CH + c
                                if n >= 2:
                                    pe.wait_ge(nd_out, n - 1)
                                for h in range(2):
                                    mm = nc.tensor.matmul(ps[:, 3 + 2 * h + n % 2, 0:CW], kvb[:, p - 1, h * P:h * P + P],
                                                          q[:, (p - 1) % 2, cols(c)], start=True, stop=True)
                                mm.then_inc(nd_done, 1)

                @block.vector
                def _(dve):
                    for p in range(FC + 1):
                        if p < FC:
                            dve.wait_ge(q_done, p + 1)
                            if p >= 1:
                                dve.wait_ge(q_out, p)
                            nc.vector.tensor_scalar(qlow[:].rearrange("p (c n) -> p c n", c=CH), ps[:, 0:CH, 0:CW], 0.0, None,
                                                    ALU.min).then_inc(q_low, 1)
                            dve.wait_ge(q_exp, p + 1)
                            if p >= 2:
                                dve.wait_ge(nd_done, CH * (p - 1))
                            nc.vector.scalar_tensor_tensor(out=q[:, p % 2, :].rearrange("p (c n) -> p c n", c=CH),
                                                           in0=ps[:, 0:CH, 0:CW], scalar=0.0,
                                                           in1=qlow[:].rearrange("p (c n) -> p c n", c=CH),
                                                           op0=ALU.max, op1=ALU.add).then_inc(q_out, 1)
                        if p >= 1:
                            for c in range(CH):
                                n = (p - 1) * CH + c
                                dve.wait_ge(nd_done, n + 1)
                                if n >= 2:
                                    dve.wait_ge(nd_out, n - 1)
                                nc.vector.reciprocal(rec[:, n % 2, :], ps[:, 5 + n % 2, 0:CW]).then_inc(inverted, 1)
                                dve.wait_ge(inverted, n + 1)
                                nc.vector.tensor_tensor(k.attT[:, p - 1, cols(c)], ps[:, 3 + n % 2, 0:CW], rec[:, n % 2, :],
                                                        ALU.mult).then_inc(nd_out, 1)

                @block.scalar
                def _(act):
                    for p in range(FC):
                        act.wait_ge(q_low, p + 1)
                        nc.scalar.activation(qlow[:], qlow[:], ACT.Exp).then_inc(q_exp, 1)


def counts_stage(k, src_dram, dst_dram, dst_groups_dram):
    nc, ps = k.nc, k.ps
    U = 4
    NG = EC // U
    PASSES = TILES // 2
    SPAN = 2 * NT
    e_in, e_f, row, g_in = k.sem("edges_in"), k.sem("edges_float"), k.sem("index_row"), k.sem("groups_in")
    order, ext, laid, bounds = k.sem("range_order"), k.sem("range_extrema"), k.sem("range_row"), k.sem("range_found")
    hot, free = [k.sem(f"onehot_made{g}") for g in range(PASSES)], [k.sem(f"onehot_free{g}") for g in range(PASSES)]
    fin, staged, diag, summed = k.sem("counts_done"), k.sem("counts_staged"), k.sem("counts_diag"), k.sem("counts_summed")
    turned, placed, far_out = k.sem("counts_turned"), k.sem("counts_placed"), [k.sem(f"far_stored{h}") for h in range(2)]
    with ExitStack() as ctx:
        ei = k.sb("edge_int", [NT, 2, EC], I32, ctx=ctx)
        ef = k.sb("edge_float", [NT, 2, EC], F32, ctx=ctx)
        gi = k.sb("group_int", [NG, U * NT], I32, ctx=ctx)
        ge = k.sb("group_extrema", [NG, 2], F32, ctx=ctx)
        gf = k.sb("group_float", [NG, U * NT], F32, ctx=ctx)
        gx = k.sb("group_index", [1, NG], F32, ctx=ctx)
        rg = k.sb("group_rows", [1, 4, NG], F32, ctx=ctx)
        ac = k.sb("group_active", [1, 3, PASSES, NG], F32, ctx=ctx)
        lim = k.sb("pass_limits", [1, 2, PASSES], F32, ctx=ctx)
        limi = k.sb("pass_limits_int", [1, 2, PASSES], I32, ctx=ctx)
        idx = k.sb("index_row", [NT, TP], F16, ctx=ctx)
        zero = k.sb("zero_weights", [NT, NT], F16, ctx=ctx)
        hs = k.sb("hot_src", [NT, U, TP], F16, ctx=ctx)
        hd = k.sb("hot_dst", [NT, U, SPAN], F16, ctx=ctx)
        st = k.sb("counts_rows", [NT, 2, TP], F32, ctx=ctx)
        far = k.sb("far_rows", [NT, TP], BF16, ctx=ctx)
        with nc.Block(no_gpsimd_drain=True) as block:
            @block.sync
            def _(sp):
                sp.dma_start(gi[:], dst_groups_dram).then_inc(g_in, 16)
                sp.dma_start(ei[:, 0, :], src_dram).then_inc(e_in, 16)
                sp.dma_start(ei[:, 1, :], dst_dram).then_inc(e_in, 16)
                for t in range(TILES):
                    sp.wait_ge(summed, 2 * t + 2)
                    sp.dma_start(k.far_dram[t], far[:, 0:T]).then_inc(far_out[t % 2], 16)
                for h in range(2):
                    sp.wait_ge(far_out[h], 16 * (TILES // 2))

            @block.gpsimd
            def _(pool):
                nc.gpsimd.memset(zero[:], 0.0).then_inc(row, 1)
                nc.gpsimd.iota(idx[:], [[1, TP]], base=0, channel_multiplier=0,
                               allow_small_or_imprecise_dtypes=True).then_inc(row, 1)
                pool.wait_ge(row, 2)
                nc.gpsimd.iota(gx[:], [[1, NG]], base=0, channel_multiplier=0,
                               allow_small_or_imprecise_dtypes=True).then_inc(row, 1)

            @block.vector
            def _(dve):
                ch = Chain(dve, order)
                nc.vector.memset(k.counts[:, :, T:TP], 0.0)
                dve.wait_ge(g_in, 16)
                ch.then(nc.vector.tensor_copy(gf[:], gi[:]))
                nc.vector.tensor_reduce(ge[:, 0:1], gf[:], AX_X, ALU.min).then_inc(ext, 1)
                nc.vector.tensor_reduce(ge[:, 1:2], gf[:], AX_X, ALU.max).then_inc(ext, 1)
                dve.wait_ge(e_in, 32)
                nc.vector.tensor_copy(ef[:], ei[:]).then_inc(e_f, 1)
                dve.wait_ge(row, 3)
                ch.step(nc.vector.tensor_scalar(rg[:, 2, :], gx[:], -64.0, None, ALU.add))
                ch.step(nc.vector.tensor_scalar(rg[:, 3, :], gx[:], 1.0, None, ALU.add))
                dve.wait_ge(laid, 1)
                ch.then(nc.vector.tensor_copy(rg[:, 0:2, :], ps[0:1, 7, 0:2 * NG].rearrange("p (a n) -> p a n", a=2)))
                for g in range(PASSES):
                    ch.step(nc.vector.tensor_scalar(ac[:, 0, g, :], rg[:, 1, :], float(SPAN * g), None, ALU.is_ge))
                ch.wait()
                for g in range(PASSES):
                    ch.step(nc.vector.scalar_tensor_tensor(out=ac[:, 1, g, :], in0=rg[:, 0, :], scalar=float(SPAN * (g + 1)),
                                                           in1=ac[:, 0, g, :], op0=ALU.is_lt, op1=ALU.mult))
                ch.wait()
                for g in range(PASSES):
                    ch.step(nc.vector.tensor_tensor(ac[:, 2, g, :], ac[:, 1, g, :], rg[:, 2, :], ALU.mult))
                    ch.step(nc.vector.tensor_tensor(ac[:, 0, g, :], ac[:, 1, g, :], rg[:, 3, :], ALU.mult))
                ch.wait()
                ch.step(nc.vector.tensor_reduce(lim[:, 0, :], ac[:, 2], AX_X, ALU.min))
                ch.then(nc.vector.tensor_reduce(lim[:, 1, :], ac[:, 0], AX_X, ALU.max))
                ch.then(nc.vector.tensor_scalar(lim[:, 0, :], lim[:, 0, :], 64.0, float(NG - 1), ALU.add, ALU.min))
                ch.then(nc.vector.tensor_tensor(lim[:, 1, :], lim[:, 1, :], lim[:, 0, :], ALU.subtract))
                ch.then(nc.vector.tensor_scalar(lim[:, 1, :], lim[:, 1, :], 1.0, None, ALU.max))
                nc.vector.tensor_copy(limi[:], lim[:]).then_inc(bounds, 1)
                dve.wait_ge(bounds, 1)
                dve.wait_ge(e_f, 1)

                def make(g, first, i):
                    for u in range(U):
                        e = nc.s_assert_within((first + i) * U + u, 0, EC - 1,
                                               skip_runtime_bounds_check_because="first + groups is at most NG")
                        dve.wait_ge(free[g], i * U + u + 1)
                        nc.vector.tensor_scalar(hs[:, u, :], idx[:], ef[:, 0, bass.ds(e, 1)], None, ALU.is_equal)
                        nc.vector.tensor_scalar(hd[:, u, :], idx[:, SPAN * g:SPAN * (g + 1)], ef[:, 1, bass.ds(e, 1)],
                                                None, ALU.is_equal).then_inc(hot[g], 1)

                for g in range(PASSES):
                    first = dve.value_load(limi[0:1, 0, g:g + 1], min_val=0, max_val=NG - 1)
                    groups = dve.value_load(limi[0:1, 1, g:g + 1], min_val=1, max_val=NG)
                    with dve.Fori(0, groups) as i:
                        make(g, first, i)
                    for h in range(2):
                        t = 2 * g + h
                        dve.wait_ge(staged, t + 1)
                        nc.vector.tensor_tensor(st[:, h, tile_cols(t)], st[:, h, tile_cols(t)], k.ident[0:NT, 0:NT],
                                                ALU.add).then_inc(diag, 1)
                        dve.wait_ge(diag, t + 1)
                        if t >= 1:
                            dve.wait_ge(far_out[(t - 1) % 2], 16 * ((t - 1) // 2 + 1))
                        nc.vector.tensor_reduce(k.dinv[:, t:t + 1], st[:, h, 0:T], AX_X, ALU.add).then_inc(summed, 1)
                        nc.vector.tensor_scalar(far[:], st[:, h, :], 0.0, BIG, ALU.is_equal, ALU.mult).then_inc(summed, 1)

            @block.tensor
            def _(pe):
                pe.wait_ge(ext, 2)
                for j in range(2):
                    mm = nc.tensor.matmul(ps[0:1, 7, NG * j:NG * j + NG], ge[:, j:j + 1], k.ident[0:NG, 0:NG], start=True, stop=True)
                mm.then_inc(laid, 1)
                pe.wait_ge(row, 2)
                pe.wait_ge(bounds, 1)
                for g in range(PASSES):
                    groups = pe.value_load(limi[0:1, 1, g:g + 1], min_val=1, max_val=NG)
                    if g >= 1:
                        pe.wait_ge(staged, 2 * g)
                    for h in range(2):
                        for c in range(CH):
                            mm = nc.tensor.matmul(ps[0:NT, 3 * h + c, 0:CW], zero[:], idx[:, cols(c)], start=True, stop=False,
                                                  skip_group_check=True)
                            if 3 * h + c < U:
                                mm.then_inc(free[g], 1)
                    with pe.Fori(0, groups) as i:
                        for u in range(U):
                            pe.wait_ge(hot[g], i * U + u + 1)
                            for h in range(2):
                                for c in range(CH):
                                    mm = nc.tensor.matmul(ps[0:NT, 3 * h + c, 0:CW], hd[:, u, h * NT:(h + 1) * NT],
                                                          hs[:, u, cols(c)], start=False, stop=False, skip_group_check=True)
                            mm.then_inc(free[g], 1)
                    for h in range(2):
                        for c in range(CH):
                            mm = nc.tensor.matmul(ps[0:NT, 3 * h + c, 0:CW], zero[:], idx[:, cols(c)], start=False, stop=True,
                                                  skip_group_check=True)
                    mm.then_inc(fin, 1)
                    for h in range(2):
                        t = 2 * g + h
                        pe.wait_ge(diag, t + 1)
                        for q in range(3):
                            n = 3 * t + q
                            if n >= 2:
                                pe.wait_ge(placed, n - 1)
                            for s in range(4 * q, min(4 * q + 4, TILES)):
                                mm = nc.tensor.transpose(ps[0:NT, 6 + n % 2, NT * (s % 4):NT * (s % 4) + NT],
                                                         st[:, h, tile_cols(s)], k.ident[0:NT, 0:NT])
                            mm.then_inc(turned, 1)

            @block.scalar
            def _(act):
                for g in range(PASSES):
                    act.wait_ge(fin, g + 1)
                    for h in range(2):
                        t = 2 * g + h
                        if g >= 1:
                            act.wait_ge(summed, 2 * (t - 1))
                        nc.scalar.activation(st[:, h, :].rearrange("p (c n) -> p c n", c=CH), ps[0:NT, 3 * h:3 * h + CH, 0:CW],
                                             ACT.Copy).then_inc(staged, 1)
                    for h in range(2):
                        t = 2 * g + h
                        for q in range(3):
                            n = 3 * t + q
                            m = min(4, TILES - 4 * q)
                            act.wait_ge(turned, n + 1)
                            nc.scalar.activation(k.counts[:, 4 * q:4 * q + m, tile_cols(t)],
                                                 ps[0:NT, 6 + n % 2, 0:m * NT].rearrange("p (s n) -> p s n", s=m),
                                                 ACT.Copy).then_inc(placed, 1)


def aggregate_stage(k):
    nc, ps = k.nc, k.ps
    rooted, inv, scaled, dg = k.sem("deg_root"), k.sem("deg_inverse"), k.sem("agg_scaled"), k.sem("agg_diag")
    rowd, rows_out, done, out = k.sem("agg_row"), k.sem("agg_row_out"), k.sem("agg_done"), k.sem("agg_out")
    cast, kept = k.sem("counts_cast"), k.sem("counts_kept")
    with ExitStack() as ctx:
        dg_sb = k.sb("agg_diag", [NT, TILES, NT], ctx=ctx)
        dinvb = k.sb("dinv_rows", [P, TP], ctx=ctx)
        whole = k.sb("counts_int", [NT, TILES, TP], I16, ctx=ctx)
        with nc.Block(no_gpsimd_drain=True) as block:
            @block.scalar
            def _(act):
                nc.scalar.activation(k.dinv[:], k.dinv[:], ACT.Sqrt).then_inc(rooted, 1)
                act.wait_ge(rowd, 1)
                nc.scalar.activation(dinvb[:, 0:1000].rearrange("p (b n) -> p b n", b=2), ps[:, 6:8, 0:500], ACT.Copy)
                nc.scalar.activation(dinvb[:, 1000:T], ps[:, 5, 0:250], ACT.Copy).then_inc(rows_out, 1)
                for t in range(TILES):
                    nc.scalar.activation(whole[:, t, :], k.counts[:, t, :], ACT.Copy).then_inc(cast, 1)

            @block.sync
            def _(sp):
                sp.wait_ge(cast, TILES)
                sp.dma_start(k.counts_dram[:, :, :], whole[:]).then_inc(kept, 16)
                sp.wait_ge(kept, 16)

            @block.vector
            def _(dve):
                nc.vector.memset(dinvb[:, T:TP], 0.0)
                dve.wait_ge(rooted, 1)
                nc.vector.reciprocal(k.dinv[:], k.dinv[:]).then_inc(inv, 1)
                dve.wait_ge(inv, 1)
                for t in range(TILES):
                    nc.vector.tensor_scalar(k.x_node[:, t, :], k.x_node[:, t, :], k.dinv[:, t:t + 1], None,
                                            ALU.mult).then_inc(scaled, 1)
                for t in range(TILES):
                    nc.vector.tensor_scalar(dg_sb[:, t, :], k.ident[0:NT, 0:NT], k.dinv[:, t:t + 1], None, ALU.mult).then_inc(dg, 1)
                dve.wait_ge(rows_out, 1)
                for f in range(FC):
                    dve.wait_ge(done, f + 1)
                    g = 3 * (f % 2) if f else 0
                    nc.vector.tensor_tensor(k.nT[:, f, :].rearrange("p (c n) -> p c n", c=CH), ps[:, g:g + CH, 0:CW],
                                            dinvb[:].rearrange("p (c n) -> p c n", c=CH), ALU.mult).then_inc(out, 1)

            @block.tensor
            def _(pe):
                pe.wait_ge(dg, TILES)
                for t in range(TILES):
                    b = (6, 7, 5)[t // 4]
                    mm = nc.tensor.matmul(ps[:, b, NT * (t % 4):NT * (t % 4) + NT], k.ones[0:NT, :], dg_sb[:, t, :],
                                          start=True, stop=True)
                mm.then_inc(rowd, 1)
                pe.wait_ge(scaled, TILES)
                for f in range(FC):
                    if f == 1:
                        pe.wait_ge(rows_out, 1)
                    if f >= 2:
                        pe.wait_ge(out, f - 1)
                    for t in range(TILES):
                        for c in range(CH):
                            mm = nc.tensor.matmul(ps[:, 3 * (f % 2) + c, 0:CW], k.x_node[:, t, P * f:P * f + P],
                                                  k.counts[:, t, cols(c)], start=(t == 0), stop=(t == TILES - 1))
                    mm.then_inc(done, 1)


def project_stage(k, name, ins, parted, w_dram, loads, prepare, vector_out, scalar_out=None):
    nc, ps = k.nc, k.ps
    nk = sum(n for _, n in ins)
    chunks = [src[:, f, :] for src, m in ins for f in range(m)]
    wl = [k.sem(f"{name}_weights{h}") for h in range(2)]
    done, out = k.sem(f"{name}_done"), k.sem(f"{name}_out")
    high, split, w_high, w_split = (k.sem(f"{name}_{n}") for n in ("high", "split", "w_high", "w_split"))
    with ExitStack() as ctx:
        w = k.sb(f"{name}_w", [P, 2, nk, P], ctx=ctx)
        whi = k.sb(f"{name}_w_hi", [P, 2, nk, P], F32R, ctx=ctx)
        wlo = k.sb(f"{name}_w_lo", [P, 2, nk, P], F32R, ctx=ctx)
        hi = k.sb(f"{name}_hi", [P, parted, TP], F32R, ctx=ctx)
        lo = k.sb(f"{name}_lo", [P, parted, TP], F32R, ctx=ctx)

        def banks(o):
            return ps[:, 3 * (o % 2):3 * (o % 2) + CH, 0:CW]

        with nc.Block(no_gpsimd_drain=True) as block:
            @block.sync
            def _(sp):
                for o in range(FC):
                    if o >= 2:
                        sp.wait_ge(w_split, o - 1)
                        if parted < nk:
                            sp.wait_ge(done, o - 1)
                    sp.dma_start(w[:, o % 2], w_dram[o]).then_inc(wl[o % 2], 16)
                    if o == 1:
                        loads(sp)

            @block.tensor
            def _(pe):
                for o in range(FC):
                    pe.wait_ge(w_split, o + 1)
                    if o >= 2:
                        pe.wait_ge(out, o - 1)
                    for n in range(nk):
                        if n < parted:
                            if o == 0:
                                pe.wait_ge(split, n + 1)
                            passes = ((whi, hi[:, n, :]), (wlo, hi[:, n, :]), (whi, lo[:, n, :]))
                        else:
                            passes = ((w, chunks[n]),)
                        for m, (a, b) in enumerate(passes):
                            for c in range(CH):
                                mm = nc.tensor.matmul(banks(o)[:, c, :], a[:, o % 2, n, :], b[:, cols(c)],
                                                      start=(n == 0 and m == 0), stop=(n == nk - 1 and m == len(passes) - 1))
                    mm.then_inc(done, 1)

            @block.scalar
            def _(act):
                def weights_high(o):
                    act.wait_ge(wl[o % 2], 16 * (o // 2 + 1))
                    if o >= 2:
                        act.wait_ge(done, o - 1)
                    nc.scalar.activation(whi[:, o % 2], w[:, o % 2], ACT.Copy).then_inc(w_high, 1)
                for n in range(parted):
                    nc.scalar.activation(hi[:, n, :], chunks[n], ACT.Copy).then_inc(high, 1)
                    if n < 2:
                        weights_high(n)
                for o in range(FC):
                    if scalar_out:
                        scalar_out(act, o, banks(o), done, out)
                    if o + 2 < FC:
                        weights_high(o + 2)

            @block.vector
            def _(dve):
                def weights_low(o):
                    dve.wait_ge(w_high, o + 1)
                    nc.vector.tensor_tensor(wlo[:, o % 2], w[:, o % 2], whi[:, o % 2].bitcast(F32), ALU.subtract).then_inc(w_split, 1)
                for n in range(parted):
                    dve.wait_ge(high, n + 1)
                    nc.vector.tensor_tensor(lo[:, n, :], chunks[n], hi[:, n, :].bitcast(F32), ALU.subtract).then_inc(split, 1)
                    if n < 2:
                        weights_low(n)
                prepare(dve)
                for o in range(FC):
                    vector_out(dve, o, banks(o), done, out)
                    if o + 2 < FC:
                        weights_low(o + 2)


def mix_project_stage(k, w_dram, bias_dram, x_dram):
    nc = k.nc
    x_in, b_in, badd = k.sem("x1_x"), k.sem("x1_bias"), k.sem("x1_bias_sum")
    with ExitStack() as ctx:
        bias = k.sb("x1_bias", [P, 2, FC], ctx=ctx)

        def loads(sp):
            for j in range(2):
                sp.dma_start(bias[:, j, :], bias_dram[j]).then_inc(b_in, 16)
            sp.dma_start(k.xT[:, :, 0:T], x_dram).then_inc(x_in, 16)

        def prepare(dve):
            nc.vector.memset(k.xT[:, :, T:TP], 0.0).then_inc(badd, 1)
            dve.wait_ge(b_in, 32)
            nc.vector.tensor_tensor(bias[:, 0, :], bias[:, 0, :], bias[:, 1, :], ALU.add).then_inc(badd, 1)
            dve.wait_ge(badd, 2)
            dve.wait_ge(x_in, 16)

        def chunk_out(dve, o, banks, done, out):
            dve.wait_ge(done, o + 1)
            xo = k.xT[:, o, :].rearrange("p (c n) -> p c n", c=CH)
            nc.vector.scalar_tensor_tensor(out=xo, in0=banks, scalar=bias[:, 0, o:o + 1], in1=xo,
                                           op0=ALU.add, op1=ALU.add).then_inc(out, 1)
        project_stage(k, "x1", [(k.nT, FC), (k.attT, FC)], FC + 2, w_dram, loads, prepare, chunk_out)


def norm_stage(k, name):
    nc, ps = k.nc, k.ps
    mean, cen, sq, var, eps, root, rec = (k.sem(f"{name}_{x}") for x in
                                          ("mean", "centred", "squared", "var", "eps", "root", "inverse"))
    with ExitStack() as ctx:
        s = k.sb(f"{name}_sq", [P, 2, TP], ctx=ctx)
        r = k.sb(f"{name}_r", [P, TP], ctx=ctx)
        r3 = r[:].rearrange("p (c n) -> p c n", c=CH)
        with nc.Block(no_gpsimd_drain=True) as block:
            @block.tensor
            def _(pe):
                for f in range(FC):
                    for c in range(CH):
                        mm = nc.tensor.matmul(ps[:, c, 0:CW], k.avg[:], k.xT[:, f, cols(c)], start=(f == 0), stop=(f == FC - 1))
                mm.then_inc(mean, 1)
                for f in range(FC):
                    pe.wait_ge(sq, f + 1)
                    for c in range(CH):
                        mm = nc.tensor.matmul(ps[:, 3 + c, 0:CW], k.avg[:], s[:, f % 2, cols(c)], start=(f == 0), stop=(f == FC - 1))
                    mm.then_inc(var, 1)

            @block.vector
            def _(dve):
                dve.wait_ge(mean, 1)
                for f in range(FC):
                    nc.vector.tensor_tensor(k.nT[:, f, :].rearrange("p (c n) -> p c n", c=CH),
                                            k.xT[:, f, :].rearrange("p (c n) -> p c n", c=CH), ps[:, 0:CH, 0:CW],
                                            ALU.subtract).then_inc(cen, 1)
                dve.wait_ge(var, FC)
                nc.vector.tensor_scalar(r3, ps[:, 3:6, 0:CW], EPS, None, ALU.add).then_inc(eps, 1)
                dve.wait_ge(root, 1)
                nc.vector.reciprocal(r[:], r[:]).then_inc(rec, 1)
                dve.wait_ge(rec, 1)
                for f in range(FC):
                    nc.vector.tensor_tensor(k.nT[:, f, :], k.nT[:, f, :], r[:], ALU.mult)

            @block.scalar
            def _(act):
                for f in range(FC):
                    act.wait_ge(cen, f + 1)
                    if f >= 2:
                        act.wait_ge(var, f - 1)
                    nc.scalar.activation(s[:, f % 2, :], k.nT[:, f, :], ACT.Square).then_inc(sq, 1)
                act.wait_ge(eps, 1)
                nc.scalar.activation(r[:], r[:], ACT.Sqrt).then_inc(root, 1)


def router_stage(k, name, E, rw_dram, rb_dram, renormalise, comb_dram, NG):
    nc, ps = k.nc, k.ps
    w_in, b_in, done, order, ex, turned, laid, stored = (k.sem(f"{name}_{x}") for x in (
        "w_in", "b_in", "scores", "order", "exp", "turned", "laid", "stored"))
    b0, cum, counted, consts = (k.sem(f"{name}_{x}") for x in ("neg", "one_hot", "counted", "consts"))
    with ExitStack() as ctx:
        w = k.sb(f"{name}_w", [P, FC, E], ctx=ctx)
        rb = k.sb(f"{name}_b", [NT, E], ctx=ctx)
        sc = k.sb(f"{name}_sc", [NT, TILES, E], ctx=ctx)
        ex_sb = k.sb(f"{name}_ex", [NT, TILES, E], ctx=ctx)
        top = k.sb(f"{name}_top", [NT, TILES, 8], ctx=ctx)
        idx = k.sb(f"{name}_idx", [NT, TILES, 8], U32, ctx=ctx)
        idf = k.sb(f"{name}_idf", [NT, TILES, 8], ctx=ctx)
        tmp = k.sb(f"{name}_tmp", [NT, 6, TILES], ctx=ctx)
        pr = k.sb(f"{name}_pr", [NT, TILES, 2], ctx=ctx)
        comb = k.sb(f"{name}_comb", [NT, 2, TILES, E], ctx=ctx)
        combT = k.sb(f"{name}_combT", [E, TP], ctx=ctx)
        hot = k.sb(f"{name}_hot", [NT, 3, TILES, E], ctx=ctx)
        before = k.sb(f"{name}_before", [NT, NT], ctx=ctx)
        thr = k.sb(f"{name}_thr", [NT, TILES], ctx=ctx)
        bidx = k.sb(f"{name}_bidx", [NT, NG], ctx=ctx)
        pos = k.sb(f"{name}_pos", [NT, TILES, E], ctx=ctx)
        carry = k.sb(f"{name}_carry", [NT, TILES + 1, E], ctx=ctx)
        over = k.sb(f"{name}_over", [NT, E, TILES], ctx=ctx)
        start = k.sb(f"{name}_start", [NT, E + 1], ctx=ctx)
        nblk = k.sb(f"{name}_nblk", [NT, E], ctx=ctx)
        row = k.sb(f"{name}_row", [NT, 2, TILES], ctx=ctx)
        past = k.sb(f"{name}_past", [1, NG, E], ctx=ctx)
        bex = k.sb(f"{name}_bex", [1, NG], ctx=ctx)
        half = k.sb(f"{name}_half", [1, NG // 2], ctx=ctx)
        quads = k.sb(f"{name}_quads", [1, 1], ctx=ctx)
        with nc.Block(no_gpsimd_drain=True) as block:
            @block.sync
            def _(sp):
                sp.dma_start(w[:], rw_dram).then_inc(w_in, 16)
                if rb_dram is not None:
                    sp.dma_start(rb[:], rb_dram.partition_broadcast(NT)).then_inc(b_in, 16)
                if comb_dram is not None:
                    sp.wait_ge(laid, 1)
                    sp.dma_start(comb_dram[0:E, :], combT[:]).then_inc(stored, 16)
                    sp.wait_ge(stored, 16)

            @block.gpsimd
            def _(pool):
                nc.gpsimd.memset(before[:], 0.0).then_inc(consts, 1)
                pool.wait_ge(consts, 1)
                nc.gpsimd.affine_select(out=before[:], in_=before[:], compare_op=ALU.is_ge, fill=1.0, base=0,
                                        pattern=[[-1, NT]], channel_multiplier=1).then_inc(consts, 1)
                pool.wait_ge(consts, 2)
                nc.gpsimd.iota(thr[:], [[GROUP, TILES]], base=0, channel_multiplier=0,
                               allow_small_or_imprecise_dtypes=True).then_inc(consts, 1)
                pool.wait_ge(consts, 3)
                nc.gpsimd.iota(bidx[:], [[1, NG]], base=0, channel_multiplier=0,
                               allow_small_or_imprecise_dtypes=True).then_inc(consts, 1)

            @block.tensor
            def _(pe):
                pe.wait_ge(w_in, 16)
                for t in range(TILES):
                    for f in range(FC):
                        mm = nc.tensor.matmul(ps[0:NT, 0, E * t:E * t + E], k.nT[:, f, tile_cols(t)], w[:, f, :],
                                              start=(f == 0), stop=(f == FC - 1))
                mm.then_inc(done, 1)
                if comb_dram is not None:
                    pe.wait_ge(b0, 2)
                    for t in range(TILES):
                        mm = nc.tensor.transpose(ps[0:E, 1 + t // 4, NT * (t % 4):NT * (t % 4) + NT], comb[:, 0, t, :],
                                                 k.ident[0:NT, 0:NT])
                    mm.then_inc(turned, 1)
                pe.wait_ge(cum, 1)
                pe.wait_ge(consts, 4)
                both = hot[:, 2].rearrange("p t e -> p (t e)")
                nc.tensor.matmul(ps[0:NT, 5, 0:TILES * E], before[:], both, start=True, stop=True)
                nc.tensor.matmul(ps[0:NT, 6, 0:TILES * E], k.ones[0:NT, 0:NT], both, start=True, stop=True).then_inc(counted, 1)

            @block.scalar
            def _(act):
                act.wait_ge(b0, 1)
                nc.scalar.activation(ex_sb[:], ex_sb[:], ACT.Exp)
                nc.scalar.activation(tmp[:, 1, :], tmp[:, 0, :], ACT.Exp).then_inc(ex, 1)
                if comb_dram is not None:
                    act.wait_ge(turned, 1)
                    nc.scalar.activation(combT[:, 0:1000].rearrange("p (b n) -> p b n", b=2), ps[0:E, 1:3, 0:500], ACT.Copy)
                    nc.scalar.activation(combT[:, 1000:T], ps[0:E, 3, 0:250], ACT.Copy).then_inc(laid, 1)

            @block.vector
            def _(dve):
                ch = Chain(dve, order)
                if comb_dram is not None:
                    ch.step(nc.vector.memset(combT[:, T:TP], 0.0))
                dve.wait_ge(done, 1)
                s3 = ps[0:NT, 0, 0:TILES * E].rearrange("p (t e) -> p t e", t=TILES)
                if rb_dram is not None:
                    dve.wait_ge(b_in, 16)
                    ch.then(nc.vector.tensor_tensor(sc[:], s3, rb[:].unsqueeze(1).broadcast_to([NT, TILES, E]), ALU.add))
                else:
                    ch.then(nc.vector.tensor_copy(sc[:], s3))
                for t in range(TILES):
                    ch.step(nc.vector.max(top[:, t, :], sc[:, t, :]))
                ch.wait()
                for t in range(TILES):
                    ch.step(nc.vector.max_index(idx[:, t, :], top[:, t, :], sc[:, t, :]))
                    ch.step(nc.vector.tensor_scalar(ex_sb[:, t, :], sc[:, t, :], top[:, t, 0:1], None, ALU.subtract))
                ch.wait()
                nc.vector.tensor_tensor(tmp[:, 0, :], top[:, :, 1], top[:, :, 0], ALU.subtract).then_inc(b0, 1)
                ch.step(nc.vector.tensor_copy(idf[:], idx[:]))
                dve.wait_ge(ex, 1)
                ch.then(nc.vector.tensor_reduce(tmp[:, 2, :], ex_sb[:], AX_X, ALU.add))
                ch.then(nc.vector.reciprocal(tmp[:, 3, :], tmp[:, 2, :]))
                ch.step(nc.vector.tensor_copy(pr[:, :, 0], tmp[:, 3, :]))
                ch.then(nc.vector.tensor_tensor(pr[:, :, 1], tmp[:, 1, :], tmp[:, 3, :], ALU.mult))
                if renormalise:
                    ch.then(nc.vector.tensor_reduce(tmp[:, 4, :], pr[:], AX_X, ALU.add))
                    ch.then(nc.vector.tensor_scalar(tmp[:, 4, :], tmp[:, 4, :], 1e-9, None, ALU.add))
                    ch.then(nc.vector.reciprocal(tmp[:, 5, :], tmp[:, 4, :]))
                    for j in range(2):
                        ch.step(nc.vector.tensor_tensor(pr[:, :, j], pr[:, :, j], tmp[:, 5, :], ALU.mult))
                    ch.wait()
                for t in range(TILES):
                    for j in range(2):
                        if comb_dram is not None:
                            ch.step(nc.vector.tensor_scalar(comb[:, j, t, :], k.index16[0:NT, 0:E], idf[:, t, j:j + 1],
                                                            pr[:, t, j:j + 1], ALU.is_equal, ALU.mult))
                        ch.step(nc.vector.tensor_scalar(hot[:, j, t, :], k.index16[0:NT, 0:E], idf[:, t, j:j + 1], None, ALU.is_equal))
                ch.step(nc.vector.tensor_copy(k.weight[:], pr[:]))
                ch.wait()
                if comb_dram is not None:
                    nc.vector.tensor_tensor(comb[:, 0, :, :], comb[:, 0, :, :], comb[:, 1, :, :], ALU.add).then_inc(b0, 1)
                nc.vector.tensor_tensor(hot[:, 2], hot[:, 0], hot[:, 1], ALU.add).then_inc(cum, 1)
                ch.step(nc.vector.memset(carry[:, 0, :], 0.0))
                ch.step(nc.vector.memset(start[:, 0:1], 0.0))
                dve.wait_ge(counted, 1)
                ch.wait()
                for t in range(TILES):
                    ch.then(nc.vector.tensor_tensor(carry[:, t + 1, :], carry[:, t, :], ps[0:NT, 6, E * t:E * t + E], ALU.add))
                ch.step(nc.vector.tensor_tensor(over[:], carry[:, TILES, :].unsqueeze(2).broadcast_to([NT, E, TILES]),
                                                thr[:].unsqueeze(1).broadcast_to([NT, E, TILES]), ALU.is_gt))
                ch.then(nc.vector.tensor_tensor(pos[:], ps[0:NT, 5, 0:TILES * E].rearrange("p (t e) -> p t e", e=E),
                                                carry[:, 0:TILES, :], ALU.add))
                ch.then(nc.vector.tensor_reduce(nblk[:], over[:], AX_X, ALU.add))
                for e in range(E):
                    ch.then(nc.vector.tensor_tensor(start[:, e + 1:e + 2], start[:, e:e + 1], nblk[:, e:e + 1], ALU.add))
                ch.step(nc.vector.tensor_tensor(past[:], bidx[0:1, :].unsqueeze(2).broadcast_to([1, NG, E]),
                                                start[0:1, 1:E + 1].unsqueeze(1).broadcast_to([1, NG, E]), ALU.is_ge))
                ch.then(nc.vector.tensor_scalar(nblk[:], start[:, 0:E], float(GROUP), None, ALU.mult))
                ch.step(nc.vector.tensor_reduce(bex[:], past[:], AX_X, ALU.add))
                ch.then(nc.vector.tensor_tensor(pos[:], pos[:], nblk[:].unsqueeze(1).broadcast_to([NT, TILES, E]), ALU.add))
                ch.then(nc.vector.tensor_scalar(half[:], bidx[0:1, 0:NG:2], start[0:1, E:E + 1], None, ALU.is_lt))
                ch.then(nc.vector.tensor_reduce(quads[:], half[:], AX_X, ALU.add))
                ch.step(nc.vector.tensor_scalar(k.more_quads[:], quads[:], -2.0, 0.0, ALU.add, ALU.max))
                ch.step(nc.vector.tensor_scalar(k.group_expert[:, 0:NG], bex[:], float(E - 1), None, ALU.min))
                for j in range(2):
                    ch.step(nc.vector.tensor_tensor(hot[:, j], hot[:, j], pos[:], ALU.mult))
                ch.wait()
                for j in range(2):
                    ch.step(nc.vector.tensor_reduce(row[:, j, :], hot[:, j], AX_X, ALU.add))
                ch.wait()
                ch.step(nc.vector.tensor_copy(k.slot[:], row[:]))


def scatter_stage(k, name, rows_dram):
    nc, ps = k.nc, k.ps
    turned, copied, sent = k.sem(f"{name}_turned"), k.sem(f"{name}_copied"), k.soft_sem(f"{name}_sent")
    with ExitStack() as ctx:
        node = k.sb(f"{name}_node", [NT, TILES, D], ctx=ctx)
        with nc.Block() as block:
            @block.tensor
            def _(pe):
                for t in range(TILES):
                    for h in range(2):
                        n = 2 * t + h
                        if n >= 8:
                            pe.wait_ge(copied, n - 7)
                        for f in range(3):
                            mm = nc.tensor.transpose(ps[0:NT, n % 8, P * f:P * f + P], k.nT[:, 3 * h + f, tile_cols(t)], k.ident[:])
                        mm.then_inc(turned, 1)

            @block.scalar
            def _(act):
                for n in range(2 * TILES):
                    act.wait_ge(turned, n + 1)
                    nc.scalar.activation(node[:, n // 2, HALF * (n % 2):HALF * (n % 2) + HALF], ps[0:NT, n % 8, 0:HALF],
                                         ACT.Copy).then_inc(copied, 1)

            @block.gpsimd
            def _(pool):
                for t in range(TILES):
                    pool.wait_ge(copied, 2 * t + 2)
                    for j in range(2):
                        pool.indirect_dma_start(rows_dram, bass.IndirectOffsetOnAxis(ap=k.slot[:, j, t:t + 1], axis=0),
                                                node[:, t, :], None).then_inc(sent, 16)
                pool.wait_ge(sent, 16 * 2 * TILES)


def combine_stage(k, name, rows_dram):
    nc, ps = k.nc, k.ps
    got = [k.soft_sem(f"{name}_got{h}") for h in range(4)]
    mixed, both, turned, added = (k.sem(f"{name}_{x}") for x in ("mixed", "both", "turned", "added"))
    with ExitStack() as ctx:
        y = k.sb(f"{name}_y", [NT, 4, 2, D], ctx=ctx)
        with nc.Block() as block:
            @block.gpsimd
            def _(pool):
                for t in range(TILES):
                    if t >= 4:
                        pool.wait_ge(turned, 2 * (t - 3))
                    for j in range(2):
                        pool.indirect_dma_start(y[:, t % 4, j, :], None, rows_dram,
                                                bass.IndirectOffsetOnAxis(ap=k.slot[:, j, t:t + 1], axis=0)).then_inc(got[t % 4], 16)

            @block.vector
            def _(dve):
                def add(t):
                    for h in range(2):
                        n = 2 * t + h
                        dve.wait_ge(turned, n + 1)
                        nc.vector.tensor_tensor(k.xT[:, 3 * h:3 * h + 3, tile_cols(t)], k.xT[:, 3 * h:3 * h + 3, tile_cols(t)],
                                                ps[:, n % 8, 0:3 * NT].rearrange("p (f n) -> p f n", f=3), ALU.add).then_inc(added, 1)
                for t in range(TILES):
                    dve.wait_ge(got[t % 4], 32 * (t // 4 + 1))
                    nc.vector.tensor_scalar(y[:, t % 4, 0, :], y[:, t % 4, 0, :], k.weight[:, t, 0:1], None, ALU.mult).then_inc(mixed, 1)
                    dve.wait_ge(mixed, t + 1)
                    nc.vector.scalar_tensor_tensor(out=y[:, t % 4, 0, :], in0=y[:, t % 4, 1, :], scalar=k.weight[:, t, 1:2],
                                                   in1=y[:, t % 4, 0, :], op0=ALU.mult, op1=ALU.add).then_inc(both, 1)
                    if t >= 1:
                        add(t - 1)
                add(TILES - 1)

            @block.tensor
            def _(pe):
                for t in range(TILES):
                    pe.wait_ge(both, t + 1)
                    for h in range(2):
                        n = 2 * t + h
                        if n >= 8:
                            pe.wait_ge(added, n - 7)
                        for f in range(3):
                            mm = nc.tensor.transpose(ps[:, n % 8, NT * f:NT * f + NT], y[:, t % 4, 0, P * (3 * h + f):P * (3 * h + f) + P],
                                                     k.ident[0:NT, 0:NT])
                        mm.then_inc(turned, 1)


class Block:

    def __init__(self, i, m, end=False):
        self.i, self.m = i, m
        self.j, self.x = 4 * i + m, m % 2
        self.g, self.w = 2 * i + m // 2, m // 2
        self.opens = m % 2 == 0
        self.first = isinstance(i, int) and i == 0 and m == 0
        self.last, self.last_group = end and m == 3, end and m >= 2

    def next(self):
        return Block(self.i, self.m + 1) if self.m < 3 else Block(self.i + 1, 0)

    def before(self):
        return Block(self.i, self.m - 1) if self.m > 0 else Block(self.i - 1, 3)

    def next_group(self):
        return Block(self.i, 2) if self.w == 0 else Block(self.i + 1, 0)


def block_stage(k, name, NG, E, w_dram, rows_dram, gated):
    nc, ps = k.nc, k.ps
    WC = FC * D
    W1 = FC * 512 if gated else WC // 2
    KH = 2
    s = {n: k.sem(f"{name}_{n}") for n in (
        "x_turned", "x_high", "x_split", "w_high", "w_split", "v_high", "v_split", "h_done", "sig", "u1", "hidden", "h_turned",
        "h_high", "h_split", "y_done", "y_out")}
    used = s["h_done" if gated else "y_done"]
    xl, wl, vl, st = ([k.sem(f"{name}_{n}{h}") for h in range(2)] for n in ("x_in", "w_in", "v_in", "stored"))
    with ExitStack() as ctx:
        w = k.sb(f"{name}_w", [P, 2, WC], ctx=ctx)
        whi = k.sb(f"{name}_wh", [P, 2, WC], F32R, ctx=ctx)
        wlo = k.sb(f"{name}_wl", [P, 2, WC], F32R, ctx=ctx)
        x = k.sb(f"{name}_x", [P, 2, D], ctx=ctx)
        xhi = k.sb(f"{name}_xh", [P, 2, FC, P], F32R, ctx=ctx)
        xlo = k.sb(f"{name}_xl", [P, 2, FC, P], F32R, ctx=ctx)
        y = k.sb(f"{name}_y", [P, 2, D], ctx=ctx)
        if gated:
            sg = k.sb(f"{name}_sg", [P, 256], ctx=ctx)
            hid = k.sb(f"{name}_hid", [P, 2, 256], ctx=ctx)
            hhi = k.sb(f"{name}_hh", [P, KH, P], F32R, ctx=ctx)
            hlo = k.sb(f"{name}_hl", [P, KH, P], F32R, ctx=ctx)

        def run(eng, step):
            more = eng.value_load(k.more_quads[0:1, 0:1], min_val=0, max_val=NG // 2 - 2)
            for m in range(4):
                step(Block(0, m))
            with eng.Fori(1, more + 1) as i:
                for m in range(4):
                    step(Block(i, m))
            for m in range(4):
                step(Block(more + 1, m, end=True))
            return Block(more + 1, 3)

        def ge(eng, sem, value):
            if not isinstance(value, int) or value > 0:
                eng.wait_ge(sem, value)

        with nc.Block(no_gpsimd_drain=True) as block:
            @block.sync
            def _(sp):
                def weights_in(b):
                    e = sp.value_load(k.group_expert[0:1, bass.ds(b.g, 1)], min_val=0, max_val=E - 1)
                    ge(sp, s["w_split"], b.g - 1)
                    sp.dma_start(w[:, b.w, 0:W1], w_dram[bass.ds(e, 1), :, 0:W1].rearrange("e p n -> (e p) n")).then_inc(wl[b.w], 16)
                    ge(sp, s["v_split"], b.g - 1)
                    sp.dma_start(w[:, b.w, W1:], w_dram[bass.ds(e, 1), :, W1:].rearrange("e p n -> (e p) n")).then_inc(vl[b.w], 16)

                def step(b):
                    ge(sp, s["x_turned"], b.j - 1)
                    sp.dma_start(x[:, b.x, :], rows_dram[bass.ds(b.j * P, P), :]).then_inc(xl[b.x], 16)
                    if b.opens and not b.last_group:
                        weights_in(b.next_group())
                weights_in(Block(0, 0))
                run(sp, step)

            @block.tensor
            def _(pe):
                def turn_x(b):
                    pe.wait_ge(xl[b.x], 16 * (b.g + 1))
                    ge(pe, s["x_split"], b.j)
                    for f in range(FC):
                        mm = nc.tensor.transpose(ps[:, f // 3, P * (f % 3):P * (f % 3) + P], x[:, b.x, P * f:P * f + P], k.ident[:])
                    mm.then_inc(s["x_turned"], 1)

                def product(b):
                    pe.wait_ge(s["x_split"], b.j + 1)
                    if b.opens:
                        pe.wait_ge(s["w_split"], b.g + 1)
                    if gated:
                        ge(pe, s["hidden"], b.j - 1)
                        for f in range(FC):
                            mm = three_passes(nc, ps[:, 2 + b.x, :], (xhi[:, b.x, f, :], xlo[:, b.x, f, :]),
                                              (whi[:, b.w, 512 * f:512 * f + 512], wlo[:, b.w, 512 * f:512 * f + 512]),
                                              f == 0, f == FC - 1)
                        mm.then_inc(s["h_done"], 1)
                    else:
                        ge(pe, s["y_out"], b.j - 1)
                        for f in range(FC):
                            if D * f == W1 and b.opens:
                                pe.wait_ge(s["v_split"], b.g + 1)
                            for q in range(2):
                                c0 = D * f + HALF * q
                                mm = three_passes(nc, ps[:, 2 + 2 * b.x + q, 0:HALF], (xhi[:, b.x, f, :], xlo[:, b.x, f, :]),
                                                  (whi[:, b.w, c0:c0 + HALF], wlo[:, b.w, c0:c0 + HALF]), f == 0, f == FC - 1)
                        mm.then_inc(s["y_done"], 1)

                def turn_hidden(b):
                    pe.wait_ge(s["hidden"], b.j + 1)
                    ge(pe, s["h_split"], b.j)
                    for f in range(KH):
                        mm = nc.tensor.transpose(ps[:, 4, P * f:P * f + P], hid[:, b.x, P * f:P * f + P], k.ident[:])
                    mm.then_inc(s["h_turned"], 1)

                def result(b):
                    pe.wait_ge(s["h_split"], b.j + 1)
                    pe.wait_ge(s["v_split"], b.g + 1)
                    ge(pe, s["y_out"], b.j)
                    for f in range(KH):
                        for q in range(2):
                            c0 = W1 + D * f + HALF * q
                            mm = three_passes(nc, ps[:, 5 + q, 0:HALF], (hhi[:, f, :], hlo[:, f, :]),
                                              (whi[:, b.w, c0:c0 + HALF], wlo[:, b.w, c0:c0 + HALF]), f == 0, f == KH - 1)
                    mm.then_inc(s["y_done"], 1)

                def step(b):
                    if gated and not b.first:
                        turn_hidden(b.before())
                    if not b.last:
                        turn_x(b.next())
                    product(b)
                    if gated and not b.first:
                        result(b.before())
                turn_x(Block(0, 0))
                b = run(pe, step)
                if gated:
                    turn_hidden(b)
                    result(b)

            @block.scalar
            def _(act):
                def weights_high(b):
                    act.wait_ge(wl[b.w], 16 * (b.i + 1))
                    ge(act, used, 2 * b.g - 2)
                    nc.scalar.activation(whi[:, b.w, 0:W1], w[:, b.w, 0:W1], ACT.Copy).then_inc(s["w_high"], 1)

                def rest_high(b):
                    act.wait_ge(vl[b.w], 16 * (b.i + 1))
                    ge(act, s["y_done"], 2 * b.g - 2)
                    nc.scalar.activation(whi[:, b.w, W1:], w[:, b.w, W1:], ACT.Copy).then_inc(s["v_high"], 1)

                def x_high(b):
                    act.wait_ge(s["x_turned"], b.j + 1)
                    ge(act, used, b.j - 1)
                    nc.scalar.activation(xhi[:, b.x, :, :].rearrange("p (b f) n -> p b (f n)", b=2), ps[:, 0:2, 0:3 * P],
                                         ACT.Copy).then_inc(s["x_high"], 1)

                def hidden_high(b):
                    act.wait_ge(s["h_turned"], b.j + 1)
                    ge(act, s["y_done"], b.j)
                    nc.scalar.activation(hhi[:].rearrange("p f n -> p (f n)"), ps[:, 4, 0:256], ACT.Copy).then_inc(s["h_high"], 1)

                def y_out(b):
                    act.wait_ge(s["y_done"], b.j + 1)
                    ge(act, st[b.x], 16 * b.g)
                    c = 5 if gated else 2 + 2 * b.x
                    nc.scalar.activation(y[:, b.x, :].rearrange("p (b n) -> p b n", b=2), ps[:, c:c + 2, 0:HALF],
                                         ACT.Copy).then_inc(s["y_out"], 1)
                    act.wait_ge(s["y_out"], b.j + 1)
                    act.dma_start(rows_dram[bass.ds(b.j * P, P), :], y[:, b.x, :]).then_inc(st[b.x], 16)

                def step(b):
                    if gated and not b.first:
                        hidden_high(b.before())
                    if not b.last:
                        x_high(b.next())
                    if b.opens and not b.last_group:
                        weights_high(b.next_group())
                    if gated:
                        act.wait_ge(s["h_done"], b.j + 1)
                        ge(act, s["u1"], b.j)
                        nc.scalar.activation(sg[:], ps[:, 2 + b.x, 0:256], ACT.Sigmoid).then_inc(s["sig"], 1)
                    if not b.opens and not b.last_group:
                        rest_high(b.next_group())
                    if not gated:
                        y_out(b)
                    elif not b.first:
                        y_out(b.before())
                x_high(Block(0, 0))
                weights_high(Block(0, 0))
                rest_high(Block(0, 0))
                b = run(act, step)
                if gated:
                    hidden_high(b)
                    y_out(b)
                for h in range(2):
                    act.wait_ge(st[h], 16 * (b.g + 1))
                    nc.scalar.activation(y[:, h, 0:1], y[:, h, 0:1], ACT.Copy)

            @block.vector
            def _(dve):
                def weights_low(b):
                    dve.wait_ge(s["w_high"], b.g + 1)
                    nc.vector.tensor_tensor(wlo[:, b.w, 0:W1], w[:, b.w, 0:W1], whi[:, b.w, 0:W1].bitcast(F32), ALU.subtract)\
                        .then_inc(s["w_split"], 1)

                def rest_low(b):
                    dve.wait_ge(s["v_high"], b.g + 1)
                    nc.vector.tensor_tensor(wlo[:, b.w, W1:], w[:, b.w, W1:], whi[:, b.w, W1:].bitcast(F32), ALU.subtract)\
                        .then_inc(s["v_split"], 1)

                def x_low(b):
                    dve.wait_ge(s["x_high"], b.j + 1)
                    nc.vector.tensor_tensor(xlo[:, b.x, :, :].rearrange("p (b f) n -> p b (f n)", b=2), ps[:, 0:2, 0:3 * P],
                                            xhi[:, b.x, :, :].rearrange("p (b f) n -> p b (f n)", b=2).bitcast(F32),
                                            ALU.subtract).then_inc(s["x_split"], 1)

                def hidden_low(b):
                    dve.wait_ge(s["h_high"], b.j + 1)
                    nc.vector.tensor_tensor(hlo[:].rearrange("p f n -> p (f n)"), ps[:, 4, 0:256],
                                            hhi[:].rearrange("p f n -> p (f n)").bitcast(F32), ALU.subtract).then_inc(s["h_split"], 1)

                def step(b):
                    if gated and not b.first:
                        hidden_low(b.before())
                    if not b.last:
                        x_low(b.next())
                    if b.opens and not b.last_group:
                        weights_low(b.next_group())
                    if gated:
                        dve.wait_ge(s["sig"], b.j + 1)
                        nc.vector.tensor_tensor(hid[:, b.x, :], ps[:, 2 + b.x, 0:256], sg[:], ALU.mult).then_inc(s["u1"], 1)
                        dve.wait_ge(s["u1"], b.j + 1)
                        nc.vector.tensor_tensor(hid[:, b.x, :], ps[:, 2 + b.x, 256:512], hid[:, b.x, :], ALU.mult)\
                            .then_inc(s["hidden"], 1)
                    if not b.opens and not b.last_group:
                        rest_low(b.next_group())
                x_low(Block(0, 0))
                weights_low(Block(0, 0))
                rest_low(Block(0, 0))
                b = run(dve, step)
                if gated:
                    hidden_low(b)


def routed_bias_stage(k, eb_dram, comb_dram, E):
    nc, ps = k.nc, k.ps
    done, eb_in, out = k.sem("rb_done"), k.sem("rb_in"), k.sem("rb_out")
    with ExitStack() as ctx:
        eb = k.sb("rb_b", [E, D], ctx=ctx)
        ct = k.sb("rb_comb", [E, TP], ctx=ctx)
        with nc.Block(no_gpsimd_drain=True) as block:
            @block.sync
            def _(sp):
                sp.dma_start(eb[:], eb_dram).then_inc(eb_in, 16)
                sp.dma_start(ct[:], comb_dram[:, :]).then_inc(eb_in, 16)

            @block.tensor
            def _(pe):
                pe.wait_ge(eb_in, 32)
                for o in range(FC):
                    if o >= 2:
                        pe.wait_ge(out, o - 1)
                    for c in range(CH):
                        mm = nc.tensor.matmul(ps[:, 3 * (o % 2) + c, 0:CW], eb[:, P * o:P * o + P], ct[:, cols(c)], start=True, stop=True)
                    mm.then_inc(done, 1)

            @block.vector
            def _(dve):
                for o in range(FC):
                    dve.wait_ge(done, o + 1)
                    g = 3 * (o % 2)
                    xo = k.xT[:, o, :].rearrange("p (c n) -> p c n", c=CH)
                    nc.vector.tensor_tensor(xo, xo, ps[:, g:g + CH, 0:CW], ALU.add).then_inc(out, 1)


def flow_attention_stage(k, w_qk, b_qk, w_v, b_v):
    nc, ps = k.nc, k.ps
    H = 2 * FC
    E6 = 1e-6
    s = {n: k.sem("fa_" + n) for n in (
        "qk_done", "qk_out", "turned", "copied", "order", "dots1", "dots2", "flow1", "sums", "v_done", "v_out",
        "columns", "flow2", "exp", "total", "comp", "vscaled", "kv", "kv_out", "att", "att_out", "att_turned", "att_copied",
        "cols_in", "eps_made")}
    wl = [k.sem(f"fa_weights{h}") for h in range(2)]
    with ExitStack() as ctx:
        qT = k.sb("fa_qT", [P, FC, TP], ctx=ctx)
        kT = k.attT
        q_node = k.sb("fa_q_node", [NT, TILES, D], ctx=ctx)
        k_node = k.sb("fa_k_node", [NT, TILES, D], ctx=ctx)
        w = k.sb("fa_w", [P, 2, FC, HALF], ctx=ctx)
        ws = w[:].rearrange("p s f n -> p s (f n)")[:, :, 0:D].rearrange("p s (f n) -> p s f n", f=FC)
        bqk = k.sb("fa_bqk", [P, 2 * FC], ctx=ctx)
        part = k.sb("fa_part", [P, 2 * FC, CH], ctx=ctx)
        vec = k.sb("fa_vec", [P, 2 * FC], ctx=ctx)
        head2 = k.sb("fa_head2", [P, 2], ctx=ctx)
        cl = k.sb("fa_columns", [P, 2, 2, FC, 2], ctx=ctx)
        epsr = k.sb("fa_eps_rows", [NT, 2, H], ctx=ctx)
        fl = k.sb("fa_flow", [NT, 5, TILES, H], ctx=ctx)
        tot = epsr
        kvb = k.sb("fa_kvb", [P, FC, P], ctx=ctx)
        epsm = kvb[:, 0, 0:NT]
        v_node, mix_node = q_node, k_node
        with nc.Block(no_gpsimd_drain=True) as block:
            @block.sync
            def _(sp):
                sp.dma_start(bqk[:], b_qk).then_inc(s["cols_in"], 16)
                for j in range(2 * FC):
                    if j >= 2:
                        sp.wait_ge(s["qk_done"], CH * (j - 1))
                    sp.dma_start(ws[:, j % 2], w_qk[j]).then_inc(wl[j % 2], 16)

            @block.vector
            def _(dve):
                nc.vector.tensor_copy(head2[:], k.heads2[:, 0:P:64])
                nc.vector.memset(epsm, E6).then_inc(s["eps_made"], 1)
                nc.vector.memset(qT[:, :, T:TP], 0.0)
                nc.vector.memset(kT[:, :, T:TP], 0.0)
                for g in range(2 * FC):
                    for q in range(3):
                        n = 3 * g + q
                        m = min(4, TILES - 4 * q)
                        dst, c = (q_node, g) if g < FC else (k_node, g - FC)
                        dve.wait_ge(s["turned"], n + 1)
                        nc.vector.tensor_copy(dst[:, 4 * q:4 * q + m, P * c:P * c + P],
                                              ps[0:NT, 6 + n % 2, 0:m * P].rearrange("p (t d) -> p t d", t=m)).then_inc(s["copied"], 1)

            @block.scalar
            def _(act):
                act.wait_ge(s["cols_in"], 16)
                for j in range(2 * FC):
                    dst = (qT if j < FC else kT)[:, j % FC, :]
                    for c in range(CH):
                        n = j * CH + c
                        act.wait_ge(s["qk_done"], n + 1)
                        wd = min(CW, T - c * CW)
                        nc.scalar.activation(dst[:, c * CW:c * CW + wd], ps[:, n % 6, 0:wd], ACT.Sigmoid, bias=bqk[:, j:j + 1],
                                             accum_out=part[:, j, c:c + 1]).then_inc(s["qk_out"], 1)

            @block.tensor
            def _(pe):
                def turn(g):
                    src, c = (qT, g) if g < FC else (kT, g - FC)
                    pe.wait_ge(s["qk_out"], CH * (g + 1))
                    for q in range(3):
                        n = 3 * g + q
                        if n >= 2:
                            pe.wait_ge(s["copied"], n - 1)
                        for t in range(4 * q, min(4 * q + 4, TILES)):
                            mm = nc.tensor.transpose(ps[0:NT, 6 + n % 2, P * (t % 4):P * (t % 4) + P], src[:, c, tile_cols(t)],
                                                     k.ident[:])
                        mm.then_inc(s["turned"], 1)
                for j in range(2 * FC):
                    pe.wait_ge(wl[j % 2], 16 * (j // 2 + 1))
                    for c in range(CH):
                        n = j * CH + c
                        if n >= 6:
                            pe.wait_ge(s["qk_out"], n - 5)
                        for f in range(FC):
                            mm = nc.tensor.matmul(ps[:, n % 6, 0:CW], ws[:, j % 2, f, :], k.nT[:, f, cols(c)],
                                                  start=(f == 0), stop=(f == FC - 1))
                        mm.then_inc(s["qk_done"], 1)
                    if j >= 1:
                        turn(j - 1)
                turn(2 * FC - 1)

        b_in, v_in = k.sem("fa_vbias_in"), [k.sem(f"fa_v_in{h}") for h in range(2)]
        bv = k.sb("fa_bv", [NT, HALF], ctx=ctx)
        with nc.Block(no_gpsimd_drain=True) as block:
            @block.sync
            def _(sp):
                sp.dma_start(bv[:], b_v[0:HALF].partition_broadcast(NT)).then_inc(b_in, 16)
                for h in range(2):
                    sp.dma_start(w[:, h], w_v[h]).then_inc(v_in[h], 16)
                sp.wait_ge(s["v_out"], TILES)
                sp.dma_start(bv[:], b_v[HALF:D].partition_broadcast(NT)).then_inc(b_in, 16)

            @block.tensor
            def _(pe):
                def dots(step, done):
                    for side, src in ((0, qT), (1, kT)):
                        for t in range(TILES):
                            for p in range(FC):
                                nc.tensor.matmul(ps[0:NT, side, H * t + 2 * p:H * t + 2 * p + 2], src[:, p, tile_cols(t)],
                                                 cl[:, step, side, p, :], start=True, stop=True)
                    for side in range(2):
                        for p in range(FC):
                            mm = nc.tensor.matmul(ps[0:NT, 2, H * side + 2 * p:H * side + 2 * p + 2], epsm,
                                                  cl[:, step, side, p, :], start=True, stop=True)
                    mm.then_inc(done, 1)
                pe.wait_ge(s["columns"], 1)
                dots(0, s["dots1"])
                pe.wait_ge(s["flow1"], 2)
                for side, src, wt in ((0, k_node, 1), (1, q_node, 0)):
                    for p in range(FC):
                        for t in range(TILES):
                            mm = nc.tensor.matmul(ps[:, 3 + side, 2 * p:2 * p + 2], src[:, t, P * p:P * p + P],
                                                  fl[:, wt, t, 2 * p:2 * p + 2], start=(t == 0), stop=(t == TILES - 1))
                mm.then_inc(s["sums"], 1)
                pe.wait_ge(s["columns"], 2)
                dots(1, s["dots2"])
                for h in range(2):
                    pe.wait_ge(v_in[h], 16)
                    for t in range(TILES):
                        n = h * TILES + t
                        if n >= 3:
                            pe.wait_ge(s["v_out"], n - 2)
                        for f in range(FC):
                            mm = nc.tensor.matmul(ps[0:NT, 5 + n % 3, 0:HALF], k.nT[:, f, tile_cols(t)], w[:, h, f, :],
                                                  start=(f == 0), stop=(f == FC - 1))
                        mm.then_inc(s["v_done"], 1)
                pe.wait_ge(s["exp"], 3)
                nc.tensor.matmul(ps[0:NT, 3, 0:H], k.ones[0:NT, 0:NT], tot[:, 0, :], start=True, stop=True).then_inc(s["total"], 1)
                pe.wait_ge(s["vscaled"], TILES)
                for p in range(FC):
                    for t in range(TILES):
                        mm = nc.tensor.matmul(ps[:, p % 2, 0:P], k_node[:, t, P * p:P * p + P], v_node[:, t, P * p:P * p + P],
                                              start=(t == 0), stop=(t == TILES - 1))
                    mm.then_inc(s["kv"], 1)
                    if p < FC - 1:
                        if p >= 1:
                            pe.wait_ge(s["kv_out"], p)
                pe.wait_ge(s["kv_out"], FC)
                for t in range(TILES):
                    for h in range(2):
                        n = 2 * t + h
                        if n >= 4:
                            pe.wait_ge(s["att_out"], n - 3)
                        for p in range(3):
                            mm = nc.tensor.matmul(ps[0:NT, n % 4, P * p:P * p + P], qT[:, 3 * h + p, tile_cols(t)],
                                                  kvb[:, 3 * h + p, :], start=True, stop=True)
                        mm.then_inc(s["att"], 1)
                for c in range(FC):
                    for q in range(3):
                        n = 3 * c + q
                        pe.wait_ge(s["att_out"], 2 * TILES)
                        if n >= 4:
                            pe.wait_ge(s["att_copied"], n - 3)
                        for t in range(4 * q, min(4 * q + 4, TILES)):
                            mm = nc.tensor.transpose(ps[:, 4 + n % 4, NT * (t % 4):NT * (t % 4) + NT],
                                                     mix_node[:, t, P * c:P * c + P], k.ident[0:NT, 0:NT])
                        mm.then_inc(s["att_turned"], 1)

            @block.scalar
            def _(act):
                act.wait_ge(s["flow2"], 1)
                nc.scalar.activation(fl[:, 2, :, :], fl[:, 2, :, :], ACT.Sigmoid).then_inc(s["exp"], 1)
                nc.scalar.activation(fl[:, 3, :, :], fl[:, 3, :, :], ACT.Exp).then_inc(s["exp"], 1)
                for c in range(FC):
                    for q in range(3):
                        n = 3 * c + q
                        m = min(4, TILES - 4 * q)
                        act.wait_ge(s["att_turned"], n + 1)
                        nc.scalar.activation(k.attT[:, c, 4 * NT * q:4 * NT * q + m * NT], ps[:, 4 + n % 4, 0:m * NT],
                                             ACT.Copy).then_inc(s["att_copied"], 1)

            @block.vector
            def _(dve):
                ch = Chain(dve, s["order"])

                def masked(step, side, values):
                    return nc.vector.scalar_tensor_tensor(out=cl[:, step, side], in0=values, scalar=E6,
                                                          in1=head2[:].unsqueeze(1).broadcast_to([P, FC, 2]), op0=ALU.add, op1=ALU.mult)
                ch.then(nc.vector.tensor_reduce(vec[:], part[:], AX_X, ALU.add))
                ch.then(masked(0, 0, vec[:, FC:].unsqueeze(2).broadcast_to([P, FC, 2])))
                masked(0, 1, vec[:, 0:FC].unsqueeze(2).broadcast_to([P, FC, 2])).then_inc(s["columns"], 1)

                def dots_out(step, sem, dst0, dst1):
                    dve.wait_ge(sem, 1)
                    ch.then(nc.vector.tensor_scalar(epsr[:], ps[0:NT, 2, 0:2 * H].rearrange("p (s h) -> p s h", s=2), E6, None, ALU.add))
                    for side, dst in ((0, dst0), (1, dst1)):
                        ch.step(nc.vector.tensor_tensor(dst, ps[0:NT, side, 0:TILES * H].rearrange("p (t h) -> p t h", h=H),
                                                        epsr[:, side, :].unsqueeze(1).broadcast_to([NT, TILES, H]), ALU.add))
                    ch.wait()
                dots_out(0, s["dots1"], fl[:, 2], fl[:, 3])
                nc.vector.reciprocal(fl[:, 0], fl[:, 2]).then_inc(s["flow1"], 1)
                nc.vector.reciprocal(fl[:, 1], fl[:, 3]).then_inc(s["flow1"], 1)
                dve.wait_ge(s["sums"], 1)
                ch.then(masked(1, 0, ps[:, 3, 0:H].rearrange("p (c h) -> p c h", h=2)))
                masked(1, 1, ps[:, 4, 0:H].rearrange("p (c h) -> p c h", h=2)).then_inc(s["columns"], 1)
                dots_out(1, s["dots2"], fl[:, 2], fl[:, 4])
                nc.vector.tensor_scalar(fl[:, 3], fl[:, 4], -1.0, 1.0, ALU.max, ALU.min).then_inc(s["flow2"], 1)
                dve.wait_ge(s["exp"], 2)
                nc.vector.tensor_reduce(tot[:, 0, :], fl[:, 3].rearrange("p t h -> p h t"), AX_X, ALU.add).then_inc(s["exp"], 1)
                ch.step(nc.vector.tensor_tensor(fl[:, 2], fl[:, 2], fl[:, 0], ALU.mult))
                for n in range(2 * TILES):
                    h, t = n // TILES, n % TILES
                    if t == 0:
                        dve.wait_ge(b_in, 16 * (h + 1))
                    dve.wait_ge(s["v_done"], n + 1)
                    nc.vector.tensor_tensor(v_node[:, t, HALF * h:HALF * h + HALF], ps[0:NT, 5 + n % 3, 0:HALF],
                                            bv[:], ALU.add).then_inc(s["v_out"], 1)
                dve.wait_ge(s["total"], 1)
                ch.then(nc.vector.reciprocal(tot[:, 1, :], ps[0:NT, 3, 0:H]))
                ch.then(nc.vector.tensor_scalar(tot[:, 1, :], tot[:, 1, :], float(T), None, ALU.mult))
                ch.then(nc.vector.tensor_tensor(fl[:, 4], fl[:, 3], tot[:, 1, :].unsqueeze(1).broadcast_to([NT, TILES, H]), ALU.mult))
                dve.wait_ge(s["v_out"], 2 * TILES)
                for t in range(TILES):
                    v3 = v_node[:, t, :].rearrange("p (h e) -> p h e", h=H)
                    nc.vector.tensor_tensor(v3, v3, fl[:, 4, t, :].unsqueeze(2).broadcast_to([NT, H, D // H]),
                                            ALU.mult).then_inc(s["vscaled"], 1)
                for p in range(FC):
                    dve.wait_ge(s["kv"], p + 1)
                    nc.vector.tensor_tensor(kvb[:, p, :], ps[:, p % 2, 0:P], k.heads2[:], ALU.mult).then_inc(s["kv_out"], 1)
                for n in range(2 * TILES):
                    t, h = n // 2, n % 2
                    dve.wait_ge(s["att"], n + 1)
                    nc.vector.tensor_tensor(mix_node[:, t, HALF * h:HALF * h + HALF].rearrange("p (h e) -> p h e", h=FC),
                                            ps[0:NT, n % 4, 0:HALF].rearrange("p (h e) -> p h e", h=FC),
                                            fl[:, 2, t, FC * h:FC * h + FC].unsqueeze(2).broadcast_to([NT, FC, D // H]),
                                            ALU.mult).then_inc(s["att_out"], 1)


def flow_project_stage(k, w_dram, bias_dram):
    nc = k.nc
    added, b_in, b2 = k.sem("fp_added"), k.sem("fp_bias_in"), k.sem("fp_bias2")
    with ExitStack() as ctx:
        g_sb = k.sb("fp_gate", [P, 2, TP], ctx=ctx)
        bias = k.sb("fp_bias", [P, FC], ctx=ctx)

        def loads(sp):
            sp.dma_start(bias[:], bias_dram).then_inc(b_in, 16)

        def prepare(dve):
            dve.wait_ge(b_in, 16)
            nc.vector.tensor_scalar(bias[:], bias[:], 2.0, None, ALU.mult).then_inc(b2, 1)

        def gate(act, o, banks, done, out):
            if o == 0:
                act.wait_ge(b2, 1)
            act.wait_ge(done, o + 1)
            if o >= 2:
                act.wait_ge(added, o - 1)
            nc.scalar.activation(g_sb[:, o % 2, :].rearrange("p (c n) -> p c n", c=CH), banks,
                                 ACT.Sigmoid, bias=bias[:, o:o + 1], scale=2.0).then_inc(out, 1)

        def add(dve, o, banks, done, out):
            dve.wait_ge(out, o + 1)
            nc.vector.tensor_tensor(k.xT[:, o, :], k.xT[:, o, :], g_sb[:, o % 2, :], ALU.add).then_inc(added, 1)
        project_stage(k, "fp", [(k.attT, FC)], FC, w_dram, loads, prepare, add, gate)


def graph_project_stage(k, w_dram, att_dram, h_dram, heads, F):
    nc, ps = k.nc, k.ps
    N = heads * TILES
    high, split, w_high, w_split, done, out, al, order = (k.sem(f"gp_{n}") for n in (
        "high", "split", "w_high", "w_split", "done", "out", "al", "order"))
    w_in, at_in = k.sem("gp_w_in"), k.sem("gp_att_in")
    st = [k.sem(f"gp_stored{h}") for h in range(4)]
    with ExitStack() as ctx:
        hi = k.sb("gp_hi", [P, FC, TP], F32R, ctx=ctx)
        lo = k.sb("gp_lo", [P, FC, TP], F32R, ctx=ctx)
        w = k.sb("gp_w", [P, FC, F], ctx=ctx)
        whi = k.sb("gp_w_hi", [P, 2, FC, F], F32R, ctx=ctx)
        wlo = k.sb("gp_w_lo", [P, 2, FC, F], F32R, ctx=ctx)
        h = k.sb("gp_h", [NT, 4, F], ctx=ctx)
        a_rows = k.nT[0:NT].rearrange("p f n -> p (f n)")[:, 0:2 * heads * F].rearrange("p (j i f) -> p j i f", j=2, i=heads)
        scr = k.sb("gp_unused", [NT, F], BF16, ctx=ctx)
        with nc.Block(no_gpsimd_drain=True) as block:
            @block.sync
            def _(sp):
                for i in range(heads):
                    if i >= 1:
                        sp.wait_ge(w_split, i)
                    sp.dma_start(w[:], w_dram[i]).then_inc(w_in, 16)
                    if i == 0:
                        sp.wait_ge(split, FC)
                        for j in range(2):
                            for m in range(heads):
                                sp.dma_start(a_rows[:, j, m, :], att_dram[j, m].partition_broadcast(NT)).then_inc(at_in, 16)

            @block.tensor
            def _(pe):
                for n in range(N):
                    i, t = n // TILES, n % TILES
                    if t == 0:
                        pe.wait_ge(w_split, i + 1)
                        pe.wait_ge(split, FC)
                    if n >= 4:
                        pe.wait_ge(out, n - 3)
                    for f in range(FC):
                        mm = three_passes(nc, ps[0:NT, n % 4, 0:F], (hi[:, f, tile_cols(t)], lo[:, f, tile_cols(t)]),
                                          (whi[:, i % 2, f, :], wlo[:, i % 2, f, :]), f == 0, f == FC - 1)
                    mm.then_inc(done, 1)

            @block.scalar
            def _(act):
                def weights_high(i):
                    act.wait_ge(w_in, 16 * (i + 1))
                    if i >= 2:
                        act.wait_ge(done, TILES * (i - 1))
                    nc.scalar.activation(whi[:, i % 2], w[:], ACT.Copy).then_inc(w_high, 1)
                for f in range(FC):
                    nc.scalar.activation(hi[:, f, :], k.nT[:, f, :], ACT.Copy).then_inc(high, 1)
                weights_high(0)
                for n in range(N):
                    if n % TILES == 1 and n // TILES + 1 < heads:
                        weights_high(n // TILES + 1)
                    act.wait_ge(done, n + 1)
                    if n >= 4:
                        act.wait_ge(st[n % 4], 16 * (n // 4))
                        act.wait_ge(al, 2 * (n - 3))
                    nc.scalar.activation(h[:, n % 4, :], ps[0:NT, n % 4, 0:F], ACT.Copy).then_inc(out, 1)
                    act.wait_ge(out, n + 1)
                    act.dma_start(h_dram[n // TILES, :, n % TILES, :], h[:, n % 4, :]).then_inc(st[n % 4], 16)
                for q in range(4):
                    act.wait_ge(st[q], 16 * (N // 4))

            @block.vector
            def _(dve):
                def weights_low(i):
                    dve.wait_ge(w_high, i + 1)
                    nc.vector.tensor_tensor(wlo[:, i % 2], w[:], whi[:, i % 2].bitcast(F32), ALU.subtract).then_inc(w_split, 1)
                for f in range(FC):
                    dve.wait_ge(high, f + 1)
                    nc.vector.tensor_tensor(lo[:, f, :], k.nT[:, f, :], hi[:, f, :].bitcast(F32), ALU.subtract).then_inc(split, 1)
                weights_low(0)
                dve.wait_ge(at_in, 16 * 2 * heads)
                for n in range(N):
                    i, t = n // TILES, n % TILES
                    if t == 1 and i + 1 < heads:
                        weights_low(i + 1)
                    dve.wait_ge(out, n + 1)
                    for j in range(2):
                        m = 2 * n + j
                        if m >= 1:
                            dve.wait_ge(al, m)
                        nc.vector.tensor_tensor_reduce(scr[:], h[:, n % 4, :], a_rows[:, j, i, :], 1.0, 0.0, ALU.mult, ALU.add,
                                                       k.al[:, i, j, t:t + 1]).then_inc(al, 1)
                dve.wait_ge(al, 2 * N)
                nc.vector.tensor_scalar(k.al[:, :, 2, :], k.al[:, :, 0, :], 0.2, None, ALU.mult).then_inc(order, 1)


def graph_layer(k, name, heads, F, h_dram, att_dram, b_dram, wide, h1_dram=None):
    nc, ps = k.nc, k.ps
    NF = F // P
    DEN = NF
    HB = 2 if wide else 1
    s = {n: k.sem(f"{name}_{n}") for n in (
        "al", "order", "as_diag", "as_row", "as_out", "far_read", "r_diag", "r_row", "r_out",
        "leaked", "low", "exped", "p_made", "summed", "agg", "inverse", "scaled", "elu_exp", "result")}
    h_in, at_in, b_in = [k.sem(f"{name}_h_in{h}") for h in range(2)], k.sem(f"{name}_att_in"), k.sem(f"{name}_b_in")
    far_in = [k.sem(f"{name}_far_in{h}") for h in range(2)]
    c_in = k.sem(f"{name}_counts_in")
    st_out = [k.sem(f"{name}_stored{h}") for h in range(2)] if wide else None
    LR = 0.2
    with ExitStack() as ctx:
        if wide:
            h_sb = k.sb(f"{name}_h", [NT, HB, TILES, F], ctx=ctx)
        else:
            h_sb = k.h2.rearrange("p (a t f) -> p a t f", a=1, t=TILES)
        counts = k.sb(f"{name}_counts", [NT, TILES, TP], I16, ctx=ctx)
        if wide:
            al = k.al
        else:
            a_rows = k.sb(f"{name}_a", [NT, 2, F], ctx=ctx)
            al = k.sb(f"{name}_al", [NT, 1, 3, TILES], ctx=ctx)
        mx = k.sb(f"{name}_mx", [NT, 5, TILES], ctx=ctx)
        rows = k.sb(f"{name}_rows", [P, 2, 2, TP], ctx=ctx)
        far = k.sb(f"{name}_far", [NT, 2, T], BF16, ctx=ctx)
        scratch = k.sb(f"{name}_scratch", [P, 4 * CW], ctx=ctx)
        o1 = scratch[:, 0:2 * CW].rearrange("p (s n) -> p s n", s=2)
        rden = scratch[:, 2 * CW:3 * CW]
        t1 = scratch[0:NT, :].rearrange("p (s n) -> p s n", n=CW)
        t2 = k.sb(f"{name}_leaked", [NT, 2, CW], ctx=ctx)
        diag = k.sb(f"{name}_diag", [NT, T], ctx=ctx)
        dg = diag[:].rearrange("p (t n) -> p t n", n=NT)
        logits_rest = diag[:, 0:F]
        maxima_rest = diag[:, 0:T // 2].bitcast(BF16)
        pr = k.sb(f"{name}_p", [NT, 2, TILES, CW], ctx=ctx)
        sm = k.sb(f"{name}_sm", [NT, 2, CW], ctx=ctx)
        o2 = k.sb(f"{name}_o2", [P, 2, CW], ctx=ctx)
        bias = k.sb(f"{name}_bias", [P, heads * NF], ctx=ctx)
        with nc.Block(no_gpsimd_drain=True) as block:
            @block.sync
            def _(sp):
                def head_in(i):
                    if i >= 2:
                        sp.wait_ge(s["agg"], CH * (NF + 1) * (i - 1))
                    sp.dma_start(h_sb[:, i % 2], h_dram[i]).then_inc(h_in[i % 2], 16)

                def far_rows(i, ts):
                    for t in ts:
                        n = i * TILES + t
                        if n >= 2:
                            sp.wait_ge(s["far_read"], n - 1)
                        sp.dma_start(far[:, n % 2, :], k.far_dram[t]).then_inc(far_in[n % 2], 16)

                def results_out(i, c):
                    for m in range(NF * (CH * i + c), NF * (CH * i + c + 1)):
                        sp.wait_ge(s["result"], m + 1)
                        sp.dma_start(h1_dram[NF * i + m % NF, :, cols(c)], o2[:, m % 2, :]).then_inc(st_out[m % 2], 16)

                sp.dma_start(bias[:], b_dram).then_inc(b_in, 16)
                if not wide:
                    for j in range(2):
                        sp.dma_start(a_rows[:, j, :], att_dram[j, 0].partition_broadcast(NT)).then_inc(at_in, 16)
                far_rows(0, range(2))
                sp.dma_start(counts[:], k.counts_dram[:, :, :]).then_inc(c_in, 16)
                if wide:
                    head_in(0)
                far_rows(0, range(2, TILES))
                if wide:
                    head_in(1)
                for i in range(heads):
                    more = i + 1 < heads
                    if more:
                        far_rows(i + 1, range(2))
                    if wide:
                        results_out(i, 0)
                    if more:
                        far_rows(i + 1, range(2, TILES))
                    if wide:
                        results_out(i, 1)
                        results_out(i, 2)
                    if i + 2 < heads:
                        head_in(i + 2)
                if wide:
                    for h in range(2):
                        sp.wait_ge(st_out[h], 16 * (NF * CH * heads // 2))

            @block.tensor
            def _(pe):
                def lay(n_diag, sem_in, wait, sem_out):
                    pe.wait_ge(sem_in, n_diag)
                    if wait:
                        pe.wait_ge(*wait)
                    for t in range(TILES):
                        b = 5 + t // 4
                        mm = nc.tensor.matmul(ps[:, b, NT * (t % 4):NT * (t % 4) + NT], k.ones[0:NT, :], dg[:, t, :],
                                              start=True, stop=True)
                    mm.then_inc(sem_out, 1)

                def a_row(i):
                    if i >= 1:
                        pe.wait_ge(s["r_out"], 4 * i)
                    lay(TILES * (i + 1), s["as_diag"], None, s["as_row"])

                def r_row(i, j):
                    lay(TILES * (2 * i + j + 1), s["r_diag"], (s["as_out"], 2 * (i + 1)) if j == 0 else (s["r_out"], 2 * (2 * i + 1)),
                        s["r_row"])

                def aggregate(i, c):
                    n = CH * i + c
                    for f in range(NF):
                        if f == 0:
                            if wide and c == 0:
                                pe.wait_ge(h_in[i % 2], 16 * (i // 2 + 1))
                            pe.wait_ge(s["p_made"], TILES * (n + 1))
                        if n >= 1:
                            pe.wait_ge(s["scaled"], NF * (n - 1) + f + 1)
                        for t in range(TILES):
                            mm = nc.tensor.matmul(ps[:, f, 0:CW], h_sb[:, i % HB, t, P * f:P * f + P], pr[:, n % 2, t, :],
                                                  start=(t == 0), stop=(t == TILES - 1))
                        mm.then_inc(s["agg"], 1)
                        if f == 0:
                            pe.wait_ge(s["summed"], TILES * (n + 1))
                            if n >= 1:
                                pe.wait_ge(s["inverse"], n)
                            nc.tensor.matmul(ps[:, DEN, 0:CW], k.ones[0:NT, :], sm[:, n % 2, :], start=True, stop=True)\
                                .then_inc(s["agg"], 1)

                a_row(0)
                r_row(0, 0)
                r_row(0, 1)
                for i in range(heads):
                    more = i + 1 < heads
                    aggregate(i, 0)
                    if more:
                        a_row(i + 1)
                    aggregate(i, 1)
                    if more:
                        r_row(i + 1, 0)
                        r_row(i + 1, 1)
                    aggregate(i, 2)

            @block.scalar
            def _(act):
                nexp = [0]

                def row_copy(i, j, sem):
                    nc.scalar.activation(rows[:, i % 2, j, 0:1000].rearrange("p (b n) -> p b n", b=2), ps[:, 5:7, 0:500],
                                         ACT.Copy).then_inc(sem, 1)
                    nc.scalar.activation(rows[:, i % 2, j, 1000:T], ps[:, 7, 0:250], ACT.Copy).then_inc(sem, 1)

                def a_copy(i):
                    act.wait_ge(s["as_row"], i + 1)
                    row_copy(i, 0, s["as_out"])

                def r_copy(i, j):
                    act.wait_ge(s["r_row"], 2 * i + j + 1)
                    row_copy(i, j, s["r_out"])

                def leak(n):
                    i, c, t = n // (CH * TILES), n // TILES % CH, n % TILES
                    if n % (CH * TILES) == 0:
                        act.wait_ge(s["r_out"], 4 * (i + 1))
                    if n >= 2:
                        act.wait_ge(s["low"], n - 1)
                    nc.scalar.activation(t2[:, n % 2, :], rows[0:NT, i % 2, 1, cols(c)], ACT.Identity,
                                         bias=al[:, i, 2, t:t + 1]).then_inc(s["leaked"], 1)

                def exps(m):
                    for _ in range(m):
                        n = nexp[0]
                        nexp[0] += 1
                        if n % (CH * TILES) == 0:
                            leak(n)
                        if (n + 1) % (CH * TILES) != 0:
                            leak(n + 1)
                        act.wait_ge(s["low"], n + 1)
                        nc.scalar.activation(t1[:, n % 4, :], t1[:, n % 4, :], ACT.Exp).then_inc(s["exped"], 1)

                def elus(n):
                    if wide:
                        for f in range(NF):
                            m = NF * n + f
                            if m == 0:
                                act.wait_ge(b_in, 16)
                            act.wait_ge(s["scaled"], m + 1)
                            if m >= 2:
                                act.wait_ge(st_out[m % 2], 16 * (m // 2))
                            b = NF * (n // CH) + f
                            nc.scalar.activation(o2[:, m % 2, :], o1[:, m % 2, :], ACT.Exp, bias=bias[:, b:b + 1]).then_inc(s["elu_exp"], 1)

                a_copy(0)
                r_copy(0, 0)
                r_copy(0, 1)
                exps(TILES)
                for i in range(heads):
                    more = i + 1 < heads
                    exps(TILES)
                    if more:
                        a_copy(i + 1)
                    elus(CH * i)
                    exps(TILES)
                    if more:
                        r_copy(i + 1, 0)
                        r_copy(i + 1, 1)
                    elus(CH * i + 1)
                    if more:
                        exps(TILES)
                    elus(CH * i + 2)

            @block.gpsimd
            def _(pool):
                for n in range(CH * heads):
                    for t in range(TILES):
                        m = n * TILES + t
                        pool.wait_ge(s["p_made"], m + 1)
                        if t == 0:
                            if n >= 2:
                                pool.wait_ge(s["inverse"], n - 1)
                            nc.gpsimd.tensor_copy(sm[:, n % 2, :], pr[:, n % 2, 0, :]).then_inc(s["summed"], 1)
                        else:
                            pool.wait_ge(s["summed"], m)
                            nc.gpsimd.tensor_tensor(sm[:, n % 2, :], sm[:, n % 2, :], pr[:, n % 2, t, :], ALU.add)\
                                .then_inc(s["summed"], 1)

            @block.vector
            def _(dve):
                ch = Chain(dve, s["order"])
                ch.step(nc.vector.memset(rows[:, :, :, T:TP], 0.0))
                made = [0]

                def logits():
                    dve.wait_ge(at_in, 32)
                    for t in range(TILES):
                        for j in range(2):
                            nc.vector.tensor_tensor_reduce(logits_rest, h_sb[:, 0, t, :], a_rows[:, j, :], 1.0, 0.0, ALU.mult, ALU.add,
                                                           al[:, 0, j, t:t + 1]).then_inc(s["al"], 1)
                            dve.wait_ge(s["al"], 2 * t + j + 1)
                    ch.then(nc.vector.tensor_scalar(al[:, 0, 2, :], al[:, 0, 0, :], LR, None, ALU.mult))

                def as_diag(i):
                    if i >= 1:
                        dve.wait_ge(s["r_row"], 2 * i)
                    for t in range(TILES):
                        nc.vector.tensor_scalar(dg[:, t, :], k.ident[0:NT, 0:NT], al[:, i, 0, t:t + 1], None,
                                                ALU.mult).then_inc(s["as_diag"], 1)

                def maxima(i):
                    dve.wait_ge(s["as_out"], 2 * (i + 1))
                    for t in range(TILES):
                        n = i * TILES + t
                        dve.wait_ge(far_in[n % 2], 16 * (n // 2 + 1))
                        nc.vector.tensor_tensor_reduce(maxima_rest, rows[0:NT, i % 2, 0, 0:T], far[:, n % 2, :], 1.0, 3 * BIG, ALU.add, ALU.max,
                                                       mx[:, 0, t:t + 1]).then_inc(s["far_read"], 1)
                        dve.wait_ge(s["far_read"], n + 1)
                    ch.then(nc.vector.tensor_tensor(mx[:, 0, :], mx[:, 0, :], al[:, i, 1, :], ALU.add))
                    ch.then(nc.vector.tensor_scalar(mx[:, 2, :], mx[:, 0, :], LR, None, ALU.mult))
                    ch.then(nc.vector.tensor_tensor(mx[:, 1, :], mx[:, 0, :], mx[:, 2, :], ALU.max))
                    ch.step(nc.vector.tensor_tensor(mx[:, 3, :], al[:, i, 1, :], mx[:, 1, :], ALU.subtract))
                    ch.then(nc.vector.scalar_tensor_tensor(out=mx[:, 4, :], in0=al[:, i, 1, :], scalar=LR, in1=mx[:, 1, :],
                                                           op0=ALU.mult, op1=ALU.subtract))

                def r_diag(i, j):
                    if j == 0:
                        dve.wait_ge(s["as_row"], i + 1)
                    else:
                        dve.wait_ge(s["r_row"], 2 * i + 1)
                    for t in range(TILES):
                        nc.vector.tensor_scalar(dg[:, t, :], k.ident[0:NT, 0:NT], mx[:, 3 + j, t:t + 1], None,
                                                ALU.mult).then_inc(s["r_diag"], 1)

                def weights(i, c):
                    n = CH * i + c
                    if c == 0:
                        dve.wait_ge(s["r_out"], 4 * (i + 1))
                    if n >= 2:
                        dve.wait_ge(s["agg"], (NF + 1) * (n - 1))
                        dve.wait_ge(s["summed"], TILES * (n - 1))
                    for t in range(TILES + 2):
                        if t < TILES:
                            m = n * TILES + t
                            dve.wait_ge(s["leaked"], m + 1)
                            if m >= 4:
                                dve.wait_ge(s["p_made"], m - 3)
                            nc.vector.scalar_tensor_tensor(out=t1[:, m % 4, :], in0=rows[0:NT, i % 2, 0, cols(c)],
                                                           scalar=al[:, i, 0, t:t + 1], in1=t2[:, m % 2, :],
                                                           op0=ALU.add, op1=ALU.max).then_inc(s["low"], 1)
                        if t >= 2:
                            m = n * TILES + t - 2
                            dve.wait_ge(s["exped"], m + 1)
                            nc.vector.scalar_tensor_tensor(out=pr[:, n % 2, t - 2, :], in0=t1[:, m % 4, :], scalar=1.0,
                                                           in1=counts[:, t - 2, cols(c)], op0=ALU.min, op1=ALU.mult)\
                                .then_inc(s["p_made"], 1)
                    dve.wait_ge(s["p_made"], TILES * (n + 1))

                def results(i, c):
                    n = CH * i + c
                    dve.wait_ge(s["agg"], (NF + 1) * n + 2)
                    ch.then(nc.vector.tensor_scalar(rden, ps[:, DEN, 0:CW], 1e-16, None, ALU.add))
                    nc.vector.reciprocal(rden, rden).then_inc(s["inverse"], 1)
                    dve.wait_ge(s["inverse"], n + 1)

                    def scale(f):
                        m = NF * n + f
                        dve.wait_ge(s["agg"], (NF + 1) * n + (1 if f == 0 else f + 2))
                        if m >= 2:
                            dve.wait_ge(s["result"], m - 1)
                        nc.vector.tensor_tensor(o1[:, m % 2, :], ps[:, f, 0:CW], rden, ALU.mult).then_inc(s["scaled"], 1)

                    def finish(f):
                        m = NF * n + f
                        b = bias[:, NF * i + f:NF * i + f + 1]
                        if wide:
                            dve.wait_ge(s["elu_exp"], m + 1)
                            ch.then(nc.vector.tensor_scalar(o2[:, m % 2, :], o2[:, m % 2, :], 1.0, -1.0, ALU.min, ALU.add))
                            nc.vector.scalar_tensor_tensor(out=o2[:, m % 2, :], in0=o1[:, m % 2, :], scalar=b, in1=o2[:, m % 2, :],
                                                           op0=ALU.add, op1=ALU.max).then_inc(s["result"], 1)
                        else:
                            dve.wait_ge(s["scaled"], m + 1)
                            nc.vector.scalar_tensor_tensor(out=k.xT[:, f, cols(c)], in0=o1[:, m % 2, :], scalar=b,
                                                           in1=k.xT[:, f, cols(c)], op0=ALU.add, op1=ALU.add).then_inc(s["result"], 1)
                    for f in range(NF):
                        scale(f)
                        if f >= 1:
                            finish(f - 1)
                    finish(NF - 1)
                    dve.wait_ge(s["result"], NF * (n + 1))
                if not wide:
                    logits()
                as_diag(0)
                maxima(0)
                r_diag(0, 0)
                r_diag(0, 1)
                dve.wait_ge(b_in, 16)
                dve.wait_ge(c_in, 16)
                weights(0, 0)
                for n in range(CH * heads):
                    i, c = n // CH, n % CH
                    if n + 1 < CH * heads:
                        weights((n + 1) // CH, (n + 1) % CH)
                    if i + 1 < heads and c == 0:
                        as_diag(i + 1)
                    if i + 1 < heads and c == 1:
                        maxima(i + 1)
                        r_diag(i + 1, 0)
                        r_diag(i + 1, 1)
                    results(i, c)


def project_wide_stage(k, w_dram, h1_dram):
    nc, ps = k.nc, k.ps
    KC = 16
    done, out = k.sem("h2_done"), k.sem("h2_out")
    w_high, w_split, h_high, h_split = (k.sem(n) for n in ("w2_high", "w2_split", "h1_high", "h1_split"))
    w_in, h_in = [k.sem(f"w2_in{h}") for h in range(2)], k.sem("h1_in")
    with ExitStack() as ctx:
        w = k.sb("w2_w", [P, 2, D], ctx=ctx)
        whi = k.sb("w2_hi", [P, KC, D], F32R, ctx=ctx)
        wlo = k.sb("w2_lo", [P, KC, D], F32R, ctx=ctx)
        h1 = k.sb("h1_tile", [P, KC, NT], ctx=ctx)
        hhi = k.sb("h1_hi", [P, 2, KC, NT], F32R, ctx=ctx)
        hlo = k.sb("h1_lo", [P, 2, KC, NT], F32R, ctx=ctx)
        with nc.Block(no_gpsimd_drain=True) as block:
            @block.sync
            def _(sp):
                def tile_in(t):
                    if t >= 1:
                        sp.wait_ge(h_split, t)
                    sp.dma_start(h1[:], h1_dram[:, :, tile_cols(t)].rearrange("c p n -> p c n")).then_inc(h_in, 16)
                tile_in(0)
                for i in range(KC):
                    if i >= 2:
                        sp.wait_ge(w_split, i - 1)
                    sp.dma_start(w[:, i % 2], w_dram[:, i, :]).then_inc(w_in[i % 2], 16)
                for t in range(1, TILES):
                    tile_in(t)

            @block.tensor
            def _(pe):
                for t in range(TILES):
                    pe.wait_ge(h_split, t + 1)
                    for h in range(2):
                        n = 2 * t + h
                        if n >= 4:
                            pe.wait_ge(out, n - 3)
                        for c in range(KC):
                            if n == 0:
                                pe.wait_ge(w_split, c + 1)
                            mm = three_passes(nc, ps[0:NT, n % 4, 0:HALF], (hhi[:, t % 2, c, :], hlo[:, t % 2, c, :]),
                                              (whi[:, c, HALF * h:HALF * h + HALF], wlo[:, c, HALF * h:HALF * h + HALF]),
                                              c == 0, c == KC - 1)
                        mm.then_inc(done, 1)

            @block.scalar
            def _(act):
                def tile_high(t):
                    act.wait_ge(h_in, 16 * (t + 1))
                    if t >= 2:
                        act.wait_ge(done, 2 * (t - 1))
                    nc.scalar.activation(hhi[:, t % 2], h1[:], ACT.Copy).then_inc(h_high, 1)
                tile_high(0)
                for i in range(KC):
                    act.wait_ge(w_in[i % 2], 16 * (i // 2 + 1))
                    nc.scalar.activation(whi[:, i, :], w[:, i % 2], ACT.Copy).then_inc(w_high, 1)
                tile_high(1)
                for t in range(TILES):
                    for n in (2 * t, 2 * t + 1):
                        act.wait_ge(done, n + 1)
                        nc.scalar.activation(k.h2[:, D * t + HALF * (n % 2):D * t + HALF * (n % 2) + HALF],
                                             ps[0:NT, n % 4, 0:HALF], ACT.Copy).then_inc(out, 1)
                    if t + 2 < TILES:
                        tile_high(t + 2)

            @block.vector
            def _(dve):
                def tile_low(t):
                    dve.wait_ge(h_high, t + 1)
                    nc.vector.tensor_tensor(hlo[:, t % 2], h1[:], hhi[:, t % 2].bitcast(F32), ALU.subtract).then_inc(h_split, 1)
                tile_low(0)
                for i in range(KC):
                    dve.wait_ge(w_high, i + 1)
                    nc.vector.tensor_tensor(wlo[:, i, :], w[:, i % 2], whi[:, i, :].bitcast(F32),
                                            ALU.subtract).then_inc(w_split, 1)
                for t in range(1, TILES):
                    tile_low(t)


def shared_expert_stage(k, w13_dram, w2_dram):
    nc, ps = k.nc, k.ps
    G = 4
    high, split, w_high, w_split, h_done, sig, u1, h_out, y_done, y_out, w2_in = (k.sem(f"sh_{n}") for n in (
        "high", "split", "w_high", "w_split", "h_done", "sig", "u1", "h_out", "y_done", "y_out", "w2_in"))
    w_in = [k.sem(f"sh_w_in{h}") for h in range(2)]
    with ExitStack() as ctx:
        hi = k.sb("sh_hi", [P, FC, TP], F32R, ctx=ctx)
        lo = k.sb("sh_lo", [P, FC, TP], F32R, ctx=ctx)
        w = k.sb("sh_w13", [P, 2, 2, FC, P], ctx=ctx)
        whi = k.sb("sh_w13_hi", [P, 2, 2, FC, P], F32R, ctx=ctx)
        wlo = k.sb("sh_w13_lo", [P, 2, 2, FC, P], F32R, ctx=ctx)
        w2 = k.sb("sh_w2", [P, G, D], ctx=ctx)
        hid = k.sb("sh_hid", [P, G, TP], ctx=ctx)
        sg = k.sb("sh_sig", [P, 2, CW], ctx=ctx)
        with nc.Block(no_gpsimd_drain=True) as block:
            @block.sync
            def _(sp):
                for g in range(G):
                    if g >= 2:
                        sp.wait_ge(w_split, g - 1)
                    sp.dma_start(w[:, g % 2], w13_dram[g // 2, :, g % 2]).then_inc(w_in[g % 2], 16)
                for e in range(2):
                    sp.dma_start(w2[:, 2 * e:2 * e + 2, :], w2_dram[e]).then_inc(w2_in, 16)

            @block.tensor
            def _(pe):
                for g in range(G):
                    pe.wait_ge(w_split, g + 1)
                    for c in range(CH):
                        n = CH * g + c
                        if n >= 2:
                            pe.wait_ge(h_out, n - 1)
                        for a in range(2):
                            for f in range(FC):
                                if n == 0 and a == 0:
                                    pe.wait_ge(split, f + 1)
                                mm = three_passes(nc, ps[:, 2 * (n % 2) + a, 0:CW], (whi[:, g % 2, a, f, :], wlo[:, g % 2, a, f, :]),
                                                  (hi[:, f, cols(c)], lo[:, f, cols(c)]), f == 0, f == FC - 1)
                        mm.then_inc(h_done, 1)
                pe.wait_ge(w2_in, 32)
                for y in range(FC * CH):
                    o, c = y // CH, y % CH
                    if y >= 4:
                        pe.wait_ge(y_out, y - 3)
                    for g in range(G):
                        if y == 0:
                            pe.wait_ge(h_out, CH * (g + 1))
                        mm = nc.tensor.matmul(ps[:, 4 + y % 4, 0:CW], w2[:, g, P * o:P * o + P], hid[:, g, cols(c)],
                                              start=(g == 0), stop=(g == G - 1))
                    mm.then_inc(y_done, 1)

            @block.scalar
            def _(act):
                def weights_high(g):
                    act.wait_ge(w_in[g % 2], 16 * (g // 2 + 1))
                    if g >= 2:
                        act.wait_ge(h_done, CH * (g - 1))
                    nc.scalar.activation(whi[:, g % 2], w[:, g % 2], ACT.Copy).then_inc(w_high, 1)
                for f in range(FC):
                    nc.scalar.activation(hi[:, f, :], k.nT[:, f, :], ACT.Copy).then_inc(high, 1)
                    if f < 2:
                        weights_high(f)
                for n in range(CH * G):
                    act.wait_ge(h_done, n + 1)
                    if n >= 2:
                        act.wait_ge(h_out, n - 1)
                    nc.scalar.activation(sg[:, n % 2, :], ps[:, 2 * (n % 2), 0:CW], ACT.Sigmoid).then_inc(sig, 1)
                    if n % CH == CH - 1 and n // CH + 2 < G:
                        weights_high(n // CH + 2)

            @block.vector
            def _(dve):
                def weights_low(g):
                    dve.wait_ge(w_high, g + 1)
                    nc.vector.tensor_tensor(wlo[:, g % 2], w[:, g % 2], whi[:, g % 2].bitcast(F32), ALU.subtract).then_inc(w_split, 1)
                for f in range(FC):
                    dve.wait_ge(high, f + 1)
                    nc.vector.tensor_tensor(lo[:, f, :], k.nT[:, f, :], hi[:, f, :].bitcast(F32), ALU.subtract).then_inc(split, 1)
                    if f < 2:
                        weights_low(f)
                for n in range(CH * G):
                    h = hid[:, n // CH, cols(n % CH)]
                    dve.wait_ge(sig, n + 1)
                    nc.vector.tensor_tensor(h, ps[:, 2 * (n % 2), 0:CW], sg[:, n % 2, :], ALU.mult).then_inc(u1, 1)
                    dve.wait_ge(u1, n + 1)
                    nc.vector.tensor_tensor(h, ps[:, 2 * (n % 2) + 1, 0:CW], h, ALU.mult).then_inc(h_out, 1)
                    if n % CH == CH - 1 and n // CH + 2 < G:
                        weights_low(n // CH + 2)
                for y in range(FC * CH):
                    o, c = y // CH, y % CH
                    dve.wait_ge(y_done, y + 1)
                    nc.vector.tensor_tensor(k.xT[:, o, cols(c)], ps[:, 4 + y % 4, 0:CW], k.xT[:, o, cols(c)], ALU.add).then_inc(y_out, 1)


def store_stage(k, src, out_dram):
    stored = k.sem("y_stored")
    with k.nc.Block(no_gpsimd_drain=True) as block:
        @block.sync
        def _(sp):
            sp.dma_start(out_dram, src[:, :, 0:T]).then_inc(stored, 16)
            sp.wait_ge(stored, 16)


def program(nc, a, out):
    with ExitStack() as ctx:
        k = Kit(nc, ctx)
        k.ps = ctx.enter_context(nc.psum_tensor("ps", [P, 8, 512], F32))
        k.sem_ctx = layer0 = ctx.enter_context(ExitStack())
        ones_stage(k)
        nbuf = k.sb("normed", [P, TILES * D])
        k.nT = nbuf[:, 0:FC * TP].rearrange("p (c n) -> p c n", c=FC)
        k.h2 = nbuf[0:NT, :]
        xbuf = k.sb("x", [P, TILES * D])
        k.xT = xbuf[:, 0:FC * TP].rearrange("p (c n) -> p c n", c=FC)
        k.x_node = xbuf[0:NT, :].rearrange("p (t d) -> p t d", t=TILES)
        k.dinv = k.sb("dinv", [NT, TILES])
        k.slot = k.sb("slot", [NT, 2, TILES], U32)
        k.weight = k.sb("choice_weight", [NT, TILES, 2])
        k.group_expert = k.sb("group_expert", [1, NG1], I32)
        k.more_quads = k.sb("more_quads", [1, 1], I32)
        rows = nc.dram_tensor("expert_rows", (NG1 * GROUP, D), F32, kind="Internal").ap()
        k.far_dram = nc.dram_tensor("far", (TILES, NT, T), BF16, kind="Internal").ap()
        k.counts_dram = nc.dram_tensor("counts_keep", (NT, TILES, TP), I16, kind="Internal").ap()
        comb0 = nc.dram_tensor("comb0", (8, TP), F32, kind="Internal").ap()
        hw_dram = nc.dram_tensor("h1_projected", (4, NT, TILES, 512), F32, kind="Internal").ap()
        h1_dram = nc.dram_tensor("h1", (16, P, TP), F32, kind="Internal").ap()
        out_f = out.rearrange("(c p) n -> p c n", p=P)

        with ExitStack() as first:
            k.attT = k.sb("attT", [P, FC, TP], ctx=first)
            norm_nodes_stage(k, a["x"])
            linear_attention_stage(k, a["L0_kv"], a["L0_q"], rows)
            with ExitStack() as edges:
                k.counts = k.sb("counts", [NT, TILES, TP], ctx=edges)
                counts_stage(k, a["src"], a["dst"], a["dst_groups"])
                aggregate_stage(k)
            mix_project_stage(k, a["L0_out"], a["L0_bias"], a["xT"])
        norm_stage(k, "ln1")
        router_stage(k, "r0", 8, a["L0_router_w"], a["L0_router_b"], True, comb0, NG0)
        scatter_stage(k, "s0", rows)
        block_stage(k, "e0", NG0, 8, a["L0_experts"], rows, False)
        combine_stage(k, "c0", rows)
        routed_bias_stage(k, a["L0_expert_b"], comb0, 8)
        k.clear_sems()
        layer0.close()
        k.sem_ctx = layer1 = ctx.enter_context(ExitStack())
        norm_stage(k, "ln2")
        with ExitStack() as att:
            k.attT = k.sb("attT1", [P, FC, TP], ctx=att)
            flow_attention_stage(k, a["L1_qk"], a["L1_b_qk"], a["L1_v"], a["L1_b_v"])
            flow_project_stage(k, a["L1_proj"], a["L1_b_proj"])
        k.al = k.sb("g1_logits", [NT, 4, 3, TILES])
        graph_project_stage(k, a["L1_W1"], a["L1_att1"], hw_dram, 4, 512)
        graph_layer(k, "g1", 4, 512, hw_dram, a["L1_att1"], a["L1_b1"], True, h1_dram)
        k.clear_sems()
        layer1.close()
        k.sem_ctx = ctx.enter_context(ExitStack())
        project_wide_stage(k, a["L1_W2"], h1_dram)
        graph_layer(k, "g2", 1, D, None, a["L1_att2"], a["L1_b2"], False)
        norm_stage(k, "ln3")
        router_stage(k, "r1", 16, a["L1_gate_w"], None, False, None, NG1)
        shared_expert_stage(k, a["L1_sw13"], a["L1_sw2"])
        scatter_stage(k, "s1", rows)
        block_stage(k, "e1", NG1, 16, a["L1_experts"], rows, True)
        combine_stage(k, "c1", rows)
        store_stage(k, k.xT, out_f)


def kernel(**inputs):
    import numpy as np
    import concourse.bacc as _bacc
    from concourse.bass_utils import run_bass_kernel_spmd as _run

    nc = _bacc.Bacc("TRN2", target_bir_lowering=False, num_devices=1)
    v = {n: np.asarray(x) for n, x in inputs.items()}

    def chunks(w):
        ni, no = w.shape[0] // P, w.shape[1] // P
        return w.reshape(ni, P, no, P).transpose(2, 1, 0, 3)

    def blocks(w, width):
        ni, nb = w.shape[0] // P, w.shape[1] // width
        return w.reshape(ni, P, nb, width).transpose(2, 1, 0, 3)

    def column(b):
        return b.reshape(-1, P).T

    def moving(w):
        e, ni, no = w.shape
        return w.reshape(e, ni // P, P, no).transpose(0, 2, 1, 3).reshape(e, P, -1)

    def pairs(w1, w3):
        e = w1.shape[0]
        return np.stack([w1, w3], 1).reshape(e, 2, 2, P, FC, P).transpose(0, 5, 2, 1, 4, 3)

    def halves(w):
        return w.reshape(2, 256, D)

    w13 = moving(np.concatenate([v["L1_ffn_w1"], v["L1_ffn_w3"]], 1).transpose(0, 2, 1))
    experts1 = np.concatenate([w13, moving(v["L1_ffn_w2"].transpose(0, 2, 1))], 2)
    host = {
        "x": v["x"], "xT": v["x"].T.reshape(FC, P, T).transpose(1, 0, 2),
        "src": v["src"].reshape(EC, NT).T, "dst": v["dst"].reshape(EC, NT).T, "dst_groups": v["dst"].reshape(EC // 4, 4 * NT),
        "L0_kv": blocks(v["L0_mix_w_qkv"][:, D:], HALF), "L0_q": chunks(v["L0_mix_w_qkv"][:, :D]),
        "L0_out": chunks(np.concatenate([v["L0_gnn_W"], v["L0_mix_w_proj"]], 0)),
        "L0_bias": np.stack([column(v["L0_gnn_b"]), column(v["L0_mix_b_proj"])]),
        "L0_router_w": v["L0_ffn_router_w"].T.reshape(FC, P, 8).transpose(1, 0, 2),
        "L0_router_b": v["L0_ffn_router_b"],
        "L0_experts": moving(v["L0_ffn_expert_w"].transpose(0, 2, 1)),
        "L0_expert_b": v["L0_ffn_expert_b"],
        "L1_qk": chunks(v["L1_mix_W_qkv"][:, :2 * D]), "L1_v": blocks(v["L1_mix_W_qkv"][:, 2 * D:], HALF),
        "L1_b_qk": column(v["L1_mix_b_qkv"][:2 * D]), "L1_b_v": v["L1_mix_b_qkv"][2 * D:],
        "L1_proj": chunks(v["L1_mix_W_proj"]), "L1_b_proj": column(v["L1_mix_b_proj"]),
        "L1_W1": blocks(v["L1_gnn_W1"], 512), "L1_att1": np.stack([v["L1_gnn_att_src1"], v["L1_gnn_att_dst1"]]),
        "L1_b1": column(v["L1_gnn_b1"]), "L1_W2": v["L1_gnn_W2"].reshape(16, P, D).transpose(1, 0, 2),
        "L1_att2": np.stack([v["L1_gnn_att_src2"], v["L1_gnn_att_dst2"]]), "L1_b2": column(v["L1_gnn_b2"]),
        "L1_gate_w": v["L1_ffn_gate_w"].T.reshape(FC, P, 16).transpose(1, 0, 2),
        "L1_sw13": pairs(halves(v["L1_ffn_sw1"]), halves(v["L1_ffn_sw3"])),
        "L1_sw2": halves(v["L1_ffn_sw2"].T).reshape(2, 2, P, D).transpose(0, 2, 1, 3),
        "L1_experts": experts1,
    }
    host = {n: np.ascontiguousarray(x) for n, x in host.items()}
    a = {n: nc.dram_tensor("in_" + n, x.shape, mybir.dt.from_np(x.dtype), kind="ExternalInput").ap() for n, x in host.items()}
    out = nc.dram_tensor("out_y", (D, T), F32, kind="ExternalOutput").ap()
    program(nc, a, out)
    r = _run(nc, [{"in_" + n: x for n, x in host.items()}], core_ids=[0])
    return np.ascontiguousarray(r.results[0]["out_y"].T)
```
